# Optimizing a Trainium2 kernel written in Bass

```python
import numpy as np
import jax
import jax.numpy as jnp

def _softmax(x, axis=-1):
    return jax.nn.softmax(x, axis=axis)

def _gelu(x):
    return jax.nn.gelu(x, approximate=True)

def _silu(x):
    return jax.nn.silu(x)

def _sigmoid(x):
    return jax.nn.sigmoid(x)

def _layernorm(x, axis=-1, eps=1e-05):
    m = jnp.mean(x, axis=axis, keepdims=True)
    v = jnp.var(x, axis=axis, keepdims=True)
    return (x - m) / jnp.sqrt(v + eps)

def _scatter_add(tgt, idx, src, axis=0):
    return tgt.at[idx].add(src)

def _segment_sum(src, seg, n):
    return jax.ops.segment_sum(src, seg, n)
kernel_name = 'mk_decoder_postln_d4_seqx_r8_2b83ed'

def setup_inputs(seed: int=0):
    np.random.seed(seed)
    _w = jnp.asarray

    def _rec_inputs():
        import jax
        import jax.numpy as jnp
        _rk = jax.random.key(seed)
        x = -0.0002928 + 1 * jax.random.normal(jax.random.fold_in(_rk, 1), (8, 128, 128), jnp.float32)
        _lenS = 128 - jax.random.randint(jax.random.fold_in(_rk, 7), (8,), 0, max(1, 128 // 4) + 1, jnp.int32)
        _lenS2 = 77 - jax.random.randint(jax.random.fold_in(_rk, 8), (8,), 0, max(1, 77 // 4) + 1, jnp.int32)
        _ctx_1024P = jax.random.normal(jax.random.fold_in(_rk, 11), (8, 16, 128), jnp.float32)
        _ctx_1024c = jax.random.dirichlet(jax.random.fold_in(_rk, 511), 0.3 * jnp.ones((16,), jnp.float32), (8, 77))
        _ctx_1024t = jnp.einsum('bsk,bkd->bsd', _ctx_1024c, _ctx_1024P)
        _ctx_1024t = _ctx_1024t * jax.lax.rsqrt(jnp.mean(jnp.square(_ctx_1024t)) + 1e-12) * 0.953939
        ctx_1024 = -1.39393e-06 + 0.999914 * (_ctx_1024t + 0.3 * jax.random.normal(jax.random.fold_in(_rk, 611), (8, 77, 128), jnp.float32))
        _validS = jnp.arange(128)[None, :] < _lenS[:, None]
        _validS2 = jnp.arange(77)[None, :] < _lenS2[:, None]
        _causal = jnp.tril(jnp.ones((128, 128), dtype=bool))
        mask_BxS2_bk0 = jnp.logical_not(jnp.broadcast_to(_validS2[:, :], (8, 77)))
        return (x, ctx_1024, mask_BxS2_bk0)
    x, ctx_1024, mask_BxS2_bk0 = _rec_inputs()

    def _L0_attn_setup():
        import jax, jax.numpy as jnp
        import numpy as np
        TTT_LR = 0.01
        LN_EPS = 1e-05
        key = jax.random.key(seed)
        ks = jax.random.split(key, 4)
        B, S, D, DS = (4, 256, 128, 64)
        sc = 1.0 / np.sqrt(D).astype(np.float32)
        return {'x': jax.random.normal(ks[0], (B, S, D), dtype=jnp.float32), 'Wk': jax.random.normal(ks[1], (DS, D), dtype=jnp.float32) * sc, 'bk': jnp.zeros((DS,), jnp.float32), 'Wv': jax.random.normal(ks[2], (D, D), dtype=jnp.float32) * sc, 'bv': jnp.zeros((D,), jnp.float32), 'Wq': jax.random.normal(ks[3], (DS, D), dtype=jnp.float32) * sc, 'bq': jnp.zeros((DS,), jnp.float32), 'gamma': jnp.ones((D,), jnp.float32), 'beta': jnp.zeros((D,), jnp.float32)}
    _L0_attn_all = _L0_attn_setup()
    _L0_attn_in = {k: v for k, v in _L0_attn_all.items() if k in ('Wk', 'bk', 'Wv', 'bv', 'Wq', 'bq', 'gamma', 'beta')}
    del _L0_attn_all

    def _L0_xattn_setup():
        import jax, jax.numpy as jnp
        import numpy as np
        import math
        B, S, D, H = (2, 256, 128, 16)
        DH = D // H
        key = jax.random.key(seed)
        ks = jax.random.split(key, 12)

        def nrm(k, shape, scale=1.0):
            return jax.random.normal(k, shape, dtype=jnp.float32) * scale
        return {'x': nrm(ks[0], (B, S, D)), 'memory': nrm(ks[1], (B, S, D)), 'mask': jax.random.randint(ks[2], (B, S), 0, 2).astype(jnp.bool_), 'wq': nrm(ks[3], (D, D), 1.0 / math.sqrt(D)), 'bq': nrm(ks[4], (D,), 0.02), 'wk': nrm(ks[5], (D, D), 1.0 / math.sqrt(D)), 'bk': nrm(ks[6], (D,), 0.02), 'wv': nrm(ks[7], (D, D), 1.0 / math.sqrt(D)), 'bv': nrm(ks[8], (D,), 0.02), 'wo': nrm(ks[9], (D, D), 1.0 / math.sqrt(D)), 'bo': nrm(ks[10], (D,), 0.02)}
    _L0_xattn_all = _L0_xattn_setup()
    _L0_xattn_in = {k: v for k, v in _L0_xattn_all.items() if k in ('wq', 'bq', 'wk', 'bk', 'wv', 'bv', 'wo', 'bo')}
    del _L0_xattn_all

    def _L0_ffn_setup():
        import jax, jax.numpy as jnp
        import numpy as np
        D = 128
        H = 512
        E = 8
        K = 2
        B, S = (4, 256)
        key = jax.random.key(seed)
        ks = jax.random.split(key, 8)

        def lin(k, fan_in, shape):
            bound = 1.0 / np.sqrt(fan_in)
            return jax.random.uniform(k, shape, jnp.float32, -bound, bound)
        return {'x': jax.random.normal(ks[0], (B, S, D), jnp.float32), 'Wg': lin(ks[1], D, (D, E)), 'bg': lin(ks[2], D, (E,)), 'W1': lin(ks[3], D, (E, D, H)), 'b1': lin(ks[4], D, (E, H)), 'W2': lin(ks[5], H, (E, H, D)), 'b2': lin(ks[6], H, (E, D))}
    _L0_ffn_all = _L0_ffn_setup()
    _L0_ffn_in = {k: v for k, v in _L0_ffn_all.items() if k in ('Wg', 'bg', 'W1', 'b1', 'W2', 'b2')}
    del _L0_ffn_all

    def _L1_attn_setup():
        import jax, jax.numpy as jnp
        import numpy as np
        NUM_HEADS = 4
        CHUNK = 64
        GATE_NORM = 16.0
        EPS = 1e-05

        def _xavier(key, fan_in, fan_out):
            gain = 2.0 ** (-2.5)
            limit = gain * np.sqrt(6.0 / (fan_in + fan_out))
            return jax.random.uniform(key, (fan_in, fan_out), jnp.float32, -limit, limit)

        def _to_chunks(t, B, H, NC, C):
            d = t.shape[-1]
            return t.reshape(B, H, NC, C, d).transpose(2, 0, 1, 3, 4)

        def _gla_forward(x, Wq, Wk, Wv, Wg, gk_w1, gk_w2, gk_b2, g_norm_w, Wo):
            B, L, D = x.shape
            H = NUM_HEADS
            C = CHUNK
            NC = L // C
            q = x @ Wq
            k = x @ Wk
            v = x @ Wv
            gk = jax.nn.log_sigmoid(x @ gk_w1 @ gk_w2 + gk_b2) / GATE_NORM

            def split_heads(t):
                return t.reshape(B, L, H, -1).transpose(0, 2, 1, 3)
            q, k, v, gk = map(split_heads, (q, k, v, gk))
            dk = q.shape[-1]
            scale = dk ** (-0.5)
            qc = _to_chunks(q, B, H, NC, C)
            kc = _to_chunks(k, B, H, NC, C)
            vc = _to_chunks(v, B, H, NC, C)
            gc = _to_chunks(gk, B, H, NC, C)
            Bcum = jnp.cumsum(gc, axis=3)
            causal = jnp.tril(jnp.ones((C, C), jnp.float32))

            def step(Hst, inp):
                qi, ki, vi, bi = inp
                qg = qi * jnp.exp(bi) * scale
                kg = ki * jnp.exp(-bi)
                o_inter = jnp.einsum('bhcd,bhde->bhce', qg, Hst)
                A = jnp.einsum('bhtd,bhsd->bhts', qg, kg) * causal
                o_intra = jnp.einsum('bhts,bhse->bhte', A, vi)
                b_last = bi[:, :, -1:, :]
                kH = ki * jnp.exp(b_last - bi)
                H_new = jnp.exp(b_last).transpose(0, 1, 3, 2) * Hst + jnp.einsum('bhcd,bhce->bhde', kH, vi)
                return (H_new, o_inter + o_intra)
            dv = v.shape[-1]
            H0 = jnp.zeros((B, H, dk, dv), jnp.float32)
            _, oc = jax.lax.scan(step, H0, (qc, kc, vc, Bcum))
            o = oc.transpose(1, 2, 0, 3, 4).reshape(B, H, L, dv)
            o = o.transpose(0, 2, 1, 3)
            rms = jnp.sqrt(jnp.mean(o * o, axis=-1, keepdims=True) + EPS)
            o_n = o / rms * g_norm_w
            g = (x @ Wg).reshape(B, L, H, dv)
            o = o_n * g * jax.nn.sigmoid(g)
            return o.reshape(B, L, H * dv) @ Wo
        key = jax.random.key(seed)
        ks = jax.random.split(key, 8)
        B, L, D = (4, 256, 128)
        Dk, Dv, R = (128, 256, 16)
        x = jax.random.normal(ks[0], (B, L, D), jnp.float32)
        return {'x': x, 'Wq': _xavier(ks[1], D, Dk), 'Wk': _xavier(ks[2], D, Dk), 'Wv': _xavier(ks[3], D, Dv), 'Wg': _xavier(ks[4], D, Dv), 'gk_w1': _xavier(ks[5], D, R), 'gk_w2': _xavier(ks[6], R, Dk), 'gk_b2': jnp.zeros((Dk,), jnp.float32), 'g_norm_w': jnp.ones((Dv // NUM_HEADS,), jnp.float32), 'Wo': _xavier(ks[7], Dv, D)}
    _L1_attn_all = _L1_attn_setup()
    _L1_attn_in = {k: v for k, v in _L1_attn_all.items() if k in ('Wq', 'Wk', 'Wv', 'Wg', 'gk_w1', 'gk_w2', 'gk_b2', 'g_norm_w', 'Wo')}
    del _L1_attn_all

    def _L1_xattn_setup():
        import jax, jax.numpy as jnp
        import numpy as np
        import math
        B, S, D, H = (1, 256, 128, 16)
        DK = D // H
        DH = 64
        LOG_T_MIN = math.log(0.1)
        LOG_T_MAX = math.log(10.0)

        def _linear(x, W, b):
            return x @ W.T + b
        key = jax.random.key(seed)
        ks = jax.random.split(key, 20)
        p = 0.02
        return {'query': jax.random.normal(ks[0], (B, S, D), jnp.float32), 'key': jax.random.normal(ks[1], (B, S, D), jnp.float32), 'value': jax.random.normal(ks[2], (B, S, D), jnp.float32), 'Wq': jax.random.normal(ks[3], (D, D), jnp.float32) * p, 'bq': jax.random.normal(ks[4], (D,), jnp.float32) * p, 'Wk': jax.random.normal(ks[5], (D, D), jnp.float32) * p, 'bk': jax.random.normal(ks[6], (D,), jnp.float32) * p, 'Wv': jax.random.normal(ks[7], (D, D), jnp.float32) * p, 'bv': jax.random.normal(ks[8], (D,), jnp.float32) * p, 'Wo': jax.random.normal(ks[9], (D, D), jnp.float32) * p, 'bo': jax.random.normal(ks[10], (D,), jnp.float32) * p, 'w1': jax.random.normal(ks[11], (DH, 3), jnp.float32) * 0.3, 'b1': jax.random.normal(ks[12], (DH,), jnp.float32) * 0.1, 'w2': jax.random.normal(ks[13], (DH, DH), jnp.float32) * 0.1, 'b2': jax.random.normal(ks[14], (DH,), jnp.float32) * 0.1, 'w3': jax.random.normal(ks[15], (1, DH), jnp.float32) * 0.1, 'b3': jnp.full((1,), (LOG_T_MIN + LOG_T_MAX) / 2, jnp.float32)}
    _L1_xattn_all = _L1_xattn_setup()
    _L1_xattn_in = {k: v for k, v in _L1_xattn_all.items() if k in ('Wq', 'bq', 'Wk', 'bk', 'Wv', 'bv', 'Wo', 'bo', 'w1', 'b1', 'w2', 'b2', 'w3', 'b3')}
    del _L1_xattn_all

    def _L1_ffn_setup():
        import jax, jax.numpy as jnp
        import numpy as np
        B, S, D, O, E, K = (2, 256, 128, 128, 8, 2)
        key = jax.random.key(seed)
        ks = jax.random.split(key, 6)

        def w(k, shape, fan_in):
            return jax.random.normal(k, shape, jnp.float32) * fan_in ** (-0.5)
        return {'x': jax.random.normal(ks[0], (B, S, D), jnp.float32), 'gate_w': w(ks[1], (E, D), D), 'gate_b': jnp.zeros((E,), jnp.float32), 'w1': w(ks[2], (E, D, O), D), 'b1': jnp.zeros((E, O), jnp.float32), 'w2': w(ks[3], (E, O, O), O), 'b2': jnp.zeros((E, O), jnp.float32), 'w3': w(ks[4], (E, O, O), O), 'b3': jnp.zeros((E, O), jnp.float32)}
    _L1_ffn_all = _L1_ffn_setup()
    _L1_ffn_in = {k: v for k, v in _L1_ffn_all.items() if k in ('gate_w', 'gate_b', 'w1', 'b1', 'w2', 'b2', 'w3', 'b3')}
    del _L1_ffn_all

    def _L2_attn_setup():
        import jax, jax.numpy as jnp
        import numpy as np
        D_MODEL = 128
        NUM_HEADS = 16
        LOCAL_WINDOW = 128
        GLOBAL_STRIDE = 64
        B, T = (4, 256)

        def _rope_tables(T, d_head, base=10000.0):
            half = d_head // 2
            pos = jnp.arange(T, dtype=jnp.float32)[:, None]
            inv_freq = 1.0 / base ** (jnp.arange(half, dtype=jnp.float32) / half)
            ang = pos * inv_freq[None, :]
            return (jnp.cos(ang), jnp.sin(ang))

        def _rope_apply(x, cos_h, sin_h):
            xe = x[..., 0::2]
            xo = x[..., 1::2]
            re = xe * cos_h - xo * sin_h
            ro = xe * sin_h + xo * cos_h
            return jnp.stack([re, ro], axis=-1).reshape(x.shape)
        key = jax.random.key(seed)
        k1, k2, k3 = jax.random.split(key, 3)
        x = jax.random.normal(k1, (B, T, D_MODEL), dtype=jnp.float32)
        W_qkv = jax.random.normal(k2, (D_MODEL, 3 * D_MODEL), dtype=jnp.float32) * D_MODEL ** (-0.5)
        W_out = jax.random.normal(k3, (D_MODEL, D_MODEL), dtype=jnp.float32) * D_MODEL ** (-0.5)
        b_out = jnp.zeros((D_MODEL,), dtype=jnp.float32)
        return {'x': x, 'W_qkv': W_qkv, 'W_out': W_out, 'b_out': b_out}
    _L2_attn_all = _L2_attn_setup()
    _L2_attn_in = {k: v for k, v in _L2_attn_all.items() if k in ('W_qkv', 'W_out', 'b_out')}
    del _L2_attn_all

    def _L2_xattn_setup():
        import jax, jax.numpy as jnp
        import numpy as np
        DIM = 128
        HEADS = 16
        HEAD_DIM = DIM // HEADS
        SCALE = HEAD_DIM ** (-0.5)
        key = jax.random.key(seed)
        ks = jax.random.split(key, 8)
        B, Nx, N, C = (4, 256, 64, DIM)
        s = C ** (-0.5)
        return {'x': jax.random.normal(ks[0], (B, Nx, C), jnp.float32), 'cls': jax.random.normal(ks[1], (B, N, C), jnp.float32), 'w_kv': jax.random.normal(ks[2], (C, 2 * C), jnp.float32) * s, 'w_q': jax.random.normal(ks[3], (C, C), jnp.float32) * s, 'w_la': jax.random.normal(ks[4], (C, HEADS), jnp.float32) * s, 'w_proj': jax.random.normal(ks[5], (C, C), jnp.float32) * s, 'b_proj': jax.random.normal(ks[6], (C,), jnp.float32) * 0.01, 'att_weight': jax.random.normal(ks[7], (1,), jnp.float32) * 0.1}
    _L2_xattn_all = _L2_xattn_setup()
    _L2_xattn_in = {k: v for k, v in _L2_xattn_all.items() if k in ('w_kv', 'w_q', 'w_la', 'w_proj', 'b_proj', 'att_weight')}
    del _L2_xattn_all

    def _L2_ffn_setup():
        import jax, jax.numpy as jnp
        import numpy as np
        B, T, D = (4, 256, 128)
        H, DH, E, SEL = (8, 64, 5, 2)

        def _topk_mask(logits, k):
            _, idx = jax.lax.top_k(logits, k)
            return jnp.sum(jax.nn.one_hot(idx, logits.shape[-1], dtype=logits.dtype), axis=-2)
        key = jax.random.key(seed)
        ks = jax.random.split(key, 7)
        s = 0.02
        x = jax.random.normal(ks[0], (B, T, D), dtype=jnp.float32)
        Wq = jax.random.normal(ks[1], (D, H * DH), dtype=jnp.float32) * s
        Wk = jax.random.normal(ks[2], (D, H * DH), dtype=jnp.float32) * s
        Ws = jax.random.normal(ks[3], (D, H * E), dtype=jnp.float32) * s
        Wd = jax.random.normal(ks[4], (D, H * E), dtype=jnp.float32) * s
        Wv = jax.random.normal(ks[5], (E, D, DH), dtype=jnp.float32) * s
        Wo = jax.random.normal(ks[6], (E, DH, D), dtype=jnp.float32) * s
        return {'x': x, 'Wq': Wq, 'Wk': Wk, 'Ws': Ws, 'Wd': Wd, 'Wv': Wv, 'Wo': Wo}
    _L2_ffn_all = _L2_ffn_setup()
    _L2_ffn_in = {k: v for k, v in _L2_ffn_all.items() if k in ('Wq', 'Wk', 'Ws', 'Wd', 'Wv', 'Wo')}
    del _L2_ffn_all

    def _L3_attn_setup():
        import jax, jax.numpy as jnp
        import numpy as np
        B, T, C, R = (8, 128, 128, 64)
        EPS = 1e-05
        key = jax.random.key(seed)
        ks = jax.random.split(key, 8)
        x = jax.random.normal(ks[0], (B, T, C), dtype=jnp.float32)
        W_attn = jax.random.normal(ks[1], (3 * C, C), dtype=jnp.float32) * 0.02
        W_proj = jax.random.normal(ks[2], (C, C), dtype=jnp.float32) * 0.02
        lora_attn_A = jax.random.normal(ks[3], (C, R), dtype=jnp.float32) * 0.02
        lora_attn_B = jax.random.normal(ks[4], (R, 3 * C), dtype=jnp.float32) * 0.02
        lora_proj_A = jax.random.normal(ks[5], (C, R), dtype=jnp.float32) * 0.02
        lora_proj_B = jax.random.normal(ks[6], (R, C), dtype=jnp.float32) * 0.02
        bn_gamma = jnp.ones((3 * C,), dtype=jnp.float32)
        bn_beta = jnp.zeros((3 * C,), dtype=jnp.float32)
        return {'x': x, 'W_attn': W_attn, 'W_proj': W_proj, 'lora_attn_A': lora_attn_A, 'lora_attn_B': lora_attn_B, 'lora_proj_A': lora_proj_A, 'lora_proj_B': lora_proj_B, 'bn_gamma': bn_gamma, 'bn_beta': bn_beta}
    _L3_attn_all = _L3_attn_setup()
    _L3_attn_in = {k: v for k, v in _L3_attn_all.items() if k in ('W_attn', 'W_proj', 'lora_attn_A', 'lora_attn_B', 'lora_proj_A', 'lora_proj_B', 'bn_gamma', 'bn_beta')}
    del _L3_attn_all

    def _L3_xattn_setup():
        import jax, jax.numpy as jnp
        import numpy as np
        N_HEAD = 16
        D_MODEL = 128
        D_K = D_MODEL // N_HEAD

        def _split_heads(x, B):
            return x.reshape(B, -1, N_HEAD, D_K).transpose(0, 2, 1, 3)
        key = jax.random.key(seed)
        ks = jax.random.split(key, 7)
        B, S = (4, 256)
        scale = 1.0 / np.sqrt(D_MODEL)
        return {'Q': jax.random.normal(ks[0], (B, S, D_MODEL), jnp.float32), 'K': jax.random.normal(ks[1], (B, S, D_MODEL), jnp.float32), 'V': jax.random.normal(ks[2], (B, S, D_MODEL), jnp.float32), 'Wq': jax.random.normal(ks[3], (D_MODEL, D_MODEL), jnp.float32) * scale, 'bq': jnp.zeros((D_MODEL,), jnp.float32), 'Wo': jax.random.normal(ks[4], (D_MODEL, D_MODEL), jnp.float32) * scale, 'bo': jnp.zeros((D_MODEL,), jnp.float32)}
    _L3_xattn_all = _L3_xattn_setup()
    _L3_xattn_in = {k: v for k, v in _L3_xattn_all.items() if k in ('Wq', 'bq', 'Wo', 'bo')}
    del _L3_xattn_all

    def _L3_ffn_setup():
        import jax, jax.numpy as jnp
        import numpy as np
        BLOCK_SIZE = 32
        FP6_E2M3_MAX = 7.5

        def _build_fp6_e2m3_grid():
            vals = set()
            for bits in range(64):
                s = bits >> 5 & 1
                e = bits >> 3 & 3
                m = bits & 7
                v = m / 8.0 if e == 0 else (1.0 + m / 8.0) * 2.0 ** (e - 1)
                vals.add(-v if s else v)
            return np.array(sorted(vals), dtype=np.float32)
        _GRID = jnp.asarray(_build_fp6_e2m3_grid())

        def _nearest_on_grid(x, grid):
            idx = jnp.clip(jnp.searchsorted(grid, x), 0, grid.shape[0] - 1)
            idx_lo = jnp.maximum(idx - 1, 0)
            v_hi = grid[idx]
            v_lo = grid[idx_lo]
            return jnp.where(jnp.abs(x - v_lo) <= jnp.abs(x - v_hi), v_lo, v_hi)

        def _mx_quantize(t, eps=1e-30):
            rows, K = t.shape
            blocks = t.reshape(rows, K // BLOCK_SIZE, BLOCK_SIZE)
            scales = jnp.maximum(jnp.max(jnp.abs(blocks), axis=-1) / FP6_E2M3_MAX, eps)
            q = _nearest_on_grid(blocks / scales[..., None], _GRID)
            return (q, scales)
        key = jax.random.key(seed)
        k1, k2, k3 = jax.random.split(key, 3)
        x = jax.random.normal(k1, (8, 1024, 128), dtype=jnp.float32)
        weight = jax.random.normal(k2, (128, 128), dtype=jnp.float32) * 0.02
        bias = jax.random.normal(k3, (128,), dtype=jnp.float32) * 0.02
        return {'x': x, 'weight': weight, 'bias': bias}
    _L3_ffn_all = _L3_ffn_setup()
    _L3_ffn_in = {k: v for k, v in _L3_ffn_all.items() if k in ('weight', 'bias')}
    del _L3_ffn_all
    return {'x': x, 'ctx_1024': ctx_1024, 'mask_BxS2_bk0': mask_BxS2_bk0, 'L0_attn_Wk': _L0_attn_in['Wk'], 'L0_attn_bk': _L0_attn_in['bk'], 'L0_attn_Wv': _L0_attn_in['Wv'], 'L0_attn_bv': _L0_attn_in['bv'], 'L0_attn_Wq': _L0_attn_in['Wq'], 'L0_attn_bq': _L0_attn_in['bq'], 'L0_attn_gamma': _L0_attn_in['gamma'], 'L0_attn_beta': _L0_attn_in['beta'], 'L0_xattn_wq': _L0_xattn_in['wq'], 'L0_xattn_bq': _L0_xattn_in['bq'], 'L0_xattn_wk': _L0_xattn_in['wk'], 'L0_xattn_bk': _L0_xattn_in['bk'], 'L0_xattn_wv': _L0_xattn_in['wv'], 'L0_xattn_bv': _L0_xattn_in['bv'], 'L0_xattn_wo': _L0_xattn_in['wo'], 'L0_xattn_bo': _L0_xattn_in['bo'], 'L0_ffn_Wg': _L0_ffn_in['Wg'], 'L0_ffn_bg': _L0_ffn_in['bg'], 'L0_ffn_W1': _L0_ffn_in['W1'], 'L0_ffn_b1': _L0_ffn_in['b1'], 'L0_ffn_W2': _L0_ffn_in['W2'], 'L0_ffn_b2': _L0_ffn_in['b2'], 'L1_attn_Wq': _L1_attn_in['Wq'], 'L1_attn_Wk': _L1_attn_in['Wk'], 'L1_attn_Wv': _L1_attn_in['Wv'], 'L1_attn_Wg': _L1_attn_in['Wg'], 'L1_attn_gk_w1': _L1_attn_in['gk_w1'], 'L1_attn_gk_w2': _L1_attn_in['gk_w2'], 'L1_attn_gk_b2': _L1_attn_in['gk_b2'], 'L1_attn_g_norm_w': _L1_attn_in['g_norm_w'], 'L1_attn_Wo': _L1_attn_in['Wo'], 'L1_xattn_Wq': _L1_xattn_in['Wq'], 'L1_xattn_bq': _L1_xattn_in['bq'], 'L1_xattn_Wk': _L1_xattn_in['Wk'], 'L1_xattn_bk': _L1_xattn_in['bk'], 'L1_xattn_Wv': _L1_xattn_in['Wv'], 'L1_xattn_bv': _L1_xattn_in['bv'], 'L1_xattn_Wo': _L1_xattn_in['Wo'], 'L1_xattn_bo': _L1_xattn_in['bo'], 'L1_xattn_w1': _L1_xattn_in['w1'], 'L1_xattn_b1': _L1_xattn_in['b1'], 'L1_xattn_w2': _L1_xattn_in['w2'], 'L1_xattn_b2': _L1_xattn_in['b2'], 'L1_xattn_w3': _L1_xattn_in['w3'], 'L1_xattn_b3': _L1_xattn_in['b3'], 'L1_ffn_gate_w': _L1_ffn_in['gate_w'], 'L1_ffn_gate_b': _L1_ffn_in['gate_b'], 'L1_ffn_w1': _L1_ffn_in['w1'], 'L1_ffn_b1': _L1_ffn_in['b1'], 'L1_ffn_w2': _L1_ffn_in['w2'], 'L1_ffn_b2': _L1_ffn_in['b2'], 'L1_ffn_w3': _L1_ffn_in['w3'], 'L1_ffn_b3': _L1_ffn_in['b3'], 'L2_attn_W_qkv': _L2_attn_in['W_qkv'], 'L2_attn_W_out': _L2_attn_in['W_out'], 'L2_attn_b_out': _L2_attn_in['b_out'], 'L2_xattn_w_kv': _L2_xattn_in['w_kv'], 'L2_xattn_w_q': _L2_xattn_in['w_q'], 'L2_xattn_w_la': _L2_xattn_in['w_la'], 'L2_xattn_w_proj': _L2_xattn_in['w_proj'], 'L2_xattn_b_proj': _L2_xattn_in['b_proj'], 'L2_xattn_att_weight': _L2_xattn_in['att_weight'], 'L2_ffn_Wq': _L2_ffn_in['Wq'], 'L2_ffn_Wk': _L2_ffn_in['Wk'], 'L2_ffn_Ws': _L2_ffn_in['Ws'], 'L2_ffn_Wd': _L2_ffn_in['Wd'], 'L2_ffn_Wv': _L2_ffn_in['Wv'], 'L2_ffn_Wo': _L2_ffn_in['Wo'], 'L3_attn_W_attn': _L3_attn_in['W_attn'], 'L3_attn_W_proj': _L3_attn_in['W_proj'], 'L3_attn_lora_attn_A': _L3_attn_in['lora_attn_A'], 'L3_attn_lora_attn_B': _L3_attn_in['lora_attn_B'], 'L3_attn_lora_proj_A': _L3_attn_in['lora_proj_A'], 'L3_attn_lora_proj_B': _L3_attn_in['lora_proj_B'], 'L3_attn_bn_gamma': _L3_attn_in['bn_gamma'], 'L3_attn_bn_beta': _L3_attn_in['bn_beta'], 'L3_xattn_Wq': _L3_xattn_in['Wq'], 'L3_xattn_bq': _L3_xattn_in['bq'], 'L3_xattn_Wo': _L3_xattn_in['Wo'], 'L3_xattn_bo': _L3_xattn_in['bo'], 'L3_ffn_weight': _L3_ffn_in['weight'], 'L3_ffn_bias': _L3_ffn_in['bias']}

def reference(x, ctx_1024, mask_BxS2_bk0, L0_attn_Wk, L0_attn_bk, L0_attn_Wv, L0_attn_bv, L0_attn_Wq, L0_attn_bq, L0_attn_gamma, L0_attn_beta, L0_xattn_wq, L0_xattn_bq, L0_xattn_wk, L0_xattn_bk, L0_xattn_wv, L0_xattn_bv, L0_xattn_wo, L0_xattn_bo, L0_ffn_Wg, L0_ffn_bg, L0_ffn_W1, L0_ffn_b1, L0_ffn_W2, L0_ffn_b2, L1_attn_Wq, L1_attn_Wk, L1_attn_Wv, L1_attn_Wg, L1_attn_gk_w1, L1_attn_gk_w2, L1_attn_gk_b2, L1_attn_g_norm_w, L1_attn_Wo, L1_xattn_Wq, L1_xattn_bq, L1_xattn_Wk, L1_xattn_bk, L1_xattn_Wv, L1_xattn_bv, L1_xattn_Wo, L1_xattn_bo, L1_xattn_w1, L1_xattn_b1, L1_xattn_w2, L1_xattn_b2, L1_xattn_w3, L1_xattn_b3, L1_ffn_gate_w, L1_ffn_gate_b, L1_ffn_w1, L1_ffn_b1, L1_ffn_w2, L1_ffn_b2, L1_ffn_w3, L1_ffn_b3, L2_attn_W_qkv, L2_attn_W_out, L2_attn_b_out, L2_xattn_w_kv, L2_xattn_w_q, L2_xattn_w_la, L2_xattn_w_proj, L2_xattn_b_proj, L2_xattn_att_weight, L2_ffn_Wq, L2_ffn_Wk, L2_ffn_Ws, L2_ffn_Wd, L2_ffn_Wv, L2_ffn_Wo, L3_attn_W_attn, L3_attn_W_proj, L3_attn_lora_attn_A, L3_attn_lora_attn_B, L3_attn_lora_proj_A, L3_attn_lora_proj_B, L3_attn_bn_gamma, L3_attn_bn_beta, L3_xattn_Wq, L3_xattn_bq, L3_xattn_Wo, L3_xattn_bo, L3_ffn_weight, L3_ffn_bias):
    import jax
    import jax.numpy as jnp

    def _L0_attn_ref(x, Wk, bk, Wv, bv, Wq, bq, gamma, beta):
        import jax, jax.numpy as jnp
        import numpy as np
        TTT_LR = 0.01
        LN_EPS = 1e-05
        B, S, D = x.shape
        DS = Wk.shape[0]
        mu = jnp.mean(x, axis=-1, keepdims=True)
        var = jnp.mean((x - mu) ** 2, axis=-1, keepdims=True)
        h = (x - mu) * jax.lax.rsqrt(var + LN_EPS) * gamma + beta
        keys = jnp.einsum('bsd,ed->bse', h, Wk) + bk
        values = jnp.einsum('bsd,ed->bse', h, Wv) + bv
        queries = jnp.einsum('bsd,ed->bse', h, Wq) + bq

        def step(W, qkv):
            q_t, k_t, v_t = qkv
            y_t = jnp.einsum('bds,bs->bd', W, q_t)
            pred = jnp.einsum('bds,bs->bd', W, k_t)
            err = pred - v_t
            W = W - TTT_LR * err[:, :, None] * k_t[:, None, :]
            return (W, y_t)
        W0 = jnp.zeros((B, D, DS), x.dtype)
        qs = jnp.swapaxes(queries, 0, 1)
        ks_ = jnp.swapaxes(keys, 0, 1)
        vs = jnp.swapaxes(values, 0, 1)
        _, ys = jax.lax.scan(step, W0, (qs, ks_, vs))
        y = jnp.swapaxes(ys, 0, 1)
        return x + y

    def _L0_xattn_ref(x, memory, mask, wq, bq, wk, bk, wv, bv, wo, bo):
        import jax, jax.numpy as jnp
        import numpy as np
        import math
        B, S, D, H = (2, 256, 128, 16)
        DH = D // H
        b, s, d = x.shape

        def split(t):
            return t.reshape(b, -1, H, DH).transpose(0, 2, 1, 3)
        q = split(x @ wq + bq) * (1.0 / math.sqrt(DH))
        k = split(memory @ wk + bk)
        v = split(memory @ wv + bv)
        logit = jnp.einsum('bhqd,bhkd->bhqk', q, k)
        neg_inf = jnp.finfo(logit.dtype).min
        logit = jnp.where(mask[:, None, None, :], -jnp.inf, logit)
        weights = jax.nn.softmax(logit, axis=-1)
        out = jnp.einsum('bhqk,bhkd->bhqd', weights, v)
        out = out.transpose(0, 2, 1, 3).reshape(b, -1, d)
        return out @ wo + bo

    def _L0_ffn_ref(x, Wg, bg, W1, b1, W2, b2):
        import jax, jax.numpy as jnp
        import numpy as np
        D = 128
        H = 512
        E = 8
        K = 2
        B, S = (4, 256)
        B_, S_, D_ = x.shape
        xt = x.reshape(-1, D_)
        logits = xt @ Wg + bg
        scores = jax.nn.softmax(logits, axis=-1)
        topk_probs, topk_idx = jax.lax.top_k(scores, K)
        h = jnp.einsum('nd,edh->enh', xt, W1) + b1[:, None, :]
        h = jax.nn.gelu(h, approximate=False)
        eo = jnp.einsum('enh,ehd->end', h, W2) + b2[:, None, :]
        eo = jnp.transpose(eo, (1, 0, 2))
        sel = jnp.take_along_axis(eo, topk_idx[:, :, None], axis=1)
        out = jnp.einsum('nk,nkd->nd', topk_probs, sel)
        return out.reshape(B_, S_, D_)

    def _L1_attn_ref(x, Wq, Wk, Wv, Wg, gk_w1, gk_w2, gk_b2, g_norm_w, Wo):
        import jax, jax.numpy as jnp
        import numpy as np
        NUM_HEADS = 4
        CHUNK = 64
        GATE_NORM = 16.0
        EPS = 1e-05

        def _xavier(key, fan_in, fan_out):
            gain = 2.0 ** (-2.5)
            limit = gain * np.sqrt(6.0 / (fan_in + fan_out))
            return jax.random.uniform(key, (fan_in, fan_out), jnp.float32, -limit, limit)

        def _to_chunks(t, B, H, NC, C):
            d = t.shape[-1]
            return t.reshape(B, H, NC, C, d).transpose(2, 0, 1, 3, 4)

        def _gla_forward(x, Wq, Wk, Wv, Wg, gk_w1, gk_w2, gk_b2, g_norm_w, Wo):
            B, L, D = x.shape
            H = NUM_HEADS
            C = CHUNK
            NC = L // C
            q = x @ Wq
            k = x @ Wk
            v = x @ Wv
            gk = jax.nn.log_sigmoid(x @ gk_w1 @ gk_w2 + gk_b2) / GATE_NORM

            def split_heads(t):
                return t.reshape(B, L, H, -1).transpose(0, 2, 1, 3)
            q, k, v, gk = map(split_heads, (q, k, v, gk))
            dk = q.shape[-1]
            scale = dk ** (-0.5)
            qc = _to_chunks(q, B, H, NC, C)
            kc = _to_chunks(k, B, H, NC, C)
            vc = _to_chunks(v, B, H, NC, C)
            gc = _to_chunks(gk, B, H, NC, C)
            Bcum = jnp.cumsum(gc, axis=3)
            causal = jnp.tril(jnp.ones((C, C), jnp.float32))

            def step(Hst, inp):
                qi, ki, vi, bi = inp
                qg = qi * jnp.exp(bi) * scale
                kg = ki * jnp.exp(-bi)
                o_inter = jnp.einsum('bhcd,bhde->bhce', qg, Hst)
                A = jnp.einsum('bhtd,bhsd->bhts', qg, kg) * causal
                o_intra = jnp.einsum('bhts,bhse->bhte', A, vi)
                b_last = bi[:, :, -1:, :]
                kH = ki * jnp.exp(b_last - bi)
                H_new = jnp.exp(b_last).transpose(0, 1, 3, 2) * Hst + jnp.einsum('bhcd,bhce->bhde', kH, vi)
                return (H_new, o_inter + o_intra)
            dv = v.shape[-1]
            H0 = jnp.zeros((B, H, dk, dv), jnp.float32)
            _, oc = jax.lax.scan(step, H0, (qc, kc, vc, Bcum))
            o = oc.transpose(1, 2, 0, 3, 4).reshape(B, H, L, dv)
            o = o.transpose(0, 2, 1, 3)
            rms = jnp.sqrt(jnp.mean(o * o, axis=-1, keepdims=True) + EPS)
            o_n = o / rms * g_norm_w
            g = (x @ Wg).reshape(B, L, H, dv)
            o = o_n * g * jax.nn.sigmoid(g)
            return o.reshape(B, L, H * dv) @ Wo
        return _gla_forward(x, Wq, Wk, Wv, Wg, gk_w1, gk_w2, gk_b2, g_norm_w, Wo)

    def _L1_xattn_ref(query, key, value, Wq, bq, Wk, bk, Wv, bv, Wo, bo, w1, b1, w2, b2, w3, b3):
        import jax, jax.numpy as jnp
        import numpy as np
        import math
        B, S, D, H = (1, 256, 128, 16)
        DK = D // H
        DH = 64
        LOG_T_MIN = math.log(0.1)
        LOG_T_MAX = math.log(10.0)

        def _linear(x, W, b):
            return x @ W.T + b
        b, sq, d = query.shape
        sk = key.shape[1]
        h, dk = (H, DK)
        Q = _linear(query, Wq, bq).reshape(b, sq, h, dk).transpose(0, 2, 1, 3)
        K = _linear(key, Wk, bk).reshape(b, sk, h, dk).transpose(0, 2, 1, 3)
        V = _linear(value, Wv, bv).reshape(b, sk, h, dk).transpose(0, 2, 1, 3)
        qk = jnp.einsum('bhqd,bhkd->bhqk', Q, K)
        scores = qk / math.sqrt(dk)
        mean_sim = scores.mean(axis=(-2, -1))
        max_sim = scores.max(axis=-1).mean(axis=-1)
        probs = jax.nn.softmax(scores, axis=-1)
        entropy_proxy = jnp.var(probs, axis=-1, ddof=1).mean(axis=-1)
        feats = jnp.stack([mean_sim, max_sim, entropy_proxy], axis=-1)
        hidden = jax.nn.gelu(_linear(feats, w1, b1), approximate=False)
        hidden = jax.nn.gelu(_linear(hidden, w2, b2), approximate=False)
        log_t = jnp.clip(_linear(hidden, w3, b3), LOG_T_MIN, LOG_T_MAX)
        t = jnp.exp(log_t)[..., None]
        attn_scores = qk / (2.0 * t)
        attn = jax.nn.softmax(attn_scores, axis=-1)
        attn = jnp.nan_to_num(attn, nan=0.0)
        out = jnp.einsum('bhqk,bhkd->bhqd', attn, V)
        out = out.transpose(0, 2, 1, 3).reshape(b, sq, d)
        return _linear(out, Wo, bo)

    def _L1_ffn_ref(x, gate_w, gate_b, w1, b1, w2, b2, w3, b3):
        import jax, jax.numpy as jnp
        import numpy as np
        B, S, D, O, E, K = (2, 256, 128, 128, 8, 2)
        probs = jax.nn.softmax(x @ gate_w.T + gate_b, axis=-1)
        _, topi = jax.lax.top_k(probs, K)
        onehot = jax.nn.one_hot(topi, E, dtype=probs.dtype)
        cw = jnp.einsum('bske,bsk->bse', onehot, probs[..., :K])
        out = jnp.zeros(x.shape[:2] + (O,), x.dtype)
        for e in range(E):
            h = jax.nn.relu(x @ w1[e] + b1[e])
            h = jax.nn.relu(h @ w2[e] + b2[e])
            h = h @ w3[e] + b3[e]
            out = out + cw[..., e:e + 1] * h
        return out

    def _L2_attn_ref(x, W_qkv, W_out, b_out):
        import jax, jax.numpy as jnp
        import numpy as np
        D_MODEL = 128
        NUM_HEADS = 16
        LOCAL_WINDOW = 128
        GLOBAL_STRIDE = 64
        B, T = (4, 256)

        def _rope_tables(T, d_head, base=10000.0):
            half = d_head // 2
            pos = jnp.arange(T, dtype=jnp.float32)[:, None]
            inv_freq = 1.0 / base ** (jnp.arange(half, dtype=jnp.float32) / half)
            ang = pos * inv_freq[None, :]
            return (jnp.cos(ang), jnp.sin(ang))

        def _rope_apply(x, cos_h, sin_h):
            xe = x[..., 0::2]
            xo = x[..., 1::2]
            re = xe * cos_h - xo * sin_h
            ro = xe * sin_h + xo * cos_h
            return jnp.stack([re, ro], axis=-1).reshape(x.shape)
        Bx, Tx, C = x.shape
        H = NUM_HEADS
        dh = C // H
        qkv = x @ W_qkv
        qkv = qkv.reshape(Bx, Tx, 3, H, dh)
        q, k, v = (qkv[:, :, 0], qkv[:, :, 1], qkv[:, :, 2])
        q = jnp.transpose(q, (0, 2, 1, 3))
        k = jnp.transpose(k, (0, 2, 1, 3))
        v = jnp.transpose(v, (0, 2, 1, 3))
        cos_h, sin_h = _rope_tables(Tx, dh)
        q = _rope_apply(q, cos_h, sin_h)
        k = _rope_apply(k, cos_h, sin_h)
        scores = jnp.einsum('bhtd,bhkd->bhtk', q, k) / jnp.sqrt(jnp.float32(dh))
        lw = min(LOCAL_WINDOW, Tx)
        gs = max(1, GLOBAL_STRIDE)
        q_idx = jnp.arange(Tx)
        k_idx = jnp.arange(Tx)
        rel = k_idx[None, :] - q_idx[:, None]
        local_ok = (rel <= 0) & (rel >= -(lw - 1))
        key_global = (k_idx % gs == 0)[None, :]
        query_is_global = (q_idx % gs == 0)[:, None]
        allowed = (local_ok | key_global | query_is_global) & (rel <= 0)
        allowed = allowed[None, None, :, :]
        scores = jnp.where(allowed, scores, jnp.float32(-1000000000.0))
        w = jax.nn.softmax(scores, axis=-1)
        out = jnp.einsum('bhtk,bhkd->bhtd', w, v)
        out = jnp.transpose(out, (0, 2, 1, 3)).reshape(Bx, Tx, C)
        return out @ W_out + b_out

    def _L2_xattn_ref(x, cls, w_kv, w_q, w_la, w_proj, b_proj, att_weight):
        import jax, jax.numpy as jnp
        import numpy as np
        DIM = 128
        HEADS = 16
        HEAD_DIM = DIM // HEADS
        SCALE = HEAD_DIM ** (-0.5)
        B, N, C = cls.shape
        Nx = x.shape[1]
        H, D = (HEADS, C // HEADS)
        kv = (x @ w_kv).reshape(B, Nx, 2, H, D)
        k = jnp.transpose(kv[:, :, 0], (0, 2, 1, 3))
        v = jnp.transpose(kv[:, :, 1], (0, 2, 1, 3))
        q = jnp.transpose((cls @ w_q).reshape(B, N, H, D), (0, 2, 1, 3))
        attn = jax.nn.softmax(jnp.einsum('bhnd,bhmd->bhnm', q, k) * SCALE, axis=-1)
        g = jnp.transpose(x @ w_la, (0, 2, 1))
        g_mean = jnp.mean(g, axis=-1)[:, :, None, None]
        g_max = jnp.max(g, axis=-1)[:, :, None, None]
        gate = 0.5 * g_mean + 0.5 * g_max
        attn2 = jax.nn.softmax(gate * attn, axis=-1)
        w = att_weight[0]
        attn = w * attn2 + (1.0 - w) * attn
        out = jnp.einsum('bhnm,bhmd->bnhd', attn, v).reshape(B, N, C)
        return out @ w_proj + b_proj

    def _L2_ffn_ref(x, Wq, Wk, Ws, Wd, Wv, Wo):
        import jax, jax.numpy as jnp
        import numpy as np
        B, T, D = (4, 256, 128)
        H, DH, E, SEL = (8, 64, 5, 2)

        def _topk_mask(logits, k):
            _, idx = jax.lax.top_k(logits, k)
            return jnp.sum(jax.nn.one_hot(idx, logits.shape[-1], dtype=logits.dtype), axis=-2)
        e, d, dh = Wv.shape
        h = Wq.shape[1] // dh
        b, t, _ = x.shape
        scale = dh ** (-0.5)
        q = (x @ Wq).reshape(b, t, h, dh).transpose(0, 2, 1, 3)
        k = (x @ Wk).reshape(b, t, h, dh).transpose(0, 2, 1, 3)
        gl_v = (x @ Ws).reshape(b, t, h, e)
        wv = _topk_mask(gl_v, SEL) * jax.nn.sigmoid(gl_v)
        xv = jnp.einsum('btd,edk->btek', x, Wv)
        v = jnp.einsum('bthe,btek->bhtk', wv, xv)
        scores = jnp.einsum('bhid,bhjd->bhij', q * scale, k)
        probs = jax.nn.softmax(scores, axis=-1)
        attn = jnp.einsum('bhij,bhjd->bihd', probs, v)
        gl_o = (x @ Wd).reshape(b, t, h, e)
        mask_o = _topk_mask(gl_o, SEL)
        out = jnp.einsum('bthe,bthk,ekd->btd', mask_o, attn, Wo)
        return out

    def _L3_attn_ref(x, W_attn, W_proj, lora_attn_A, lora_attn_B, lora_proj_A, lora_proj_B, bn_gamma, bn_beta):
        import jax, jax.numpy as jnp
        import numpy as np
        B, T, C, R = (8, 128, 128, 64)
        EPS = 1e-05
        Bb, Tt, Cc = x.shape
        Wm_attn = W_attn + (lora_attn_A @ lora_attn_B).reshape(W_attn.shape)
        xa = jnp.einsum('btc,dc->btd', x, Wm_attn)
        mean = xa.mean(axis=(0, 1))
        var = xa.var(axis=(0, 1))
        xa = (xa - mean) * jax.lax.rsqrt(var + EPS) * bn_gamma + bn_beta
        q, k, v = jnp.split(xa, 3, axis=-1)
        scale = 1.0 / jnp.sqrt(jnp.asarray(Cc, dtype=x.dtype))
        att = jnp.einsum('btc,bsc->bts', q, k) * scale
        causal = jnp.tril(jnp.ones((Tt, Tt), dtype=bool))
        att = jnp.where(causal[None, :, :], att, -jnp.inf)
        att = jax.nn.softmax(att, axis=-1)
        y = jnp.einsum('bts,bsc->btc', att, v)
        y = jnp.einsum('btc,dc->btd', y, W_proj)
        Wm_proj = W_proj + (lora_proj_A @ lora_proj_B).reshape(W_proj.shape)
        y = jnp.einsum('btc,dc->btd', y, Wm_proj)
        return y

    def _L3_xattn_ref(Q, K, V, Wq, bq, Wo, bo):
        import jax, jax.numpy as jnp
        import numpy as np
        N_HEAD = 16
        D_MODEL = 128
        D_K = D_MODEL // N_HEAD

        def _split_heads(x, B):
            return x.reshape(B, -1, N_HEAD, D_K).transpose(0, 2, 1, 3)
        B = Q.shape[0]
        q = _split_heads(Q @ Wq + bq, B)
        k = _split_heads(K @ Wq + bq, B)
        v = _split_heads(V @ Wq + bq, B)
        scores = jnp.einsum('bhqd,bhkd->bhqk', q, k) / jnp.sqrt(jnp.asarray(D_K, q.dtype))
        attn = jax.nn.softmax(scores, axis=-1)
        out = jnp.einsum('bhqk,bhkd->bhqd', attn, v)
        out = out.transpose(0, 2, 1, 3).reshape(B, -1, D_MODEL)
        return out @ Wo + bo

    def _L3_ffn_ref(x, weight, bias):
        import jax, jax.numpy as jnp
        import numpy as np
        BLOCK_SIZE = 32
        FP6_E2M3_MAX = 7.5

        def _build_fp6_e2m3_grid():
            vals = set()
            for bits in range(64):
                s = bits >> 5 & 1
                e = bits >> 3 & 3
                m = bits & 7
                v = m / 8.0 if e == 0 else (1.0 + m / 8.0) * 2.0 ** (e - 1)
                vals.add(-v if s else v)
            return np.array(sorted(vals), dtype=np.float32)
        _GRID = jnp.asarray(_build_fp6_e2m3_grid())

        def _nearest_on_grid(x, grid):
            idx = jnp.clip(jnp.searchsorted(grid, x), 0, grid.shape[0] - 1)
            idx_lo = jnp.maximum(idx - 1, 0)
            v_hi = grid[idx]
            v_lo = grid[idx_lo]
            return jnp.where(jnp.abs(x - v_lo) <= jnp.abs(x - v_hi), v_lo, v_hi)

        def _mx_quantize(t, eps=1e-30):
            rows, K = t.shape
            blocks = t.reshape(rows, K // BLOCK_SIZE, BLOCK_SIZE)
            scales = jnp.maximum(jnp.max(jnp.abs(blocks), axis=-1) / FP6_E2M3_MAX, eps)
            q = _nearest_on_grid(blocks / scales[..., None], _GRID)
            return (q, scales)
        batch_shape = x.shape[:-1]
        in_features = x.shape[-1]
        x2 = x.astype(jnp.float32).reshape(-1, in_features)
        w2 = weight.astype(jnp.float32)
        xq, xs = _mx_quantize(x2)
        wq, ws = _mx_quantize(w2)
        xd = (xq * xs[..., None]).reshape(x2.shape)
        wd = (wq * ws[..., None]).reshape(w2.shape)
        out = xd @ wd.T + bias
        return out.reshape(*batch_shape, -1)
    x = _layernorm(x + _L0_attn_ref(x, L0_attn_Wk, L0_attn_bk, L0_attn_Wv, L0_attn_bv, L0_attn_Wq, L0_attn_bq, L0_attn_gamma, L0_attn_beta), axis=-1)
    x = _layernorm(x + _L0_xattn_ref(x, ctx_1024, mask_BxS2_bk0, L0_xattn_wq, L0_xattn_bq, L0_xattn_wk, L0_xattn_bk, L0_xattn_wv, L0_xattn_bv, L0_xattn_wo, L0_xattn_bo), axis=-1)
    x = _layernorm(x + _L0_ffn_ref(x, L0_ffn_Wg, L0_ffn_bg, L0_ffn_W1, L0_ffn_b1, L0_ffn_W2, L0_ffn_b2), axis=-1)
    x = _layernorm(x + _L1_attn_ref(x, L1_attn_Wq, L1_attn_Wk, L1_attn_Wv, L1_attn_Wg, L1_attn_gk_w1, L1_attn_gk_w2, L1_attn_gk_b2, L1_attn_g_norm_w, L1_attn_Wo), axis=-1)
    x = _layernorm(x + _L1_xattn_ref(x, ctx_1024, ctx_1024, L1_xattn_Wq, L1_xattn_bq, L1_xattn_Wk, L1_xattn_bk, L1_xattn_Wv, L1_xattn_bv, L1_xattn_Wo, L1_xattn_bo, L1_xattn_w1, L1_xattn_b1, L1_xattn_w2, L1_xattn_b2, L1_xattn_w3, L1_xattn_b3), axis=-1)
    x = _layernorm(x + _L1_ffn_ref(x, L1_ffn_gate_w, L1_ffn_gate_b, L1_ffn_w1, L1_ffn_b1, L1_ffn_w2, L1_ffn_b2, L1_ffn_w3, L1_ffn_b3), axis=-1)
    x = _layernorm(x + _L2_attn_ref(x, L2_attn_W_qkv, L2_attn_W_out, L2_attn_b_out), axis=-1)
    x = _layernorm(x + _L2_xattn_ref(ctx_1024, x, L2_xattn_w_kv, L2_xattn_w_q, L2_xattn_w_la, L2_xattn_w_proj, L2_xattn_b_proj, L2_xattn_att_weight), axis=-1)
    x = _layernorm(x + _L2_ffn_ref(x, L2_ffn_Wq, L2_ffn_Wk, L2_ffn_Ws, L2_ffn_Wd, L2_ffn_Wv, L2_ffn_Wo), axis=-1)
    x = _layernorm(x + _L3_attn_ref(x, L3_attn_W_attn, L3_attn_W_proj, L3_attn_lora_attn_A, L3_attn_lora_attn_B, L3_attn_lora_proj_A, L3_attn_lora_proj_B, L3_attn_bn_gamma, L3_attn_bn_beta), axis=-1)
    x = _layernorm(x + _L3_xattn_ref(x, ctx_1024, ctx_1024, L3_xattn_Wq, L3_xattn_bq, L3_xattn_Wo, L3_xattn_bo), axis=-1)
    x = _layernorm(x + _L3_ffn_ref(x, L3_ffn_weight, L3_ffn_bias), axis=-1)
    return x

_drawn_inputs = setup_inputs


def setup_inputs(seed=0):
    import zlib

    import numpy as np

    out = dict(_drawn_inputs(seed))
    spreads = {'L0_attn_bk': (0.0, 0.1),
     'L0_attn_bv': (0.0, 0.1),
     'L0_attn_bq': (0.0, 0.1),
     'L0_attn_gamma': (1.0, 0.2),
     'L0_attn_beta': (0.0, 0.1),
     'L1_attn_gk_b2': (0.0, 2.0),
     'L1_attn_g_norm_w': (1.0, 0.6),
     'L1_ffn_gate_b': (0.0, 0.1),
     'L1_ffn_b1': (0.0, 0.75),
     'L1_ffn_b2': (0.0, 0.537),
     'L1_ffn_b3': (0.0, 0.408),
     'L2_attn_b_out': (0.0, 0.1),
     'L3_attn_bn_gamma': (1.0, 0.6),
     'L3_attn_bn_beta': (0.0, 0.8),
     'L3_xattn_bq': (0.0, 0.1),
     'L3_xattn_bo': (0.0, 0.1)}
    factors = {'L0_xattn_bq': 5.78,
     'L0_xattn_bk': 200.0,
     'L0_ffn_bg': 4.089,
     'L0_ffn_b1': 4.949,
     'L0_ffn_b2': 3.944,
     'L1_attn_Wq': 2.861,
     'L1_attn_Wk': 2.858,
     'L1_attn_Wg': 2.933,
     'L1_attn_gk_w1': 8.0,
     'L1_attn_gk_w2': 8.0,
     'L1_xattn_Wq': 8.0,
     'L1_xattn_bq': 22.227,
     'L1_xattn_Wk': 8.0,
     'L1_xattn_bk': 64.0,
     'L1_xattn_bv': 5.001,
     'L1_xattn_w1': 26.195,
     'L1_xattn_b1': 163.034,
     'L1_xattn_w2': 130.596,
     'L1_xattn_b2': 8.0,
     'L1_xattn_w3': 128.818,
     'L2_xattn_w_la': 200.0,
     'L2_xattn_b_proj': 5.481,
     'L2_ffn_Wq': 8.0,
     'L2_ffn_Wk': 8.0,
     'L3_attn_lora_attn_A': 8.0,
     'L3_attn_lora_attn_B': 8.0,
     'L3_attn_lora_proj_A': 8.0,
     'L3_attn_lora_proj_B': 8.0,
     'L3_ffn_bias': 2.953}
    for name, (base, spread) in spreads.items():
        noise = np.random.default_rng([zlib.crc32(name.encode()), seed]).standard_normal(out[name].shape)
        drawn = base * np.exp(spread * noise) if base else spread * noise
        out[name] = jnp.asarray(drawn.astype(out[name].dtype))
    for name, factor in factors.items():
        out[name] = (out[name] * factor).astype(out[name].dtype)
    return out
```

```python
from contextlib import ExitStack

import numpy as np

import concourse.bass as bass
from concourse import mybir

F32 = mybir.dt.float32
BF16 = mybir.dt.bfloat16
U8 = mybir.dt.uint8
ALU = mybir.AluOpType
ACT = mybir.ActivationFunctionType
AX = mybir.AxisListType

BATCH, TOK, DIM, CTX = 8, 128, 128, 77
GROUP = 4
GROUPS = BATCH // GROUP
GT = GROUP * TOK
GC = GROUP * CTX
HEADS, DH = 16, 8
HALF = 8
UNITS = 2 * GROUP
EPS = 1e-5
TTT_LR = 0.01
GATE_NORM = 16.0
CHUNK = 64
MASKED = -1e30
ROUND = 1.5 * 2.0 ** 23


def columns(pieces):
    at, n = {}, 0
    for name, width in pieces:
        at[name] = (n, width)
        n += width
    return at, n


W128_PIECES = [
    ("l0a_gamma", 1), ("l0a_beta", 1), ("l0a_wk", 64), ("l0a_wq", 64), ("l0a_wv", 128),
    ("l0x_wq", 128), ("l0x_wk", 128), ("l0x_wv", 128), ("l0x_wo", 128), ("l0x_bq", 1), ("l0x_bk", 1),
    ("l0f_wg", 8), ("l0f_b1", 32), ("l0f_w1", 4096), ("l0f_w2", 4096),
    ("l1a_wq", 128), ("l1a_wk", 128), ("l1a_wv", 256), ("l1a_wg", 256), ("l1a_w1", 16), ("l1a_b2", 1),
    ("l1a_wo", 256),
    ("l1x_wq", 128), ("l1x_wk", 128), ("l1x_wv", 128), ("l1x_wo", 128), ("l1x_bq", 1), ("l1x_bk", 1),
    ("l1f_wg", 8), ("l1f_b1", 8), ("l1f_b2", 8), ("l1f_w1", 1024), ("l1f_w2", 1024), ("l1f_w3", 1024),
    ("l2a_wq", 128), ("l2a_wk", 128), ("l2a_wqs", 128), ("l2a_wks", 128), ("l2a_wv", 128), ("l2a_wo", 128),
    ("l2x_wk", 128), ("l2x_wv", 128), ("l2x_wq", 128), ("l2x_wla", 16), ("l2x_wo", 128),
    ("l2f_wq", 512), ("l2f_wk", 512), ("l2f_wg", 80), ("l2f_wv", 320), ("l2f_wo", 256),
    ("l3a_w", 384), ("l3a_wp", 128), ("l3a_wpT", 128), ("l3a_gamma", 3), ("l3a_beta", 3),
    ("l3x_wq", 128), ("l3x_wo", 128), ("l3x_bq", 1), ("l3f_w", 128),
]
W128, W128_N = columns(W128_PIECES)
W128_CUTS = ["l0f_w1", "l0f_w2", "l1a_wq", "l2a_wq"]
W64, W64_N = columns([("l0a_bk", 1), ("l0a_bq", 1), ("l1x_w2", 64), ("l1x_w3", 1), ("l1x_b1", 1), ("l1x_b2", 1),
                      ("l2f_wo2", 128), ("l3a_A", 128), ("l3a_B", 384), ("l3a_pA", 128), ("l3a_pB", 128)])
ROW, ROW_N = columns([("l0a_bv", 128), ("l0x_bv", 128), ("l0x_bo", 128), ("l0f_bg", 8), ("l1a_gn", 64),
                      ("l1x_bv", 128), ("l1x_bo", 128), ("l1x_w1", 192), ("l1x_b3", 1), ("l1f_bg", 8),
                      ("l2a_bo", 128), ("l2x_bo", 128), ("l2x_w", 1), ("l3x_bv", 128), ("l3x_bo", 128),
                      ("l3f_b", 128)])
CON, CON_N = columns([("ident", 128), ("hm8", 8), ("hm16", 16), ("hm4", 4), ("low", 128), ("up", 128),
                      ("sup", 128), ("incl", 128), ("causal", 128), ("scan", 512), ("tie8", 64), ("tie5", 25),
                      ("cos", 128), ("sin", 128), ("ones", 128)])


def constants():
    c = np.zeros((128, CON_N), np.float32)

    def put(name, a):
        o, w = CON[name]
        c[:, o:o + w] = np.asarray(a, np.float32).reshape(-1, w)

    d = np.arange(128)
    put("ident", np.eye(128))
    put("hm8", (d[:, None] % 64) // DH == np.arange(8))
    put("hm16", d[:, None] // DH == np.arange(16))
    put("hm4", d[:, None] // 32 == np.arange(4))
    put("low", -TTT_LR * (d[:, None] > d[None, :]))
    put("up", -TTT_LR * (d[:, None] < d[None, :]))
    put("sup", d[:, None] < d[None, :])
    put("incl", d[:, None] <= d[None, :])
    put("causal", np.where(d[None, :] > d[:, None], MASKED, 0.0))
    put("scan", np.tile((np.arange(512) % CHUNK != 0), (128, 1)))
    put("tie8", np.tile((np.arange(8)[None, :] < np.arange(8)[:, None]).reshape(1, 64), (128, 1)))
    put("tie5", np.tile((np.arange(5)[None, :] < np.arange(5)[:, None]).reshape(1, 25), (128, 1)))
    half = DH // 2
    inv = (1.0 / 10000.0 ** (np.arange(half, dtype=np.float32) / half)).astype(np.float32)
    ang = d.astype(np.float32)[None, :] * inv[(d % DH) // 2][:, None]
    put("cos", np.cos(ang))
    put("sin", np.sin(ang) * np.where(d % 2 == 0, -1.0, 1.0)[:, None])
    put("ones", np.ones((128, 128)))
    return c


def decoder(nc, x_in, ctx_in, mask_in, w128_in, w64_in, w16_in, w8_in, row_in, con_in, out):
    with ExitStack() as ctx:
        def sb(name, shape, dt=F32):
            return ctx.enter_context(nc.sbuf_tensor(name, shape, dt))

        body_sems, once_sems = {}, {}

        shared = {"l3a_normed": "l0a_kT", "l3a_v": "l0a_v", "l3a_v_kept": "l0a_qT", "l3a_scores": "l0a_kk",
                  "l3a_shifted": "l0a_masked", "l3a_exp": "l0a_k_kept", "l3a_pT": "l0a_kq", "l3a_pT_kept": "l0a_q_kept",
                  "l3a_o": "l0a_level", "l3f_quantised": "l0a_u", "l3f_turned": "l0a_step", "l3f_kept": "l0a_powers",
                  "l3f_y": "l0a_y", "dve_chain2": "dve_chain"}

        def sem(name):
            name = shared.get(name, name)
            if name not in body_sems:
                body_sems[name] = ctx.enter_context(nc.semaphore(name))
            return body_sems[name]

        def once(name):
            if name not in once_sems:
                once_sems[name] = ctx.enter_context(nc.semaphore(name))
            return once_sems[name]

        def bc(ap, axis, n):
            a = ap.unsqueeze(axis)
            shape = list(a.shape)
            shape[axis] = n
            return a.to_broadcast(shape)

        w128 = sb("w128", [128, W128_N])
        w64 = sb("w64", [64, W64_N])
        w16 = sb("w16", [16, 128])
        w8 = sb("w8", [8, 256])
        row = sb("row", [128, ROW_N])
        con = sb("con", [128, CON_N])
        ident_bf = sb("ident_bf", [128, 128], BF16)
        causal_bf = sb("causal_bf", [128, 4, 128], BF16)
        ones_bf = sb("ones_bf", [1, 128], BF16)
        eps_col = sb("eps_col", [128, 1])
        one_col = sb("one_col", [128, 1])
        w3_rep = sb("w3_rep", [64, 128])
        att_mix = sb("att_mix", [128, 1])
        l3_wT = sb("l3_wT", [128, 384])
        l3_proj = sb("l3_proj", [128, 128])
        l3_wpT = sb("l3_wpT", [128, 128])
        x_all = sb("x_all", [128, BATCH * DIM])
        ctx_all = sb("ctx_all", [128, BATCH * CTX])
        mask_u8 = sb("mask_u8", [1, BATCH * CTX], U8)
        qkv_all = sb("qkv_all", [128, 3, BATCH * TOK])

        X = sb("X", [128, GROUP, DIM])
        XR = sb("XR", [128, GROUP, DIM])
        Y = sb("Y", [128, GROUP, DIM])
        XT = sb("XT", [128, GT])
        CT = sb("CT", [128, GC])
        stats = sb("stats", [128, GROUP, 6])
        mv = sb("mv", [128, GROUP, 2])
        rstd = sb("rstd", [128, GROUP])

        QT = sb("QT", [128, 1, GT])
        KT = sb("KT", [128, 1, GT])
        V = sb("V", [128, GROUP, HEADS, DH + 1])
        VB = sb("VB", [128, GROUP, 4, 128])
        KB = sb("KB", [128, 2, HALF, 128])
        E = sb("E", [128, 3, HALF * 128])
        E2 = sb("E2", [128, 2, HALF * 128])
        PT = sb("PT", [128, 2, HALF * 128])
        mx = sb("mx", [128, UNITS, HALF])
        rec = sb("rec", [128, GROUP, 2, HEADS])
        ON = sb("ON", [128, GROUP, 256])
        ONT = sb("ONT", [128, 2, 2, 128])
        mask_b = sb("mask_b", [1, GROUP, 4, CTX], BF16)
        big = sb("big", [128, UNITS, HALF * CTX])
        big2 = big[:].rearrange("p u k -> p (u k)")[:, 0:4096]
        small = sb("small", [128, 2048])

        def w(name, a=0, n=None):
            o, width = W128[name]
            return w128[:, o + a:o + a + (width if n is None else n)]

        def h64(name, a=0, n=None):
            o, width = W64[name]
            return w64[:, o + a:o + a + (width if n is None else n)]

        def r(name, a=0, n=None):
            o, width = ROW[name]
            return row[:, o + a:o + a + (width if n is None else n)]

        def c(name, a=0, n=None):
            o, width = CON[name]
            return con[:, o + a:o + a + (width if n is None else n)]

        ident = c("ident")

        PS = ctx.enter_context(nc.psum_tensor("PS", [128, 8, 512], F32))

        def bank(b, n=512):
            return PS[:, b, 0:n]

        y_ps = PS[:, 7, 0:128]
        ont_ps = PS[:, 7, 256:384]
        xt_ps = PS[:, 7, 384:512]

        block = ctx.enter_context(nc.Block())

        def linker(eng, name):
            count = [0]

            def link(ins):
                count[0] += 1
                ins.then_inc(sem(name), 1)
                eng.wait_ge(sem(name), count[0])
            return link

        def norm_stats(dve, link, n, g, y, res):
            link(nc.vector.tensor_tensor(Y[:, g], y, res[:, g], ALU.add))
            link(nc.vector.bn_stats(stats[:, g], Y[:, g]))
            nc.vector.bn_aggr(mv[:, g], stats[:, g]).then_inc(sem("norm_var"), 1)

        def norm_rstd(act, link, n, g):
            act.wait_ge(sem("norm_var"), n * GROUP + g + 1)
            link(nc.scalar.activation(rstd[:, g:g + 1], mv[:, g, 1:2], ACT.Ln, bias=eps_col[:, 0:1]))
            nc.scalar.activation(rstd[:, g:g + 1], rstd[:, g:g + 1], ACT.Exp, scale=-0.5).then_inc(sem("norm_rstd"), 1)

        def norm_apply(dve, n, g, src, dst):
            dve.wait_ge(sem("norm_var"), n * GROUP + g + 1)
            dve.wait_ge(sem("norm_rstd"), n * GROUP + g + 1)
            nc.vector.tensor_scalar(dst, src, mv[:, g, 0:1], rstd[:, g:g + 1],
                                    ALU.subtract, ALU.mult).then_inc(sem("x_ready"), 1)

        def turn_x(pe, n, g, src):
            pe.wait_ge(sem("x_ready"), n * GROUP + g + 1)
            if n * GROUP + g > 0:
                pe.wait_ge(sem("xT_ready"), n * GROUP + g)
            nc.tensor.transpose(xt_ps, src, ident).then_inc(sem("xT_turned"), 1)

        def keep_xT(act, n, g):
            act.wait_ge(sem("xT_turned"), n * GROUP + g + 1)
            nc.scalar.activation(XT[:, g * 128:(g + 1) * 128], xt_ps, ACT.Copy).then_inc(sem("xT_ready"), 1)

        def norms_dve(dve, link, n, ready, y, res, outs=None):
            for g in range(GROUP + 1):
                if g < GROUP:
                    dve.wait_ge(sem(ready), g + 1)
                    norm_stats(dve, link, n, g, y(g), res)
                if g >= 1:
                    norm_apply(dve, n, g - 1, Y[:, g - 1], X[:, g - 1] if outs is None else outs(g - 1))

        def norms_act(act, link, n):
            for g in range(GROUP + 1):
                if g < GROUP:
                    norm_rstd(act, link, n, g)
                if g >= 1:
                    keep_xT(act, n, g - 1)

        def norms_pe(pe, n):
            for g in range(GROUP):
                turn_x(pe, n, g, X[:, g])

        def add_bias(pool, n, bias):
            pool.wait_ge(sem("x_ready"), (n + 1) * GROUP)
            nc.gpsimd.tensor_tensor(XR[:], X[:], bc(bias, 1, GROUP), ALU.add).then_inc(sem("residual"), 1)

        def spread_keys(pool, a, g, K):
            if a * GROUP + g >= 2:
                pool.wait_ge(sem("scores"), (a * GROUP + g - 2) * 2 + 2)
            nc.gpsimd.tensor_tensor(KB[:, g % 2, :, 0:K], bc(KT[:, 0, g * K:(g + 1) * K], 1, HALF),
                                    bc(c("hm8"), 2, K), ALU.mult).then_inc(sem("keys_spread"), 1)

        def s_view(u, K):
            b = 2 * (u % 2)
            return PS[:, b:b + 2, 0:4 * K].rearrange("p b (h k) -> p b h k", h=4)

        def scores(pe, a, u, K, extra=None):
            g, p = u // 2, 64 * (u % 2)
            pe.wait_ge(sem("keys_spread"), a * GROUP + g + 1)
            if a * UNITS + u >= 2:
                pe.wait_ge(sem("shifted"), a * UNITS + u - 1)
            for j in range(2):
                o = PS[:, 2 * (u % 2) + j, 0:4 * K]
                m = nc.tensor.matmul(o, QT[p:p + 64, 0, g * 128:(g + 1) * 128],
                                     KB[p:p + 64, g % 2, 4 * j:4 * j + 4, 0:K], start=True, stop=extra is None)
                if extra is not None:
                    m = nc.tensor.matmul(o, extra[0], extra[1](g), start=False, stop=True)
            m.then_inc(sem("scores"), 1)

        def shift(dve, link, a, u, K, dst):
            dve.wait_ge(sem("scores"), a * UNITS + u + 1)
            s = s_view(u, K)
            m = mx[:, u].rearrange("p (b h) -> p b h", b=2)
            link(nc.vector.tensor_reduce(m, s, AX.X, ALU.max))
            nc.vector.tensor_tensor(dst.rearrange("p (b h k) -> p b h k", b=2, h=4), s, bc(m, 3, K),
                                    ALU.subtract).then_inc(sem("shifted"), 1)

        def turn_probs(pe, m, K, src):
            if m >= 1:
                pe.wait_ge(sem("probs_kept"), m)
            for h in range(HALF):
                t = nc.tensor.transpose(PS[0:K, 4 + h // 4, (h % 4) * 128:(h % 4) * 128 + 128],
                                        src[:, h * K:(h + 1) * K], ident)
            t.then_inc(sem("probs_turned"), 1)

        def keep_probs(act, m, K):
            act.wait_ge(sem("probs_turned"), m + 1)
            if m >= 2:
                act.wait_ge(sem("values_done"), m - 1)
            nc.scalar.activation(PT[0:K, m % 2, :].rearrange("p (b k) -> p b k", b=2), PS[0:K, 4:6, :],
                                 ACT.Copy).then_inc(sem("probs_kept"), 1)

        def o_view(slot):
            return PS[:, 6, 144 * slot:144 * slot + 144].rearrange("p (h d) -> p h d", h=HEADS)

        def values(pe, m, u, K, slot):
            pe.wait_ge(sem("probs_kept"), m + 1)
            g, half = u // 2, u % 2
            for h in range(HALF):
                t = nc.tensor.matmul(o_view(slot)[:, half * HALF + h], PT[0:K, m % 2, h * 128:(h + 1) * 128],
                                     V[0:K, g, half * HALF + h, :], start=True, stop=True)
            t.then_inc(sem("values_done"), 1)

        def normalise(dve, link, m, g):
            dve.wait_ge(sem("values_done"), m + 1)
            o = o_view(0)
            link(nc.vector.reciprocal(rec[:, g, 0], o[:, :, DH]))
            nc.vector.tensor_tensor(ON[:, g, 0:128].rearrange("p (h d) -> p h d", h=HEADS), o[:, :, 0:DH],
                                    bc(rec[:, g, 0], 2, DH), ALU.mult).then_inc(sem("attended"), 1)

        def turn_out(pe, o, g, n):
            pe.wait_ge(sem("attended"), o + 1)
            pe.wait_ge(sem("xT_ready"), n * GROUP + g)
            nc.tensor.transpose(ont_ps, ON[:, g, 0:128], ident).then_inc(sem("out_turned"), 1)

        def keep_out(act, o, g):
            act.wait_ge(sem("out_turned"), o + 1)
            nc.scalar.activation(ONT[:, g % 2, 0], ont_ps, ACT.Copy).then_inc(sem("out_kept"), 1)

        def project_out(pe, o, g, weights):
            pe.wait_ge(sem("out_kept"), o + 1)
            nc.tensor.matmul(y_ps, ONT[:, g % 2, 0], weights, start=True, stop=True).then_inc(sem("y_done"), 1)

        STEPS = 2 * GROUP + 6

        def attend_pe(pe, a, m0, o0, n, K, weights, extra=None, scored=False, probs="exps", probs0=0):
            for i in range(STEPS):
                if 2 <= i < UNITS + 2:
                    pe.wait_ge(sem(probs), probs0 + i - 1)
                    turn_probs(pe, m0 + i - 2, K, E[:, (i - 2) % 3])
                if i < UNITS and not scored:
                    scores(pe, a, i, K, extra)
                if 2 <= i < UNITS + 2:
                    if i % 2 == 0 and i > 2:
                        pe.wait_ge(sem("attended"), o0 + (i - 2) // 2)
                    values(pe, m0 + i - 2, i - 2, K, 0)
                if i >= 7 and i % 2:
                    turn_x(pe, n, (i - 7) // 2, X[:, (i - 7) // 2])
                if i >= 5 and i % 2 and (i - 5) // 2 < GROUP:
                    g = (i - 5) // 2
                    turn_out(pe, o0 + g, g, n)
                    project_out(pe, o0 + g, g, weights)

        def attend_act(act, link, m0, o0, n, K, exp, last=False):
            for i in range(STEPS):
                if 2 <= i < UNITS + 2:
                    keep_probs(act, m0 + i - 2, K)
                if i < UNITS:
                    exp(i)
                if i >= 7 and i % 2:
                    keep_xT(act, n, (i - 7) // 2)
                if i >= 5 and i % 2 and (i - 5) // 2 < GROUP:
                    keep_out(act, o0 + (i - 5) // 2, (i - 5) // 2)
                if i >= 6 and i % 2 == 0:
                    norm_rstd(act, link, n, (i - 6) // 2)

        def attend_dve(dve, link, m0, o0, n, res, unit):
            for i in range(STEPS):
                if i >= 4 and i % 2 == 0 and (i - 4) // 2 < GROUP:
                    normalise(dve, link, m0 + i - 3, (i - 4) // 2)
                if i < UNITS:
                    unit(i)
                if i >= 6 and i % 2 == 0:
                    g = (i - 6) // 2
                    dve.wait_ge(sem("y_done"), o0 + g + 1)
                    norm_stats(dve, link, n, g, y_ps, res)
                if i >= 7 and i % 2:
                    norm_apply(dve, n, (i - 7) // 2, Y[:, (i - 7) // 2], X[:, (i - 7) // 2])

        def project_ctx(pe, a, n, wq, wk, wv, bv=None):
            pe.wait_ge(once("w128_loaded"), 16 * (len(W128_CUTS) + 1))
            pe.wait_ge(sem("xT_ready"), (n + 1) * GROUP)
            nc.tensor.matmul(bank(0), wq, XT[:, :], start=True, stop=True).then_inc(sem("q_psum"), 1)
            nc.tensor.matmul(bank(1, GC), wk, CT[:, :], start=True, stop=True).then_inc(sem("k_psum"), 1)
            for g in range(GROUP):
                m = nc.tensor.matmul(PS[0:CTX, 2, g * 128:(g + 1) * 128], CT[:, g * CTX:(g + 1) * CTX], wv,
                                     start=True, stop=True)
            m.then_inc(sem("v_psum"), 1)
            pe.wait_ge(sem("q_kept"), a + 1)
            pe.wait_ge(sem("v_kept"), a + 1)

        def keep_qk(act, a, bq, bk):
            act.wait_ge(sem("k_psum"), a + 1)
            nc.scalar.activation(KT[:, 0, 0:GC], bank(1, GC), ACT.Identity, bias=bk).then_inc(sem("k_kept"), 1)
            nc.scalar.activation(QT[:, 0, :], bank(0), ACT.Identity, bias=bq).then_inc(sem("q_kept"), 1)

        def keep_v(dve, a, bv):
            dve.wait_ge(sem("v_psum"), a + 1)
            src = PS[0:CTX, 2, :].rearrange("p (g h d) -> p g h d", g=GROUP, h=HEADS)
            if bv is None:
                nc.vector.tensor_copy(V[0:CTX, :, :, 0:DH], src).then_inc(sem("v_kept"), 1)
            else:
                nc.vector.tensor_tensor(V[0:CTX, :, :, 0:DH], src,
                                        bc(bv[0:CTX].rearrange("p (h d) -> p h d", h=HEADS), 1, GROUP),
                                        ALU.add).then_inc(sem("v_kept"), 1)

        def spread_all(pool, a, K, ready, count):
            pool.wait_ge(sem(ready), count)
            for g in range(GROUP):
                spread_keys(pool, a, g, K)

        def plain_exp(act, a, scale, base):
            def exp(u):
                act.wait_ge(sem("shifted"), a * UNITS + u + 1)
                nc.scalar.activation(E[:, u % 3], E[:, u % 3], ACT.Exp, scale=scale).then_inc(sem("exps"), 1)
            return exp

        def exp_unit(act, a, u, K, scale):
            act.wait_ge(sem("shifted"), a * UNITS + u + 1)
            nc.scalar.activation(E[:, u % 3, 0:HALF * K], E[:, u % 3, 0:HALF * K], ACT.Exp,
                                 scale=scale).then_inc(sem("exps"), 1)

        def shift_unit(dve, link, a, u, K, m0):
            if u >= 3:
                dve.wait_ge(sem("probs_turned"), m0 + u - 2)
            shift(dve, link, a, u, K, E[:, u % 3, 0:HALF * K])

        SCALE = DH ** -0.5

        LEVELS = 7
        powers = big2[:, 0:2048].rearrange("p (l g k) -> p l g k", l=2, g=GROUP)
        attT = small[:, GT:2 * GT]
        kmat = KT[0:64, 0, :]
        qmat = QT[0:64, 0, :]

        def l0a_pe(pe):
            pe.wait_ge(once("con_loaded"), 16)
            for g in range(GROUP):
                turn_x(pe, 0, g, ON[:, g, 0:128])
            pe.wait_ge(once("w128_loaded"), 16 * (len(W128_CUTS) + 1))
            pe.wait_ge(sem("xT_ready"), GROUP)
            nc.tensor.matmul(PS[0:64, 0, :], w("l0a_wk"), XT[:, :], start=True, stop=True).then_inc(sem("l0a_kT"), 1)
            nc.tensor.matmul(PS[0:64, 1, :], w("l0a_wq"), XT[:, :], start=True, stop=True).then_inc(sem("l0a_qT"), 1)
            for g in range(GROUP):
                m = nc.tensor.matmul(PS[:, 2, g * 128:(g + 1) * 128], XT[:, g * 128:(g + 1) * 128], w("l0a_wv"),
                                     start=True, stop=True)
            m.then_inc(sem("l0a_v"), 1)
            pe.wait_ge(sem("l0a_k_kept"), 1)
            for g in range(GROUP):
                k = kmat[:, g * 128:(g + 1) * 128]
                m = nc.tensor.matmul(PS[:, 4, g * 128:(g + 1) * 128], k, k, start=True, stop=True)
            m.then_inc(sem("l0a_kk"), 1)
            pe.wait_ge(sem("l0a_q_kept"), 1)
            for g in range(GROUP):
                m = nc.tensor.matmul(PS[:, 5, g * 128:(g + 1) * 128], kmat[:, g * 128:(g + 1) * 128],
                                     qmat[:, g * 128:(g + 1) * 128], start=True, stop=True)
            m.then_inc(sem("l0a_kq"), 1)
            pe.wait_ge(sem("l0a_masked"), 3)
            pe.wait_ge(sem("l0a_u0"), 1)
            for l in range(LEVELS):
                for g in range(GROUP):
                    if l >= 1:
                        pe.wait_ge(sem("l0a_u"), (l - 1) * GROUP + g + 1)
                        pe.wait_ge(sem("l0a_powers"), (l - 1) * GROUP + g + 1)
                    p, pt = powers[:, l % 2, g, 0:128], powers[:, l % 2, g, 128:256]
                    nc.tensor.matmul(PS[:, 4 + g, 0:128], pt, VB[:, g, l % 2],
                                     start=True, stop=True).then_inc(sem("l0a_step"), 1)
                    if l < LEVELS - 1:
                        nc.tensor.matmul(PS[:, g, 0:128], pt, p, start=True, stop=True)
                        nc.tensor.matmul(PS[:, g, 128:256], p, pt, start=True, stop=True).then_inc(sem("l0a_level"), 1)
            for g in range(GROUP):
                pe.wait_ge(sem("l0a_u"), (LEVELS - 1) * GROUP + g + 1)
                nc.tensor.matmul(PS[:, g, 0:128], attT[:, g * 128:(g + 1) * 128],
                                 VB[:, g, LEVELS % 2], start=True, stop=True).then_inc(sem("l0a_y"), 1)
            norms_pe(pe, 1)

        def l0a_act(act, link):
            act.wait_ge(once("consts"), 3)
            act.wait_ge(once("w128_loaded"), 16 * (len(W128_CUTS) + 1))
            act.wait_ge(once("w64_loaded"), 48)
            for g in range(GROUP + 1):
                if g < GROUP:
                    norm_rstd(act, link, 0, g)
                if g >= 1:
                    act.wait_ge(sem("xT_turned"), g)
                    nc.scalar.activation(XT[:, (g - 1) * 128:g * 128], xt_ps, ACT.Identity, scale=w("l0a_gamma"),
                                         bias=w("l0a_beta")).then_inc(sem("xT_ready"), 1)
            act.wait_ge(sem("l0a_kT"), 1)
            nc.scalar.activation(kmat, PS[0:64, 0, :], ACT.Identity, bias=h64("l0a_bk")).then_inc(sem("l0a_k_kept"), 1)
            act.wait_ge(sem("l0a_qT"), 1)
            nc.scalar.activation(qmat, PS[0:64, 1, :], ACT.Identity, bias=h64("l0a_bq")).then_inc(sem("l0a_q_kept"), 1)
            for l in range(LEVELS - 1):
                for g in range(GROUP):
                    act.wait_ge(sem("l0a_level"), l * GROUP + g + 1)
                    nc.scalar.activation(powers[:, (l + 1) % 2, g], PS[:, g, 0:256],
                                         ACT.Copy).then_inc(sem("l0a_powers"), 1)
            norms_act(act, link, 1)

        def l0a_dve(dve, link, i):
            dve.wait_ge(once("x_loaded"), 16)
            dve.wait_ge(once("row_loaded"), 16)
            dve.wait_ge(once("con_loaded"), 16)
            dve.wait_ge(once("consts"), 3)
            link(nc.vector.tensor_copy(X[:].rearrange("p g d -> p (g d)"), x_all[:, bass.ds(i * GT, GT)]))
            for g in range(GROUP):
                link(nc.vector.bn_stats(stats[:, g], X[:, g]))
                nc.vector.bn_aggr(mv[:, g], stats[:, g]).then_inc(sem("norm_var"), 1)
            for g in range(GROUP):
                norm_apply(dve, 0, g, X[:, g], ON[:, g, 0:128])
            dve.wait_ge(sem("l0a_v"), 1)
            link(nc.vector.tensor_tensor(VB[:, :, 1], PS[:, 2].rearrange("p (g d) -> p g d", g=GROUP),
                                         bc(r("l0a_bv"), 1, GROUP), ALU.add))
            nc.vector.tensor_scalar(VB[:, :, 0], VB[:, :, 1], TTT_LR, None, ALU.mult).then_inc(sem("l0a_u0"), 1)
            dve.wait_ge(sem("l0a_kk"), 1)
            kk = PS[:, 4].rearrange("p (g d) -> p g d", g=GROUP)
            nc.vector.tensor_tensor(powers[:, 0, :, 0:128], kk, bc(c("low"), 1, GROUP),
                                    ALU.mult).then_inc(sem("l0a_masked"), 1)
            nc.vector.tensor_tensor(powers[:, 0, :, 128:256], kk, bc(c("up"), 1, GROUP),
                                    ALU.mult).then_inc(sem("l0a_masked"), 1)
            dve.wait_ge(sem("l0a_kq"), 1)
            nc.vector.tensor_tensor(attT.rearrange("p (g d) -> p g d", g=GROUP),
                                    PS[:, 5].rearrange("p (g d) -> p g d", g=GROUP), bc(c("sup"), 1, GROUP),
                                    ALU.mult).then_inc(sem("l0a_masked"), 1)
            dve.wait_ge(sem("l0a_u0"), 1)
            for l in range(LEVELS):
                for g in range(GROUP):
                    dve.wait_ge(sem("l0a_step"), l * GROUP + g + 1)
                    if l >= 1:
                        dve.wait_ge(sem("l0a_u"), (l - 1) * GROUP + g + 1)
                    nc.vector.tensor_tensor(VB[:, g, (l + 1) % 2], VB[:, g, l % 2], PS[:, 4 + g, 0:128],
                                            ALU.add).then_inc(sem("l0a_u"), 1)
            dve.wait_ge(sem("l0a_doubled"), 1)
            norms_dve(dve, link, 1, "l0a_y", lambda g: PS[:, g, 0:128], XR)

        def l0a_pool(pool, i):
            pool.wait_ge(once("ctx_loaded"), 32)
            nc.gpsimd.tensor_copy(CT[:, :], ctx_all[:, bass.ds(i * GC, GC)]).then_inc(sem("ctx_ready"), 1)
            nc.gpsimd.tensor_copy(small[0:1, 0:GC], mask_u8[:, bass.ds(i * GC, GC)]).then_inc(sem("ctx_ready"), 1)
            pool.wait_ge(sem("ctx_ready"), 2)
            nc.gpsimd.tensor_scalar(mask_b[:], bc(small[0:1, 0:GC].rearrange("p (g k) -> p g k", g=GROUP), 2, 4),
                                    MASKED, None, ALU.mult).then_inc(sem("ctx_ready"), 1)
            pool.wait_ge(sem("norm_var"), GROUP)
            nc.gpsimd.tensor_scalar(XR[:], X[:], 2.0, None, ALU.mult).then_inc(sem("l0a_doubled"), 1)

        def l0x_pe(pe):
            pe.wait_ge(sem("ctx_ready"), 3)
            pe.wait_ge(once("casts"), 3)
            project_ctx(pe, 0, 1, w("l0x_wq"), w("l0x_wk"), w("l0x_wv"))
            attend_pe(pe, 0, 0, 0, 2, CTX, w("l0x_wo"),
                      (ones_bf[:, :], lambda g: mask_b[:, g].rearrange("p h k -> p (h k)")))

        def l0x_act(act, link):
            keep_qk(act, 0, w("l0x_bq"), w("l0x_bk"))
            attend_act(act, link, 0, 0, 2, CTX, lambda u: exp_unit(act, 0, u, CTX, SCALE))

        def l0x_dve(dve, link):
            dve.wait_ge(once("consts"), 3)
            keep_v(dve, 0, r("l0x_bv"))
            dve.wait_ge(sem("residual"), 1)
            attend_dve(dve, link, 0, 0, 2, XR, lambda u: shift_unit(dve, link, 0, u, CTX, 0))

        def l0x_pool(pool):
            add_bias(pool, 1, r("l0x_bo"))
            spread_all(pool, 0, CTX, "k_kept", 1)

        def ranks(dve, link, logits, M, n, tie, rank, t1, t2):
            other, own = bc(logits, 2, n), bc(logits, 3, n)
            link(nc.vector.tensor_tensor(t1, other, own, ALU.is_gt))
            link(nc.vector.tensor_tensor(t2, other, own, ALU.is_equal))
            link(nc.vector.tensor_tensor(t2, t2, bc(tie.rearrange("p (e f) -> p e f", e=n), 1, M), ALU.mult))
            link(nc.vector.tensor_tensor(t1, t1, t2, ALU.add))
            link(nc.vector.tensor_reduce(rank, t1, AX.X, ALU.add))

        EXPERTS = 8
        g8 = lambda k: small[:, 32 * k:32 * k + 32].rearrange("p (g e) -> p g e", g=GROUP)
        logits, shifted8, probs, rank8, weight, tmp8 = (g8(k) for k in range(6))
        route_max = small[:, 192:192 + GROUP]
        route_sum = small[:, 200:200 + GROUP]
        pair1 = small[:, 256:512].rearrange("p (g e f) -> p g e f", g=GROUP, e=8)
        pair2 = small[:, 512:768].rearrange("p (g e f) -> p g e f", g=GROUP, e=8)
        weightT = small[0:8, 768:768 + GT]

        def route_pe(pe, tag, n, wg, b2):
            pe.wait_ge(sem("xT_ready"), (n + 1) * GROUP)
            for g in range(GROUP):
                m = nc.tensor.matmul(PS[:, 6, g * 8:(g + 1) * 8], XT[:, g * 128:(g + 1) * 128], wg,
                                     start=True, stop=True)
            m.then_inc(sem(tag + "_logits"), 1)

        def route_bias_pe(pe, tag, b2):
            pe.wait_ge(sem(tag + "_weights"), 1)
            for g in range(GROUP):
                m = nc.tensor.transpose(PS[0:8, 6, g * 128:(g + 1) * 128], weight[:, g], ident)
            m.then_inc(sem(tag + "_wT"), 1)
            pe.wait_ge(sem(tag + "_wT_kept"), 1)
            for g in range(GROUP):
                m = nc.tensor.matmul(PS[:, 7, g * 128:(g + 1) * 128], weightT[:, g * 128:(g + 1) * 128], b2,
                                     start=True, stop=True)
            m.then_inc(sem(tag + "_bias"), 1)

        def route_dve(dve, link, tag, bias, combine):
            dve.wait_ge(sem(tag + "_logits"), 1)
            link(nc.vector.tensor_tensor(logits, PS[:, 6, 0:32].rearrange("p (g e) -> p g e", g=GROUP),
                                         bc(bias, 1, GROUP), ALU.add))
            link(nc.vector.tensor_reduce(route_max, logits, AX.X, ALU.max))
            nc.vector.tensor_tensor(shifted8, logits, bc(route_max, 2, EXPERTS),
                                    ALU.subtract).then_inc(sem(tag + "_shifted"), 1)
            ranks(dve, link, logits, GROUP, EXPERTS, c("tie8"), rank8, pair1, pair2)
            dve.wait_ge(sem(tag + "_exp"), 1)
            link(nc.vector.tensor_reduce(route_sum, probs, AX.X, ALU.add))
            link(nc.vector.reciprocal(route_sum, route_sum))
            link(nc.vector.tensor_tensor(probs, probs, bc(route_sum, 2, EXPERTS), ALU.mult))
            combine(link).then_inc(sem(tag + "_weights"), 1)

        def route_act(act, tag):
            act.wait_ge(sem(tag + "_shifted"), 1)
            nc.scalar.activation(probs, shifted8, ACT.Exp).then_inc(sem(tag + "_exp"), 1)
            act.wait_ge(sem(tag + "_wT"), 1)
            nc.scalar.activation(weightT, PS[0:8, 6, :], ACT.Copy).then_inc(sem(tag + "_wT_kept"), 1)

        def start_sum(dve, link, tag):
            dve.wait_ge(sem(tag + "_bias"), 1)
            link(nc.vector.tensor_tensor(Y[:], X[:], PS[:, 7].rearrange("p (g d) -> p g d", g=GROUP), ALU.add))

        def add_expert(dve, tag, down, e):
            dve.wait_ge(sem(down), e + 1)
            if e >= 1:
                dve.wait_ge(sem(tag + "_added"), e)
            for g in range(GROUP):
                m = nc.vector.scalar_tensor_tensor(Y[:, g], PS[:, 4 + e % 2, g * 128:(g + 1) * 128],
                                                   weight[:, g, e:e + 1], Y[:, g], ALU.mult, ALU.add)
            m.then_inc(sem(tag + "_added"), 1)

        def norms_of_sum(dve, link, n, summed):
            dve.wait_ge(sem(summed[0]), summed[1])
            for g in range(GROUP):
                link(nc.vector.bn_stats(stats[:, g], Y[:, g]))
                nc.vector.bn_aggr(mv[:, g], stats[:, g]).then_inc(sem("norm_var"), 1)
            for g in range(GROUP):
                norm_apply(dve, n, g, Y[:, g], X[:, g])

        TILES = 4
        hidden = big2.rearrange("p (i t) -> p i t", i=8)

        def l0f_pe(pe):
            route_pe(pe, "l0f", 2, w("l0f_wg"), None)

            def up(e):
                for t in range(TILES):
                    i = e * TILES + t
                    if i >= 4:
                        pe.wait_ge(sem("l0f_gelu"), i - 3)
                    nc.tensor.matmul(bank(i % 4), w("l0f_w1", e * 512 + t * 128, 128), XT[:, :],
                                     start=True, stop=True).then_inc(sem("l0f_up"), 1)

            def down(e):
                pe.wait_ge(sem("l0f_gelu"), (e + 1) * TILES)
                if e >= 2:
                    pe.wait_ge(sem("l0f_added"), e - 1)
                for g in range(GROUP):
                    for t in range(TILES):
                        m = nc.tensor.matmul(PS[:, 4 + e % 2, g * 128:(g + 1) * 128],
                                             hidden[:, (e * TILES + t) % 8, g * 128:(g + 1) * 128],
                                             w("l0f_w2", e * 512 + t * 128, 128), start=t == 0, stop=t == TILES - 1)
                m.then_inc(sem("l0f_down"), 1)

            up(0)
            route_bias_pe(pe, "l0f", w8[:, 0:128])
            for e in range(EXPERTS):
                if e + 1 < EXPERTS:
                    up(e + 1)
                down(e)
            norms_pe(pe, 3)

        def l0f_act(act, link):
            route_act(act, "l0f")
            act.preload_act_table_set("gelu_and_others")
            for i in range(EXPERTS * TILES):
                act.wait_ge(sem("l0f_up"), i + 1)
                if i >= 8:
                    act.wait_ge(sem("l0f_down"), i // TILES - 1)
                nc.scalar.activation(hidden[:, i % 8], bank(i % 4), ACT.Gelu,
                                     bias=w("l0f_b1", i, 1)).then_inc(sem("l0f_gelu"), 1)
            act.preload_act_table_set("natural_log_exp_and_others")
            norms_act(act, link, 3)

        def l0f_dve(dve, link):
            route_dve(dve, link, "l0f", r("l0f_bg"), lambda link: nc.vector.scalar_tensor_tensor(
                weight, rank8, 2.0, probs, ALU.is_lt, ALU.mult))
            start_sum(dve, link, "l0f")
            for e in range(EXPERTS):
                add_expert(dve, "l0f", "l0f_down", e)
            norms_of_sum(dve, link, 3, ("l0f_added", EXPERTS))

        def l0f_pool(pool):
            pass

        GH, GK, GV = 4, 32, 64
        gate_abs = E[:, 0, 0:GT]
        gate_min = E[:, 1, 0:GT]
        gate = E[:, 2, 0:GT]
        run_sum = E2[:, 1, 0:GT]
        low_rank = E2[0:16, 0, 0:GT]
        exp_b, exp_nb = gate_abs, gate_min
        tail_b = PT[:, 0, 0:GROUP * CHUNK].rearrange("p (g t) -> p g t", g=GROUP)
        k_carry = small[:, 0:GT].rearrange("p (g c t) -> p g c t", g=GROUP, c=2)
        gla_v = VB[:, :, 0:2]
        gla_g = VB[:, :, 2:4]
        rms = small[:, 600:600 + 4 * GROUP].rearrange("p (g h) -> p g h", g=GROUP)

        def wide(b):
            return PS[:, b:b + 2, :].rearrange("p b (g d) -> p (b g) d", g=2)

        def l1a_pe(pe):
            pe.wait_ge(sem("xT_ready"), 4 * GROUP)
            nc.tensor.matmul(PS[0:16, 2, :], w("l1a_w1"), XT[:, :], start=True, stop=True).then_inc(sem("l1a_low"), 1)
            nc.tensor.matmul(bank(0), w("l1a_wq"), XT[:, :], start=True, stop=True)
            nc.tensor.matmul(bank(1), w("l1a_wk"), XT[:, :], start=True, stop=True).then_inc(sem("l1a_qk"), 1)
            pe.wait_ge(sem("l1a_low_kept"), 1)
            nc.tensor.matmul(bank(3), w16[:, :], low_rank, start=True, stop=True).then_inc(sem("l1a_z"), 1)
            for b, name, s in ((4, "l1a_wv", "l1a_v"), (6, "l1a_wg", "l1a_g")):
                for g in range(GROUP):
                    m = nc.tensor.matmul(wide(b)[:, g], XT[:, g * 128:(g + 1) * 128], w(name), start=True, stop=True)
                m.then_inc(sem(s), 1)
            pe.wait_ge(sem("l1a_v_kept"), 1)
            pe.wait_ge(sem("l1a_gated"), 1)
            pe.wait_ge(sem("l1a_keys"), 3)
            for i in range(GROUP + 3):
                if i < GROUP:
                    pe.wait_ge(sem("l1a_spread"), i + 1)
                    if i >= 2:
                        pe.wait_ge(sem("l1a_masked"), i - 1)
                    kb = KB[:, i % 2].rearrange("p h k -> p (h k)")
                    nc.tensor.matmul(PS[:, i % 2, 0:256], KT[:, 0, i * 128:(i + 1) * 128], kb[:, 0:256],
                                     start=True, stop=True)
                    nc.tensor.matmul(PS[:, i % 2, 256:512], k_carry[:, i], kb[:, 256:512],
                                     start=True, stop=True).then_inc(sem("l1a_scores"), 1)
                if i >= 3:
                    turn_x(pe, 4, i - 3, X[:, i - 3])
                if 1 <= i <= GROUP:
                    g = i - 1
                    pe.wait_ge(sem("l1a_masked"), g + 1)
                    if g >= 2:
                        pe.wait_ge(sem("attended"), O_L1A + g - 1)
                    at = E2[:, g % 2, 0:512].rearrange("p (h t) -> p h t", h=GH)
                    for h in range(GH):
                        m = nc.tensor.matmul(PS[:, 2 + g % 2, h * GV:(h + 1) * GV], at[:, h],
                                             VB[:, g, h // 2, (h % 2) * GV:(h % 2) * GV + GV], start=True, stop=True)
                    m.then_inc(sem("l1a_o"), 1)
                if 2 <= i <= GROUP + 1:
                    g = i - 2
                    pe.wait_ge(sem("attended"), O_L1A + g + 1)
                    for k in range(2):
                        m = nc.tensor.transpose(PS[:, 4 + g % 2, 128 * k:128 * k + 128],
                                                ON[:, g, 128 * k:128 * k + 128], ident)
                    m.then_inc(sem("out_turned"), 1)
                    pe.wait_ge(sem("out_kept"), O_L1A + g + 1)
                    if g >= 1:
                        pe.wait_ge(sem("x_ready"), 4 * GROUP + g)
                    for k in range(2):
                        m = nc.tensor.matmul(PS[:, 6, 0:128], ONT[:, g % 2, k], w("l1a_wo", 128 * k, 128),
                                             start=k == 0, stop=k == 1)
                    m.then_inc(sem("y_done"), 1)

        def l1a_act(act, link):
            act.wait_ge(sem("l1a_low"), 1)
            nc.scalar.activation(low_rank, PS[0:16, 2, :], ACT.Copy).then_inc(sem("l1a_low_kept"), 1)
            act.wait_ge(sem("l1a_z"), 1)
            nc.scalar.activation(gate_abs, bank(3), ACT.Abs, bias=w("l1a_b2")).then_inc(sem("l1a_abs"), 1)
            act.wait_ge(sem("l1a_abs"), 1)
            link(nc.scalar.activation(gate_abs, gate_abs, ACT.Exp, scale=-1.0))
            nc.scalar.activation(gate_abs, gate_abs, ACT.Ln, bias=one_col[:, 0:1]).then_inc(sem("l1a_softplus"), 1)
            act.wait_ge(sem("l1a_v"), 1)
            nc.scalar.activation(gla_v.rearrange("p g c d -> p g (c d)"), wide(4), ACT.Copy).then_inc(sem("l1a_v_kept"), 1)
            act.wait_ge(sem("l1a_g"), 1)
            nc.scalar.activation(gla_g.rearrange("p g c d -> p g (c d)"), wide(6), ACT.Exp,
                                 scale=-1.0).then_inc(sem("l1a_expg"), 1)
            act.wait_ge(sem("l1a_run"), 1)
            nc.scalar.activation(exp_b, run_sum, ACT.Exp, scale=1.0 / GATE_NORM).then_inc(sem("l1a_expb"), 1)
            nc.scalar.activation(exp_nb, run_sum, ACT.Exp, scale=-1.0 / GATE_NORM).then_inc(sem("l1a_expb"), 1)
            act.wait_ge(sem("l1a_tail"), 1)
            nc.scalar.activation(tail_b, tail_b, ACT.Exp, scale=1.0 / GATE_NORM).then_inc(sem("l1a_expb"), 1)
            for i in range(GROUP + 3):
                if i >= 3:
                    keep_xT(act, 4, i - 3)
                if 1 <= i <= GROUP:
                    g = i - 1
                    act.wait_ge(sem("l1a_o"), g + 1)
                    nc.scalar.activation(PT[:, g % 2, 0:256], PS[:, 2 + g % 2, 0:256],
                                         ACT.Square).then_inc(sem("l1a_square"), 1)
                    act.wait_ge(sem("l1a_ms"), g + 1)
                    link(nc.scalar.activation(rms[:, g], rms[:, g], ACT.Ln, bias=eps_col[:, 0:1], scale=1.0 / GV))
                    nc.scalar.activation(rms[:, g], rms[:, g], ACT.Exp, scale=-0.5).then_inc(sem("l1a_rms"), 1)
                if 2 <= i <= GROUP + 1:
                    g = i - 2
                    act.wait_ge(sem("out_turned"), O_L1A + g + 1)
                    nc.scalar.activation(ONT[:, g % 2].rearrange("p k t -> p (k t)"), PS[:, 4 + g % 2, 0:256],
                                         ACT.Copy).then_inc(sem("out_kept"), 1)
                    norm_rstd(act, link, 4, g)

        def l1a_dve(dve, link):
            dve.wait_ge(sem("l1a_abs"), 1)
            nc.vector.tensor_scalar(gate_min, bank(3), w("l1a_b2"), 0.0, ALU.add, ALU.min).then_inc(sem("l1a_min"), 1)
            dve.wait_ge(sem("l1a_softplus"), 1)
            dve.wait_ge(sem("l1a_min"), 1)
            link(nc.vector.tensor_tensor(gate, gate_min, gate_abs, ALU.subtract))
            nc.vector.tensor_tensor_scan(run_sum, c("scan"), gate, 0.0, ALU.mult, ALU.add).then_inc(sem("l1a_run"), 1)
            dve.wait_ge(sem("l1a_run"), 1)
            b0 = run_sum.rearrange("p (g c t) -> p g c t", g=GROUP, c=2)[:, :, 0]
            nc.vector.tensor_tensor(tail_b, b0[:, :, CHUNK - 1:CHUNK].to_broadcast([128, GROUP, CHUNK]), b0,
                                    ALU.subtract).then_inc(sem("l1a_tail"), 1)
            dve.wait_ge(sem("l1a_expg"), 1)
            gg = gla_g.rearrange("p g c d -> p g (c d)")
            link(nc.vector.tensor_scalar(gg, gg, 1.0, None, ALU.add))
            link(nc.vector.reciprocal(gg, gg))
            link(nc.vector.tensor_tensor(gg, gg, wide(6), ALU.mult))
            g4 = gg.rearrange("p g (h d) -> p g h d", h=GH)
            for g in range(GROUP):
                m = nc.vector.tensor_tensor(g4[:, g], g4[:, g], bc(r("l1a_gn"), 1, GH), ALU.mult)
            m.then_inc(sem("l1a_gated"), 1)
            dve.wait_ge(sem("l1a_qk"), 1)
            dve.wait_ge(sem("l1a_expb"), 3)
            nc.vector.scalar_tensor_tensor(QT[:, 0], bank(0), GK ** -0.5, exp_b,
                                           ALU.mult, ALU.mult).then_inc(sem("l1a_keys"), 1)
            nc.vector.tensor_tensor(KT[:, 0], bank(1), exp_nb, ALU.mult).then_inc(sem("l1a_keys"), 1)
            kk = bank(1).rearrange("p (g c t) -> p g c t", g=GROUP, c=2)
            link(nc.vector.tensor_tensor(k_carry[:, :, 0], kk[:, :, 0], tail_b, ALU.mult))
            dve.wait_ge(sem("l1a_keys"), 2)
            nc.vector.tensor_copy(k_carry[:, :, 1], KT[:, 0].rearrange("p (g c t) -> p g c t", g=GROUP, c=2)[:, :, 1]
                                  ).then_inc(sem("l1a_keys"), 1)
            dve.wait_ge(sem("l1a_gated"), 1)
            for i in range(GROUP + 3):
                if i < GROUP:
                    dve.wait_ge(sem("l1a_scores"), i + 1)
                    if i >= 2:
                        dve.wait_ge(sem("l1a_o"), i - 1)
                    mask = bc(c("incl").rearrange("p (c t) -> p c t", c=2), 2, GH)
                    nc.vector.tensor_tensor(E2[:, i % 2, 0:512].rearrange("p (h c t) -> p c h t", c=2, h=GH),
                                            bank(i % 2).rearrange("p (c h t) -> p c h t", c=2, h=GH), mask,
                                            ALU.mult).then_inc(sem("l1a_masked"), 1)
                if i >= 3:
                    norm_apply(dve, 4, i - 3, Y[:, i - 3], X[:, i - 3])
                if 1 <= i <= GROUP:
                    g = i - 1
                    dve.wait_ge(sem("l1a_square"), g + 1)
                    nc.vector.tensor_reduce(rms[:, g], PT[:, g % 2, 0:256].rearrange("p (h d) -> p h d", h=GH),
                                            AX.X, ALU.add).then_inc(sem("l1a_ms"), 1)
                    dve.wait_ge(sem("l1a_rms"), g + 1)
                    o4 = ON[:, g].rearrange("p (h d) -> p h d", h=GH)
                    link(nc.vector.tensor_tensor(o4, PS[:, 2 + g % 2, 0:256].rearrange("p (h d) -> p h d", h=GH),
                                                 bc(rms[:, g], 2, GV), ALU.mult))
                    nc.vector.tensor_tensor(ON[:, g], ON[:, g], gg[:, g], ALU.mult).then_inc(sem("attended"), 1)
                if 2 <= i <= GROUP + 1:
                    g = i - 2
                    dve.wait_ge(sem("y_done"), O_L1A + g + 1)
                    norm_stats(dve, link, 4, g, PS[:, 6, 0:128], X)

        def l1a_pool(pool):
            pool.wait_ge(sem("l1a_keys"), 3)
            for g in range(GROUP):
                if g >= 2:
                    pool.wait_ge(sem("l1a_scores"), g - 1)
                q = QT[:, 0, g * 128:(g + 1) * 128].rearrange("p (c t) -> p c t", c=2)
                for ch in range(2):
                    m = nc.gpsimd.tensor_tensor(
                        KB[:, g % 2].rearrange("p h k -> p (h k)")[:, 256 * ch:256 * ch + 256].rearrange(
                            "p (h t) -> p h t", h=GH),
                        bc(q[:, ch], 1, GH), bc(c("hm4"), 2, CHUNK), ALU.mult)
                m.then_inc(sem("l1a_spread"), 1)

        O_L1A = GROUP

        NH = GROUP * HEADS
        LOG_T_MIN, LOG_T_MAX = float(np.log(0.1)), float(np.log(10.0))
        flat_mx = mx[:].rearrange("p u h -> p (u h)")
        sum1, sum2, feat_max, feat_var, feat_mean, half_t = (small[:, NH * k:NH * k + NH] for k in range(6))
        q_sum = small[:, 400:400 + GROUP]
        k_sum = small[:, 408:408 + GROUP]
        mlp1, mlp2 = small[0:64, 420:420 + NH], small[0:64, 484:484 + NH]

        def l1x_pe(pe):
            project_ctx(pe, 1, 4, w("l1x_wq"), w("l1x_wk"), w("l1x_wv"))
            for u in range(UNITS):
                scores(pe, 1, u, CTX)
            pe.wait_ge(sem("l1x_feats"), 3)
            pe.wait_ge(once("casts"), 5)
            feats = (feat_mean, feat_max, feat_var)
            for j in range(3):
                m = nc.tensor.matmul(PS[0:64, 3, 0:NH], r("l1x_w1", 64 * j, 64), feats[j], start=j == 0, stop=j == 2)
            m.then_inc(sem("l1x_mlp"), 1)
            pe.wait_ge(sem("l1x_gelu"), 1)
            nc.tensor.matmul(PS[0:64, 2, 0:NH], h64("l1x_w2"), mlp1, start=True, stop=True).then_inc(sem("l1x_mlp"), 1)
            pe.wait_ge(sem("l1x_gelu"), 2)
            nc.tensor.matmul(PS[:, 3, 0:NH], w3_rep[:, :], mlp2, start=True, stop=True).then_inc(sem("l1x_mlp"), 1)
            attend_pe(pe, 1, UNITS, 2 * GROUP, 5, CTX, w("l1x_wo"), scored=True, probs0=UNITS)

        def l1x_act(act, link):
            keep_qk(act, 1, w("l1x_bq"), w("l1x_bk"))
            for u in range(UNITS):
                act.wait_ge(sem("shifted"), UNITS + u + 1)
                if u >= 3:
                    act.wait_ge(sem("l1x_sums"), u - 2)
                nc.scalar.activation(E[:, u % 3, 0:HALF * CTX], big[:, u], ACT.Exp,
                                     scale=SCALE).then_inc(sem("l1x_exp"), 1)
            act.preload_act_table_set("gelu_and_others")
            act.wait_ge(sem("l1x_mlp"), 1)
            nc.scalar.activation(mlp1, PS[0:64, 3, 0:NH], ACT.Gelu, bias=h64("l1x_b1")).then_inc(sem("l1x_gelu"), 1)
            act.wait_ge(sem("l1x_mlp"), 2)
            nc.scalar.activation(mlp2, PS[0:64, 2, 0:NH], ACT.Gelu, bias=h64("l1x_b2")).then_inc(sem("l1x_gelu"), 1)
            act.preload_act_table_set("natural_log_exp_and_others")
            act.wait_ge(sem("l1x_logt"), 1)
            nc.scalar.activation(half_t, half_t, ACT.Exp, scale=-1.0).then_inc(sem("l1x_t"), 1)

            def exp(u):
                act.wait_ge(sem("l1x_scaled"), u + 1)
                nc.scalar.activation(E[:, u % 3, 0:HALF * CTX], E[:, u % 3, 0:HALF * CTX], ACT.Exp,
                                     scale=0.5).then_inc(sem("exps"), 1)

            attend_act(act, link, UNITS, 2 * GROUP, 5, CTX, exp)

        def l1x_dve(dve, link):
            keep_v(dve, 1, r("l1x_bv"))

            def sums(u):
                dve.wait_ge(sem("l1x_exp"), u + 1)
                nc.vector.tensor_reduce(sum1[:, u * HALF:(u + 1) * HALF], E[:, u % 3, 0:HALF * CTX].rearrange(
                    "p (h k) -> p h k", h=HALF), AX.X, ALU.add)
                dve.wait_ge(sem("l1x_square"), u + 1)
                nc.vector.tensor_reduce(sum2[:, u * HALF:(u + 1) * HALF], E2[:, u % 2, 0:HALF * CTX].rearrange(
                    "p (h k) -> p h k", h=HALF), AX.X, ALU.add).then_inc(sem("l1x_sums"), 1)

            for u in range(UNITS + 2):
                if u < UNITS:
                    shift(dve, link, 1, u, CTX, big[:, u])
                if u >= 2:
                    sums(u - 2)
            nc.vector.tensor_scalar(feat_max, flat_mx, SCALE / TOK, None, ALU.mult).then_inc(sem("l1x_feats"), 1)
            dve.wait_ge(sem("l1x_sums"), UNITS)
            link(nc.vector.reciprocal(sum1, sum1))
            link(nc.vector.tensor_tensor(sum2, sum2, sum1, ALU.mult))
            link(nc.vector.tensor_tensor(sum2, sum2, sum1, ALU.mult))
            nc.vector.tensor_scalar(feat_var, sum2, -1.0 / CTX, 1.0 / ((CTX - 1) * TOK), ALU.add,
                                    ALU.mult).then_inc(sem("l1x_feats"), 1)
            dve.wait_ge(sem("q_kept"), 2)
            link(nc.vector.tensor_reduce(q_sum, QT[:, 0].rearrange("p (g t) -> p g t", g=GROUP), AX.X, ALU.add))
            link(nc.vector.tensor_reduce(k_sum, KT[:, 0, 0:GC].rearrange("p (g k) -> p g k", g=GROUP), AX.X, ALU.add))
            link(nc.vector.scalar_tensor_tensor(q_sum, q_sum, SCALE / (TOK * CTX), k_sum, ALU.mult, ALU.mult))
            nc.vector.tensor_tensor(feat_mean.rearrange("p (g h) -> p g h", g=GROUP), bc(q_sum, 2, HEADS),
                                    bc(c("hm16"), 1, GROUP), ALU.mult).then_inc(sem("l1x_feats"), 1)
            dve.wait_ge(sem("l1x_mlp"), 3)
            link(nc.vector.tensor_scalar(half_t, PS[:, 3, 0:NH], r("l1x_b3"), LOG_T_MIN, ALU.add, ALU.max))
            nc.vector.tensor_scalar(half_t, half_t, LOG_T_MAX, None, ALU.min).then_inc(sem("l1x_logt"), 1)
            dve.wait_ge(sem("l1x_t"), 1)
            dve.wait_ge(sem("residual"), 2)

            def scaled(u):
                if u >= 3:
                    dve.wait_ge(sem("probs_turned"), UNITS + u - 2)
                nc.vector.tensor_tensor(E[:, u % 3, 0:HALF * CTX].rearrange("p (h k) -> p h k", h=HALF),
                                        big[:, u].rearrange("p (h k) -> p h k", h=HALF),
                                        bc(half_t[:, u * HALF:(u + 1) * HALF], 2, CTX),
                                        ALU.mult).then_inc(sem("l1x_scaled"), 1)

            attend_dve(dve, link, UNITS, 2 * GROUP, 5, XR, scaled)

        def l1x_pool(pool):
            add_bias(pool, 4, r("l1x_bo"))
            pool.wait_ge(sem("k_kept"), 2)
            for u in range(UNITS + 2):
                if u % 2 == 0 and u < UNITS:
                    spread_keys(pool, 1, u // 2, CTX)
                if u >= 2:
                    v = u - 2
                    pool.wait_ge(sem("l1x_exp"), v + 1)
                    if v >= 2:
                        pool.wait_ge(sem("l1x_sums"), v - 1)
                    nc.gpsimd.tensor_tensor(E2[:, v % 2, 0:HALF * CTX], E[:, v % 3, 0:HALF * CTX],
                                            E[:, v % 3, 0:HALF * CTX], ALU.mult).then_inc(sem("l1x_square"), 1)

        first_h = [big2[:, 512 * k:512 * k + 512] for k in range(2)]
        second_h = [big2[:, 1024 + 512 * k:1536 + 512 * k] for k in range(2)]

        def l1f_pe(pe):
            route_pe(pe, "l1f", 5, w("l1f_wg"), None)
            for i in range(EXPERTS + 2):
                if i < EXPERTS:
                    if i >= 2:
                        pe.wait_ge(sem("l1f_relu1"), i - 1)
                    nc.tensor.matmul(bank(i % 2), w("l1f_w1", 128 * i, 128), XT[:, :],
                                     start=True, stop=True).then_inc(sem("l1f_up1"), 1)
                if 1 <= i <= EXPERTS:
                    j = i - 1
                    pe.wait_ge(sem("l1f_relu1"), j + 1)
                    if j >= 2:
                        pe.wait_ge(sem("l1f_relu2"), j - 1)
                    nc.tensor.matmul(bank(2 + j % 2), w("l1f_w2", 128 * j, 128), first_h[j % 2],
                                     start=True, stop=True).then_inc(sem("l1f_up2"), 1)
                if i >= 2:
                    j = i - 2
                    pe.wait_ge(sem("l1f_relu2"), j + 1)
                    if j >= 2:
                        pe.wait_ge(sem("l1f_added"), j - 1)
                    for g in range(GROUP):
                        m = nc.tensor.matmul(PS[:, 4 + j % 2, g * 128:(g + 1) * 128],
                                             second_h[j % 2][:, g * 128:(g + 1) * 128], w("l1f_w3", 128 * j, 128),
                                             start=True, stop=True)
                    m.then_inc(sem("l1f_down"), 1)
                if i == 1:
                    route_bias_pe(pe, "l1f", w8[:, 128:256])
            norms_pe(pe, 6)

        def l1f_act(act, link):
            for i in range(EXPERTS):
                act.wait_ge(sem("l1f_up1"), i + 1)
                if i >= 2:
                    act.wait_ge(sem("l1f_up2"), i - 1)
                nc.scalar.activation(first_h[i % 2], bank(i % 2), ACT.Relu,
                                     bias=w("l1f_b1", i, 1)).then_inc(sem("l1f_relu1"), 1)
                if i == 0:
                    route_act(act, "l1f")
                if i >= 1:
                    relu2(act, i - 1)
            relu2(act, EXPERTS - 1)
            norms_act(act, link, 6)

        def relu2(act, j):
            act.wait_ge(sem("l1f_up2"), j + 1)
            if j >= 2:
                act.wait_ge(sem("l1f_down"), j - 1)
            nc.scalar.activation(second_h[j % 2], bank(2 + j % 2), ACT.Relu,
                                 bias=w("l1f_b2", j, 1)).then_inc(sem("l1f_relu2"), 1)

        def l1f_dve(dve, link):
            def combine(link):
                link(nc.vector.scalar_tensor_tensor(tmp8, rank8, 0.0, probs[:, :, 0:1].to_broadcast([128, GROUP, 8]),
                                                    ALU.is_equal, ALU.mult))
                link(nc.vector.scalar_tensor_tensor(weight, rank8, 1.0, probs[:, :, 1:2].to_broadcast([128, GROUP, 8]),
                                                    ALU.is_equal, ALU.mult))
                return nc.vector.tensor_tensor(weight, weight, tmp8, ALU.add)

            route_dve(dve, link, "l1f", r("l1f_bg"), combine)
            start_sum(dve, link, "l1f")
            for e in range(EXPERTS):
                add_expert(dve, "l1f", "l1f_down", e)
            norms_of_sum(dve, link, 6, ("l1f_added", EXPERTS))

        def l1f_pool(pool):
            pass

        rot = [E[:, 0, 0:GT], E[:, 1, 0:GT], E[:, 2, 0:GT], E2[:, 0, 0:GT]]

        def l2a_pe(pe):
            pe.wait_ge(sem("xT_ready"), 7 * GROUP)
            for b, name in enumerate(("l2a_wk", "l2a_wks", "l2a_wq", "l2a_wqs")):
                nc.tensor.matmul(bank(b), w(name), XT[:, :], start=True, stop=True).then_inc(sem("l2a_qk"), 1)
            for g in range(GROUP):
                m = nc.tensor.matmul(PS[:, 4, g * 128:(g + 1) * 128], XT[:, g * 128:(g + 1) * 128], w("l2a_wv"),
                                     start=True, stop=True)
            m.then_inc(sem("l2a_v"), 1)
            pe.wait_ge(sem("l2a_rotated"), 4)
            pe.wait_ge(sem("l2a_q"), 1)
            pe.wait_ge(sem("l2a_v_kept"), 1)
            causal = causal_bf[:].rearrange("p h k -> p (h k)")
            attend_pe(pe, 2, 2 * UNITS, 3 * GROUP, 7, TOK, w("l2a_wo"), (ident_bf[:, :], lambda g: causal),
                      probs0=2 * UNITS)

        def l2a_act(act, link):
            act.wait_ge(sem("l2a_v"), 1)
            nc.scalar.activation(V[:, :, :, 0:DH].rearrange("p g h d -> p (g h) d"),
                                 PS[:, 4, :].rearrange("p (n d) -> p n d", d=DH), ACT.Copy).then_inc(sem("l2a_v_kept"), 1)
            attend_act(act, link, 2 * UNITS, 3 * GROUP, 7, TOK, lambda u: exp_unit(act, 2, u, TOK, SCALE))

        def l2a_dve(dve, link):
            for b in range(4):
                dve.wait_ge(sem("l2a_qk"), b + 1)
                nc.vector.tensor_tensor(rot[b].rearrange("p (g t) -> p g t", g=GROUP),
                                        bank(b).rearrange("p (g t) -> p g t", g=GROUP),
                                        bc(c("sin" if b % 2 else "cos"), 1, GROUP),
                                        ALU.mult).then_inc(sem("l2a_rotated"), 1)
            dve.wait_ge(sem("l2a_q"), 1)
            dve.wait_ge(sem("residual"), 3)
            attend_dve(dve, link, 2 * UNITS, 3 * GROUP, 7, XR, lambda u: shift_unit(dve, link, 2, u, TOK, 2 * UNITS))

        def l2a_pool(pool):
            pool.wait_ge(sem("l2a_rotated"), 2)
            nc.gpsimd.tensor_tensor(KT[:, 0], rot[0], rot[1], ALU.add).then_inc(sem("l2a_k"), 1)
            pool.wait_ge(sem("l2a_k"), 1)
            spread_keys(pool, 2, 0, TOK)
            pool.wait_ge(sem("l2a_rotated"), 4)
            nc.gpsimd.tensor_tensor(QT[:, 0], rot[2], rot[3], ALU.add).then_inc(sem("l2a_q"), 1)
            spread_keys(pool, 2, 1, TOK)
            add_bias(pool, 6, r("l2a_bo"))
            for g in range(2, GROUP):
                spread_keys(pool, 2, g, TOK)

        gate_hm = small[0:16, 0:NH].rearrange("p (g h) -> p g h", g=GROUP)
        gate_mean, gate_top = small[0:16, 64:64 + GROUP], small[0:16, 72:72 + GROUP]
        gates = small[:, 128:128 + NH]
        scale1 = small[:, 192:192 + NH]
        mx2 = small[:, 256:256 + NH]
        mixed = small[:, 512:1024].rearrange("p (g d) -> p g d", g=GROUP)
        U2 = 3 * UNITS

        def l2x_pe(pe):
            pe.wait_ge(sem("xT_ready"), 8 * GROUP)
            nc.tensor.matmul(PS[0:16, 3, 0:GC], w("l2x_wla"), CT[:, :], start=True, stop=True).then_inc(sem("l2x_la"), 1)
            project_ctx(pe, 2, 7, w("l2x_wq"), w("l2x_wk"), w("l2x_wv"))
            pe.wait_ge(sem("l2x_gate"), 1)
            nc.tensor.matmul(PS[:, 6, 0:NH], c("ones")[0:16], gate_hm.rearrange("p g h -> p (g h)"),
                             start=True, stop=True).then_inc(sem("l2x_gates"), 1)
            pe.wait_ge(sem("l2x_gates_kept"), 1)
            for i in range(STEPS):
                if i < UNITS:
                    scores(pe, 3, i, CTX)
                if 2 <= i < UNITS + 2:
                    u = i - 2
                    if u % 2 == 0 and u > 0:
                        pe.wait_ge(sem("attended"), 4 * GROUP + u // 2)
                    for k in range(2):
                        m = U2 + 2 * u + k
                        pe.wait_ge(sem("exps" if k == 0 else "l2x_exps2"), U2 + u + 1 if k == 0 else u + 1)
                        turn_probs(pe, m, CTX, E[:, u % 3] if k == 0 else E2[:, u % 2])
                        values(pe, m, u, CTX, k)
                if i >= 7 and i % 2:
                    turn_x(pe, 8, (i - 7) // 2, X[:, (i - 7) // 2])
                if i >= 5 and i % 2 and (i - 5) // 2 < GROUP:
                    g = (i - 5) // 2
                    turn_out(pe, 4 * GROUP + g, g, 8)
                    project_out(pe, 4 * GROUP + g, g, w("l2x_wo"))

        def l2x_act(act, link):
            act.wait_ge(sem("k_psum"), 3)
            nc.scalar.activation(KT[:, 0, 0:GC], bank(1, GC), ACT.Copy).then_inc(sem("k_kept"), 1)
            nc.scalar.activation(QT[:, 0, :], bank(0), ACT.Copy).then_inc(sem("q_kept"), 1)
            for i in range(STEPS):
                if 2 <= i < UNITS + 2:
                    for k in range(2):
                        keep_probs(act, U2 + 2 * (i - 2) + k, CTX)
                if i < UNITS:
                    act.wait_ge(sem("shifted"), 3 * UNITS + i + 1)
                    nc.scalar.activation(E[:, i % 3, 0:HALF * CTX], E[:, i % 3, 0:HALF * CTX], ACT.Exp,
                                         scale=SCALE).then_inc(sem("exps"), 1)
                if 1 <= i < UNITS + 1:
                    u = i - 1
                    act.wait_ge(sem("l2x_shifted2"), u + 1)
                    nc.scalar.activation(E2[:, u % 2, 0:HALF * CTX], E2[:, u % 2, 0:HALF * CTX],
                                         ACT.Exp).then_inc(sem("l2x_exps2"), 1)
                if i >= 7 and i % 2:
                    keep_xT(act, 8, (i - 7) // 2)
                if i >= 5 and i % 2 and (i - 5) // 2 < GROUP:
                    keep_out(act, 4 * GROUP + (i - 5) // 2, (i - 5) // 2)
                if i >= 6 and i % 2 == 0:
                    norm_rstd(act, link, 8, (i - 6) // 2)

        def l2x_dve(dve, link):
            keep_v(dve, 2, None)
            dve.wait_ge(sem("l2x_la"), 1)
            la = PS[0:16, 3, 0:GC].rearrange("p (g k) -> p g k", g=GROUP)
            link(nc.vector.tensor_reduce(gate_mean, la, AX.X, ALU.add))
            link(nc.vector.tensor_reduce(gate_top, la, AX.X, ALU.max))
            link(nc.vector.tensor_scalar(gate_mean, gate_mean, 0.5 / CTX, None, ALU.mult))
            link(nc.vector.scalar_tensor_tensor(gate_mean, gate_top, 0.5, gate_mean, ALU.mult, ALU.add))
            nc.vector.tensor_tensor(gate_hm, bc(gate_mean, 2, HEADS), bc(ident[0:16, 0:16], 1, GROUP),
                                    ALU.mult).then_inc(sem("l2x_gate"), 1)
            dve.wait_ge(sem("l2x_gates"), 1)
            nc.vector.tensor_copy(gates, PS[:, 6, 0:NH]).then_inc(sem("l2x_gates_kept"), 1)
            dve.wait_ge(sem("l2x_gates_kept"), 1)
            dve.wait_ge(sem("residual"), 4)

            def second(u):
                e1 = E[:, u % 3, 0:HALF * CTX].rearrange("p (h k) -> p h k", h=HALF)
                e2 = E2[:, u % 2, 0:HALF * CTX].rearrange("p (h k) -> p h k", h=HALF)
                s1, m2 = scale1[:, u * HALF:(u + 1) * HALF], mx2[:, u * HALF:(u + 1) * HALF]
                dve.wait_ge(sem("exps"), U2 + u + 1)
                link(nc.vector.tensor_reduce(s1, e1, AX.X, ALU.add))
                link(nc.vector.reciprocal(s1, s1))
                link(nc.vector.tensor_tensor(s1, s1, gates[:, u * HALF:(u + 1) * HALF], ALU.mult))
                if u >= 2:
                    dve.wait_ge(sem("probs_turned"), U2 + 2 * (u - 2) + 2)
                link(nc.vector.tensor_tensor(e2, e1, bc(s1, 2, CTX), ALU.mult))
                link(nc.vector.tensor_reduce(m2, e2, AX.X, ALU.max))
                nc.vector.tensor_tensor(e2, e2, bc(m2, 2, CTX), ALU.subtract).then_inc(sem("l2x_shifted2"), 1)

            for i in range(STEPS):
                if i >= 4 and i % 2 == 0 and (i - 4) // 2 < GROUP:
                    g = (i - 4) // 2
                    dve.wait_ge(sem("values_done"), U2 + 4 * g + 4)
                    for k, share in ((0, att_mix[:, 0:1]), (1, r("l2x_w"))):
                        o, rc = o_view(k), rec[:, g, k]
                        link(nc.vector.reciprocal(rc, o[:, :, DH]))
                        link(nc.vector.tensor_scalar(rc, rc, share, None, ALU.mult))
                        dst = (mixed if k == 0 else ON)[:, g, 0:128].rearrange("p (h d) -> p h d", h=HEADS)
                        link(nc.vector.tensor_tensor(dst, o[:, :, 0:DH], bc(rc, 2, DH), ALU.mult))
                    nc.vector.tensor_tensor(ON[:, g, 0:128], ON[:, g, 0:128], mixed[:, g],
                                            ALU.add).then_inc(sem("attended"), 1)
                if i < UNITS:
                    if i >= 3:
                        dve.wait_ge(sem("probs_turned"), U2 + 2 * (i - 3) + 1)
                    shift(dve, link, 3, i, CTX, E[:, i % 3, 0:HALF * CTX])
                if 1 <= i < UNITS + 1:
                    second(i - 1)
                if i >= 6 and i % 2 == 0:
                    g = (i - 6) // 2
                    dve.wait_ge(sem("y_done"), 4 * GROUP + g + 1)
                    norm_stats(dve, link, 8, g, y_ps, XR)
                if i >= 7 and i % 2:
                    norm_apply(dve, 8, (i - 7) // 2, Y[:, (i - 7) // 2], X[:, (i - 7) // 2])

        def l2x_pool(pool):
            add_bias(pool, 7, r("l2x_bo"))
            spread_all(pool, 3, CTX, "k_kept", 3)

        NE, WH, WD = 5, 8, 64
        wide_q = big2[:, 0:2048].rearrange("p (j t) -> p j t", j=4)
        wide_k = big2[:, 2048:4096].rearrange("p (j t) -> p j t", j=4)
        flatE = E[:].rearrange("p n k -> p (n k)")
        xv = flatE[:, 1024:1024 + GROUP * 320].rearrange("p (g e d) -> p g e d", g=GROUP, e=NE)
        gl = small[:, 0:320].rearrange("p (m e) -> p m e", e=NE)
        glrank = small[:, 320:640].rearrange("p (m e) -> p m e", e=NE)
        glsig = small[:, 640:800].rearrange("p (g h e) -> p g h e", g=GROUP, e=NE)
        v_pick = small[:, 800:960].rearrange("p (g h e) -> p g h e", g=GROUP, e=NE)
        o_pick = small[:, 960:1120].rearrange("p (g h e) -> p g h e", g=GROUP, e=NE)
        head_sum = small[:, 1120:1120 + 32].rearrange("p (g h) -> p g h", g=GROUP)
        gl_pairs = [b[:].rearrange("p n k -> p (n k)")[:, 0:1600].rearrange("p (m e f) -> p m e f", e=NE, f=NE)
                    for b in (PT, E2)]
        v_parts = [b[:].rearrange("p n k -> p (n k)").rearrange("p (e h d) -> p e h d", e=4, h=WH) for b in (E2, PT)]
        wide_v = VB[:].rearrange("p g c d -> p g (c d)").rearrange("p g (h d) -> p g h d", h=WH)
        o_kept = [KB[:, k].rearrange("p h k -> p (h k)")[:, 0:512].rearrange("p (h d) -> p h d", h=WH) for k in range(2)]
        o_part4 = [KB[:, k].rearrange("p h k -> p (h k)")[:, 512:1024].rearrange("p (h d) -> p h d", h=WH)
                   for k in range(2)]
        o_parts = E2[:].rearrange("p n k -> p (n k)").rearrange("p (e h d) -> p e h d", e=4, h=WH)
        per_expert = [small[:, 1200 + 320 * k:1520 + 320 * k] for k in range(2)]
        per_expertT = [ON[:].rearrange("p g d -> p (g d)")[:, 384 * k:384 * k + 384] for k in range(2)]
        M0 = U2 + 2 * UNITS
        S0 = 4 * UNITS
        O0 = 5 * GROUP

        def slot(h):
            return 4 * (h % 2) + h // 2

        def l2f_pe(pe):
            pe.wait_ge(sem("xT_ready"), 9 * GROUP)
            for b in range(8):
                nc.tensor.matmul(bank(b), w("l2f_wq" if b < 4 else "l2f_wk", 128 * (b % 4), 128), XT[:, :],
                                 start=True, stop=True).then_inc(sem("l2f_q" if b < 4 else "l2f_k"), 1)
            pe.wait_ge(sem("l2f_q_kept"), 4)
            for g in range(GROUP):
                m = nc.tensor.matmul(PS[:, 0, 80 * g:80 * g + 80], XT[:, g * 128:(g + 1) * 128], w("l2f_wg"),
                                     start=True, stop=True)
            m.then_inc(sem("l2f_gl"), 1)
            pe.wait_ge(sem("l2f_k_kept"), 4)
            for g in range(GROUP):
                nc.tensor.matmul(PS[:, 2 + g, 0:320], XT[:, g * 128:(g + 1) * 128], w("l2f_wv"),
                                 start=True, stop=True).then_inc(sem("l2f_xv"), 1)
            pe.wait_ge(sem("l2f_gl_kept"), 1)
            pe.wait_ge(sem("l2f_xv_kept"), GROUP)
            pe.wait_ge(sem("l2f_v"), GROUP)
            for i in range(GROUP + 3):
                if i < GROUP:
                    if i >= 1:
                        pe.wait_ge(sem("shifted"), S0 + i)
                    for h in range(WH):
                        p, t = 64 * (h % 2), slice(i * 128, (i + 1) * 128)
                        m = nc.tensor.matmul(PS[:, h % 2, (h // 2) * 128:(h // 2) * 128 + 128],
                                             wide_q[p:p + 64, h // 2, t], wide_k[p:p + 64, h // 2, t],
                                             start=True, stop=True)
                    m.then_inc(sem("scores"), 1)
                if i >= 3:
                    turn_x(pe, 9, i - 3, X[:, i - 3])
                if 1 <= i <= GROUP:
                    g = i - 1
                    pe.wait_ge(sem("exps"), S0 + g + 1)
                    turn_probs(pe, M0 + g, TOK, E[:, g % 2])
                    pe.wait_ge(sem("probs_kept"), M0 + g + 1)
                    if g >= 2:
                        pe.wait_ge(sem("l2f_o_kept"), g - 1)
                    for h in range(WH):
                        m = nc.tensor.matmul(PS[:, 2 + g % 2, h * WD:(h + 1) * WD],
                                             PT[:, (M0 + g) % 2, slot(h) * 128:slot(h) * 128 + 128], wide_v[:, g, h],
                                             start=True, stop=True)
                    m.then_inc(sem("values_done"), 1)
                if 2 <= i <= GROUP + 1:
                    g = i - 2
                    pe.wait_ge(sem("attended"), O0 + g + 1)
                    for k, n in ((0, 128), (1, 128), (2, 64)):
                        m = nc.tensor.transpose(PS[0:n, 6, 128 * k:128 * k + 128],
                                                per_expert[g % 2][:, 128 * k:128 * k + n], ident)
                    m.then_inc(sem("out_turned"), 1)
                    pe.wait_ge(sem("out_kept"), O0 + g + 1)
                    pe.wait_ge(sem("xT_ready"), 9 * GROUP + g)
                    a = per_expertT[g % 2]
                    nc.tensor.matmul(y_ps, a[:, 0:128], w("l2f_wo", 0, 128), start=True, stop=False)
                    nc.tensor.matmul(y_ps, a[:, 128:256], w("l2f_wo", 128, 128), start=False, stop=False)
                    nc.tensor.matmul(y_ps, a[0:64, 256:384], h64("l2f_wo2"), start=False,
                                     stop=True).then_inc(sem("y_done"), 1)

        def l2f_act(act, link):
            for j in range(4):
                act.wait_ge(sem("l2f_q"), j + 1)
                nc.scalar.activation(wide_q[:, j], bank(j), ACT.Copy).then_inc(sem("l2f_q_kept"), 1)
            act.wait_ge(sem("l2f_gl_kept"), 1)
            gs = gl.rearrange("p (g s h) e -> p g s (h e)", g=GROUP, s=2)[:, :, 0]
            nc.scalar.activation(glsig.rearrange("p g h e -> p g (h e)"), gs, ACT.Exp,
                                 scale=-1.0).then_inc(sem("l2f_expg"), 1)
            for g in range(GROUP):
                act.wait_ge(sem("l2f_xv"), g + 1)
                nc.scalar.activation(xv[:, g].rearrange("p e d -> p (e d)"), PS[:, 2 + g, 0:320],
                                     ACT.Copy).then_inc(sem("l2f_xv_kept"), 1)
            for i in range(GROUP + 3):
                if i >= 3:
                    keep_xT(act, 9, i - 3)
                if 1 <= i <= GROUP:
                    keep_probs(act, M0 + i - 1, TOK)
                if i < GROUP:
                    act.wait_ge(sem("shifted"), S0 + i + 1)
                    nc.scalar.activation(E[:, i % 2], E[:, i % 2], ACT.Exp, scale=WD ** -0.5).then_inc(sem("exps"), 1)
                if 1 <= i <= GROUP:
                    g = i - 1
                    act.wait_ge(sem("values_done"), M0 + g + 1)
                    if g >= 2:
                        act.wait_ge(sem("attended"), O0 + g - 1)
                    nc.scalar.activation(o_kept[g % 2].rearrange("p h d -> p (h d)"), bank(2 + g % 2),
                                         ACT.Copy).then_inc(sem("l2f_o_kept"), 1)
                if 2 <= i <= GROUP + 1:
                    g = i - 2
                    act.wait_ge(sem("out_turned"), O0 + g + 1)
                    a = per_expertT[g % 2]
                    link(nc.scalar.activation(a[:, 0:256], PS[:, 6, 0:256], ACT.Copy))
                    nc.scalar.activation(a[0:64, 256:384], PS[0:64, 6, 256:384], ACT.Copy).then_inc(sem("out_kept"), 1)
                    norm_rstd(act, link, 9, g)

        def l2f_dve(dve, link):
            for j in range(4):
                dve.wait_ge(sem("l2f_k"), j + 1)
                nc.vector.tensor_copy(wide_k[:, j], bank(4 + j)).then_inc(sem("l2f_k_kept"), 1)
            dve.wait_ge(sem("l2f_gl"), 1)
            nc.vector.tensor_copy(gl.rearrange("p m e -> p (m e)"), PS[:, 0, 0:320]).then_inc(sem("l2f_gl_kept"), 1)
            dve.wait_ge(sem("l2f_gl_kept"), 1)
            ranks(dve, link, gl, 64, NE, c("tie5"), glrank, *gl_pairs)
            dve.wait_ge(sem("l2f_expg"), 1)
            flat_sig = small[:, 640:800]
            link(nc.vector.tensor_scalar(flat_sig, flat_sig, 1.0, None, ALU.add))
            link(nc.vector.reciprocal(flat_sig, flat_sig))
            rank4 = glrank.rearrange("p (g s h) e -> p g s (h e)", g=GROUP, s=2)
            link(nc.vector.scalar_tensor_tensor(v_pick.rearrange("p g h e -> p g (h e)"), rank4[:, :, 0], 2.0,
                                                glsig.rearrange("p g h e -> p g (h e)"), ALU.is_lt, ALU.mult))
            nc.vector.tensor_scalar(o_pick.rearrange("p g h e -> p g (h e)"), rank4[:, :, 1], 2.0, None,
                                    ALU.is_lt).then_inc(sem("l2f_picked"), 1)
            for g in range(GROUP):
                dve.wait_ge(sem("l2f_parts"), g + 1)
                for e in range(4):
                    m = nc.vector.tensor_tensor(wide_v[:, g], wide_v[:, g], v_parts[g % 2][:, e], ALU.add)
                    if e < 3:
                        link(m)
                m.then_inc(sem("l2f_v"), 1)
            dve.wait_ge(sem("l2f_picked"), 1)
            for i in range(GROUP + 3):
                if i >= 3:
                    norm_apply(dve, 9, i - 3, Y[:, i - 3], X[:, i - 3])
                if i < GROUP:
                    dve.wait_ge(sem("scores"), S0 + i + 1)
                    if i >= 2:
                        dve.wait_ge(sem("probs_turned"), M0 + i - 1)
                    s = s_view(0, TOK)
                    m = mx[:, i].rearrange("p (b h) -> p b h", b=2)
                    link(nc.vector.tensor_reduce(m, s, AX.X, ALU.max))
                    nc.vector.tensor_tensor(E[:, i % 2].rearrange("p (b h k) -> p b h k", b=2, h=4), s, bc(m, 3, TOK),
                                            ALU.subtract).then_inc(sem("shifted"), 1)
                if 1 <= i <= GROUP:
                    g = i - 1
                    dve.wait_ge(sem("exps"), S0 + g + 1)
                    link(nc.vector.tensor_reduce(head_sum[:, g].rearrange("p (j b) -> p b j", b=2),
                                                 E[:, g % 2].rearrange("p (b j k) -> p b j k", b=2, j=4),
                                                 AX.X, ALU.add))
                    link(nc.vector.reciprocal(head_sum[:, g], head_sum[:, g]))
                    nc.vector.tensor_tensor(o_pick[:, g], o_pick[:, g], bc(head_sum[:, g], 2, NE),
                                            ALU.mult).then_inc(sem("l2f_shares"), 1)
                if 2 <= i <= GROUP + 1:
                    g = i - 2
                    dve.wait_ge(sem("l2f_o_parts"), g + 1)
                    a = per_expert[g % 2].rearrange("p (e d) -> p e d", e=NE)
                    link(nc.vector.tensor_reduce(a[:, 0:4], o_parts.rearrange("p e h d -> p e d h"), AX.X, ALU.add))
                    nc.vector.tensor_reduce(a[:, 4], o_part4[g % 2].rearrange("p h d -> p d h"), AX.X,
                                            ALU.add).then_inc(sem("attended"), 1)
                    dve.wait_ge(sem("y_done"), O0 + g + 1)
                    norm_stats(dve, link, 9, g, y_ps, X)

        def l2f_pool(pool):
            pool.wait_ge(sem("l2f_picked"), 1)
            for g in range(GROUP):
                pool.wait_ge(sem("l2f_xv_kept"), g + 1)
                if g >= 2:
                    pool.wait_ge(sem("l2f_v"), g - 1)
                for e in range(NE):
                    m = nc.gpsimd.tensor_tensor(wide_v[:, g] if e == 4 else v_parts[g % 2][:, e],
                                                bc(xv[:, g, e], 1, WH), bc(v_pick[:, g, :, e], 2, WD), ALU.mult)
                m.then_inc(sem("l2f_parts"), 1)
            for g in range(GROUP):
                pool.wait_ge(sem("l2f_shares"), g + 1)
                pool.wait_ge(sem("l2f_o_kept"), g + 1)
                if g >= 1:
                    pool.wait_ge(sem("attended"), O0 + g)
                for e in range(NE):
                    m = nc.gpsimd.tensor_tensor(o_parts[:, e] if e < 4 else o_part4[g % 2], o_kept[g % 2],
                                                bc(o_pick[:, g, :, e], 2, WD), ALU.mult)
                m.then_inc(sem("l2f_o_parts"), 1)

        def prepare_l3_pe(pe):
            pe.wait_ge(once("w64_loaded"), 48)
            for j in range(3):
                nc.tensor.matmul(PS[:, j, 0:128], h64("l3a_B", 128 * j, 128), h64("l3a_A"),
                                 start=True, stop=True).then_inc(once("l3_adapted"), 1)
            nc.tensor.matmul(PS[:, 3, 0:128], h64("l3a_pB"), h64("l3a_pA"),
                             start=True, stop=True).then_inc(once("l3_adapted"), 1)
            pe.wait_ge(once("l3_weights"), 4)
            nc.tensor.matmul(PS[:, 4, 0:128], w("l3a_wp"), l3_wpT[:, :],
                             start=True, stop=True).then_inc(once("l3_adapted"), 1)
            pe.wait_ge(once("l3_weights"), 5)

        def prepare_l3_dve(dve):
            dve.wait_ge(once("w128_loaded"), 16 * (len(W128_CUTS) + 1))
            for j in range(3):
                dve.wait_ge(once("l3_adapted"), j + 1)
                nc.vector.tensor_tensor(l3_wT[:, :].rearrange("p (i j) -> p i j", j=3)[:, :, j], PS[:, j, 0:128],
                                        w("l3a_w", 128 * j, 128), ALU.add).then_inc(once("l3_weights"), 1)
            dve.wait_ge(once("l3_adapted"), 4)
            nc.vector.tensor_tensor(l3_wpT[:, :], PS[:, 3, 0:128], w("l3a_wpT"),
                                    ALU.add).then_inc(once("l3_weights"), 1)
            dve.wait_ge(once("l3_adapted"), 5)
            nc.vector.tensor_copy(l3_proj[:, :], PS[:, 4, 0:128]).then_inc(once("l3_weights"), 1)

        def l3a_first_pe(pe):
            pe.wait_ge(sem("xT_ready"), 10 * GROUP)
            for j in range(3):
                nc.tensor.matmul(bank(j), l3_wT[:, 128 * j:128 * j + 128], XT[:, :],
                                 start=True, stop=True).then_inc(sem("l3a_qkv"), 1)

        def l3a_first_act(act, i):
            for j in range(3):
                act.wait_ge(sem("l3a_qkv"), j + 1)
                nc.scalar.activation(qkv_all[:, j, bass.ds(i * GT, GT)], bank(j), ACT.Copy).then_inc(once("qkv_kept"), 1)

        ch_stats = small[:, 0:36].rearrange("p (j n s) -> p j n s", j=3, n=2)
        ch_mv = small[:, 40:46].rearrange("p (j s) -> p j s", j=3)
        ch_scale = small[:, 2000:2003]
        ch_shift = small[:, 2004:2007]
        w_quant = small[:, 128:256]
        wqT = l3_wpT

        def norm_channels_dve(dve):
            def link(ins):
                chain[0] += 1
                ins.then_inc(once("between_chain"), 1)
                dve.wait_ge(once("between_chain"), chain[0])

            chain = [0]
            quantise(link, w("l3f_w"), 4, w_quant)
            nc.vector.tensor_copy(ch_scale, w_quant[:, 0:3]).then_inc(once("w_quantised"), 1)
            dve.wait_ge(once("qkv_kept"), 3 * GROUPS)
            for j in range(3):
                for n in range(2):
                    link(nc.vector.bn_stats(ch_stats[:, j, n], qkv_all[:, j, GT * n:GT * n + GT]))
                link(nc.vector.bn_aggr(ch_mv[:, j], ch_stats[:, j].rearrange("p n s -> p (n s)")))
            nc.vector.tensor_copy(ch_shift, ch_mv[:, :, 1]).then_inc(once("channel_var"), 1)
            dve.wait_ge(once("channel_rstd"), 1)
            link(nc.vector.tensor_tensor(ch_scale, ch_shift, w("l3a_gamma"), ALU.mult))
            link(nc.vector.tensor_tensor(ch_shift, ch_mv[:, :, 0], ch_scale, ALU.mult))
            link(nc.vector.tensor_tensor(ch_shift, w("l3a_beta"), ch_shift, ALU.subtract))
            dve.wait_ge(once("wT_turned"), 1)
            nc.vector.tensor_copy(wqT[:, :], PS[:, 0, 0:128]).then_inc(once("wT_kept"), 1)
            dve.wait_ge(once("wT_kept"), 1)

        def norm_channels_act(act):
            act.wait_ge(once("channel_var"), 1)
            nc.scalar.activation(ch_shift, ch_shift, ACT.Ln, bias=eps_col[:, 0:1]).then_inc(once("channel_ln"), 1)
            act.wait_ge(once("channel_ln"), 1)
            nc.scalar.activation(ch_shift, ch_shift, ACT.Exp, scale=-0.5).then_inc(once("channel_rstd"), 1)

        def turn_quantised(pe):
            pe.wait_ge(once("w_quantised"), 1)
            nc.tensor.transpose(PS[:, 0, 0:128], w_quant, ident).then_inc(once("wT_turned"), 1)
            pe.wait_ge(once("wT_kept"), 1)

        def quantise(link, src, blocks, dst):
            n = 32 * blocks
            y, y2, a, b = flatE[:, 0:n], flatE[:, 512:512 + n], flatE[:, 1024:1024 + n], flatE[:, 1536:1536 + n]
            inv, rnd = flatE[:, 2048:2048 + n], flatE[:, 2560:2560 + n]
            top, scale, rs = (small[:, 1024 + 16 * k:1024 + 16 * k + blocks] for k in range(3))

            def blk(ap):
                return ap.rearrange("p (b k) -> p b k", k=32)

            link(nc.vector.tensor_reduce(top, blk(src), AX.X, ALU.max, apply_absolute_value=True))
            link(nc.vector.tensor_scalar(scale, top, 1.0 / 7.5, 1e-30, ALU.mult, ALU.max))
            link(nc.vector.reciprocal(rs, scale))
            link(nc.vector.tensor_tensor(blk(y), blk(src), bc(rs, 2, 32), ALU.mult))
            link(nc.vector.tensor_tensor(y2, y, y, ALU.mult))
            link(nc.vector.tensor_scalar(a, y2, 4.0, -4.0, ALU.is_ge, ALU.mult))
            link(nc.vector.tensor_scalar(b, y2, 16.0, -2.0, ALU.is_ge, ALU.mult))
            link(nc.vector.scalar_tensor_tensor(inv, a, 8.0, b, ALU.add, ALU.add))
            link(nc.vector.tensor_tensor(y, y, inv, ALU.mult))
            link(nc.vector.tensor_scalar(rnd, y, ROUND, ROUND, ALU.add, ALU.subtract))
            link(nc.vector.tensor_tensor(y, y, rnd, ALU.subtract))
            link(nc.vector.scalar_tensor_tensor(y, y, -0.5, rnd, ALU.is_equal, ALU.subtract))
            link(nc.vector.reciprocal(inv, inv))
            link(nc.vector.scalar_tensor_tensor(y, y, -1.0, inv, ALU.mult, ALU.mult))
            link(nc.vector.tensor_tensor(blk(dst), blk(y), bc(scale, 2, 32), ALU.mult))

        qkv = [big2[:, GT * j:GT * j + GT] for j in range(3)]
        vmat = VB[:, :, 0]
        p_sum = small[:, 64:64 + GROUP]

        def l3a_pe(pe):
            pe.wait_ge(sem("l3a_normed"), 3)
            for g in range(GROUP):
                m = nc.tensor.transpose(PS[:, 6, g * 128:(g + 1) * 128], qkv[2][:, g * 128:(g + 1) * 128], ident)
            m.then_inc(sem("l3a_v"), 1)
            for i in range(GROUP + 3):
                if i < GROUP:
                    t = slice(i * 128, (i + 1) * 128)
                    if i >= 2:
                        pe.wait_ge(sem("l3a_shifted"), i - 1)
                    nc.tensor.matmul(PS[:, i % 2, 0:128], qkv[0][:, t], qkv[1][:, t], start=True, stop=False)
                    nc.tensor.matmul(PS[:, i % 2, 0:128], ident_bf[:, :], causal_bf[:, 0], start=False,
                                     stop=True).then_inc(sem("l3a_scores"), 1)
                if i >= 3:
                    turn_x(pe, 0, i - 3, X[:, i - 3])
                if 1 <= i <= GROUP:
                    g = i - 1
                    pe.wait_ge(sem("l3a_exp"), g + 1)
                    nc.tensor.transpose(PS[:, 2 + g % 2, 0:128], E[:, g % 2, 0:128], ident).then_inc(sem("l3a_pT"), 1)
                    pe.wait_ge(sem("l3a_pT_kept"), g + 1)
                    if g == 0:
                        pe.wait_ge(sem("l3a_v_kept"), 1)
                    if g >= 2:
                        pe.wait_ge(sem("attended"), g - 1)
                    nc.tensor.matmul(PS[:, 4 + g % 2, 0:128], PT[:, g % 2, 0:128], vmat[:, g],
                                     start=True, stop=True).then_inc(sem("l3a_o"), 1)
                if 2 <= i <= GROUP + 1:
                    g = i - 2
                    pe.wait_ge(sem("attended"), g + 1)
                    if g >= 1:
                        pe.wait_ge(sem("xT_ready"), g)
                    nc.tensor.transpose(ont_ps, ON[:, g, 0:128], ident).then_inc(sem("out_turned"), 1)
                    project_out(pe, g, g, l3_proj[:, :])

        def l3a_act(act, link):
            act.wait_ge(sem("l3a_v"), 1)
            nc.scalar.activation(vmat, PS[:, 6].rearrange("p (g d) -> p g d", g=GROUP),
                                 ACT.Copy).then_inc(sem("l3a_v_kept"), 1)
            for i in range(GROUP + 3):
                if i >= 3:
                    keep_xT(act, 0, i - 3)
                if 1 <= i <= GROUP:
                    g = i - 1
                    act.wait_ge(sem("l3a_pT"), g + 1)
                    if g >= 2:
                        act.wait_ge(sem("l3a_o"), g - 1)
                    nc.scalar.activation(PT[:, g % 2, 0:128], PS[:, 2 + g % 2, 0:128],
                                         ACT.Copy).then_inc(sem("l3a_pT_kept"), 1)
                if i < GROUP:
                    act.wait_ge(sem("l3a_shifted"), i + 1)
                    nc.scalar.activation(E[:, i % 2, 0:128], E[:, i % 2, 0:128], ACT.Exp,
                                         scale=DIM ** -0.5).then_inc(sem("l3a_exp"), 1)
                if 2 <= i <= GROUP + 1:
                    keep_out(act, i - 2, i - 2)
                    norm_rstd(act, link, 0, i - 2)

        def l3a_dve(dve, link, i):
            link(nc.vector.tensor_copy(X[:].rearrange("p g d -> p (g d)"), x_all[:, bass.ds(i * GT, GT)]))
            for j in range(3):
                nc.vector.tensor_scalar(qkv[j], qkv_all[:, j, bass.ds(i * GT, GT)], ch_scale[:, j:j + 1],
                                        ch_shift[:, j:j + 1], ALU.mult, ALU.add).then_inc(sem("l3a_normed"), 1)
            for i in range(GROUP + 3):
                if i >= 3:
                    norm_apply(dve, 0, i - 3, Y[:, i - 3], X[:, i - 3])
                if i < GROUP:
                    dve.wait_ge(sem("l3a_scores"), i + 1)
                    link(nc.vector.tensor_reduce(mx[:, i, 0:1], PS[:, i % 2, 0:128], AX.X, ALU.max))
                    if i >= 2:
                        dve.wait_ge(sem("l3a_pT"), i - 1)
                    nc.vector.tensor_scalar(E[:, i % 2, 0:128], PS[:, i % 2, 0:128], mx[:, i, 0:1], None,
                                            ALU.subtract).then_inc(sem("l3a_shifted"), 1)
                if 1 <= i <= GROUP:
                    g = i - 1
                    dve.wait_ge(sem("l3a_exp"), g + 1)
                    link(nc.vector.tensor_reduce(p_sum[:, g:g + 1], E[:, g % 2, 0:128], AX.X, ALU.add))
                    link(nc.vector.reciprocal(p_sum[:, g:g + 1], p_sum[:, g:g + 1]))
                    dve.wait_ge(sem("l3a_o"), g + 1)
                    nc.vector.tensor_scalar(ON[:, g, 0:128], PS[:, 4 + g % 2, 0:128], p_sum[:, g:g + 1], None,
                                            ALU.mult).then_inc(sem("attended"), 1)
                if 2 <= i <= GROUP + 1:
                    g = i - 2
                    dve.wait_ge(sem("y_done"), g + 1)
                    norm_stats(dve, link, 0, g, y_ps, X)

        x_quant = ON[:].rearrange("p g d -> p (g d)")[:, 0:GT]
        x_quantT = E2[:, 0, 0:GT]

        def second_pe(pe):
            l3a_pe(pe)
            pe.wait_ge(sem("ctx_ready"), 1)
            project_ctx(pe, 0, 0, w("l3x_wq"), w("l3x_wq"), w("l3x_wq"))
            attend_pe(pe, 0, 0, GROUP, 1, CTX, w("l3x_wo"))
            for g in range(GROUP):
                pe.wait_ge(sem("l3f_quantised"), 1)
                nc.tensor.transpose(PS[:, g, 0:128], x_quant[:, g * 128:(g + 1) * 128],
                                    ident).then_inc(sem("l3f_turned"), 1)
            for g in range(GROUP):
                pe.wait_ge(sem("l3f_kept"), g + 1)
                nc.tensor.matmul(PS[:, 4 + g % 3, 0:128] if g < 3 else PS[:, 0, 0:128],
                                 x_quantT[:, g * 128:(g + 1) * 128], wqT[:, :],
                                 start=True, stop=True).then_inc(sem("l3f_y"), 1)

        def second_act(act, link, i):
            l3a_act(act, link)
            keep_qk(act, 0, w("l3x_bq"), w("l3x_bq"))
            attend_act(act, link, 0, GROUP, 1, CTX, lambda u: exp_unit(act, 0, u, CTX, SCALE))
            for g in range(GROUP):
                act.wait_ge(sem("l3f_turned"), g + 1)
                nc.scalar.activation(x_quantT[:, g * 128:(g + 1) * 128], PS[:, g, 0:128],
                                     ACT.Copy).then_inc(sem("l3f_kept"), 1)
            for g in range(GROUP):
                norm_rstd(act, link, 2, g)

        def second_dve(dve, link, i):
            l3a_dve(dve, link, i)
            keep_v(dve, 0, r("l3x_bv"))
            dve.wait_ge(sem("residual"), 1)
            attend_dve(dve, link, 0, GROUP, 1, XR, lambda u: shift_unit(dve, link, 0, u, CTX, 0))
            dve.wait_ge(sem("x_ready"), 2 * GROUP)
            quantise(link, X[:].rearrange("p g d -> p (g d)"), 4 * GROUP, x_quant)
            nc.vector.tensor_copy(small[:, 1100:1101], x_quant[:, 0:1]).then_inc(sem("l3f_quantised"), 1)
            dve.wait_ge(sem("residual"), 2)
            norms_dve(dve, link, 2, "l3f_y", lambda g: PS[:, 4 + g, 0:128] if g < 3 else PS[:, 0, 0:128], XR)
            dve.wait_ge(sem("x_ready"), 3 * GROUP)
            nc.vector.tensor_copy(x_all[:, bass.ds(i * GT, GT)],
                                  X[:].rearrange("p g d -> p (g d)")).then_inc(once("x_kept"), 1)

        def second_pool(pool, i):
            nc.gpsimd.tensor_copy(CT[:, :], ctx_all[:, bass.ds(i * GC, GC)]).then_inc(sem("ctx_ready"), 1)
            add_bias(pool, 0, r("l3x_bo"))
            spread_all(pool, 0, CTX, "k_kept", 1)
            add_bias(pool, 1, r("l3f_b"))

        pool_stages = [l0x_pool, l0f_pool, l1a_pool, l1x_pool, l1f_pool, l2a_pool, l2x_pool, l2f_pool]
        act_stages = [l0x_act, l0f_act, l1a_act, l1x_act, l1f_act, l2a_act, l2x_act, l2f_act]
        dve_stages = [l0x_dve, l0f_dve, l1a_dve, l1x_dve, l1f_dve, l2a_dve, l2x_dve, l2f_dve]
        pe_stages = [l0x_pe, l0f_pe, l1a_pe, l1x_pe, l1f_pe, l2a_pe, l2x_pe, l2f_pe]

        def load_all(sp):
            sp.dma_start(x_all[:, :], x_in).then_inc(once("x_loaded"), 16)
            sp.dma_start(con[:, :], con_in).then_inc(once("con_loaded"), 16)
            sp.dma_start(row[:, :], row_in.to_broadcast([128, ROW_N])).then_inc(once("row_loaded"), 16)
            sp.dma_start(ctx_all[:, :], ctx_in).then_inc(once("ctx_loaded"), 16)
            sp.dma_start(mask_u8[:, :], mask_in).then_inc(once("ctx_loaded"), 16)
            sp.dma_start(w64[:, :], w64_in).then_inc(once("w64_loaded"), 16)
            sp.dma_start(w16[:, :], w16_in).then_inc(once("w64_loaded"), 16)
            sp.dma_start(w8[:, :], w8_in).then_inc(once("w64_loaded"), 16)
            cuts = [0] + [W128[n][0] for n in W128_CUTS] + [W128_N]
            for lo, hi in zip(cuts, cuts[1:]):
                sp.dma_start(w128[:, lo:hi], w128_in[:, lo:hi]).then_inc(once("w128_loaded"), 16)

        def once_pool(pool):
            nc.gpsimd.memset(eps_col[:, :], EPS).then_inc(once("consts"), 1)
            nc.gpsimd.memset(one_col[:, :], 1.0).then_inc(once("consts"), 1)
            nc.gpsimd.memset(V[:, :, :, DH:DH + 1], 1.0).then_inc(once("consts"), 1)

        def once_dve(dve):
            dve.wait_ge(once("con_loaded"), 16)
            dve.wait_ge(once("w64_loaded"), 48)
            dve.wait_ge(once("row_loaded"), 16)
            nc.vector.tensor_copy(ident_bf[:, :], ident).then_inc(once("casts"), 1)
            nc.vector.tensor_copy(causal_bf[:], bc(c("causal"), 1, 4)).then_inc(once("casts"), 1)
            nc.vector.tensor_copy(ones_bf[:, :], c("ones")[0:1, :]).then_inc(once("casts"), 1)
            nc.vector.tensor_copy(w3_rep[:, :], h64("l1x_w3").to_broadcast([64, 128])).then_inc(once("casts"), 1)
            nc.vector.tensor_scalar(att_mix[:, :], r("l2x_w"), -1.0, 1.0, ALU.mult, ALU.add).then_inc(once("casts"), 1)

        def turn_around(eng, i, first):
            eng.drain().then_inc(once("iteration_done"), 1)
            eng.wait_ge(once("iteration_go"), i + first + 1)

        @block.gpsimd
        def _(pool):
            once_pool(pool)
            with pool.Fori(0, GROUPS) as i:
                l0a_pool(pool, i)
                for s in pool_stages:
                    s(pool)
                turn_around(pool, i, 0)
            with pool.Fori(0, GROUPS) as i:
                second_pool(pool, i)
                turn_around(pool, i, GROUPS)

        @block.scalar
        def _(act):
            with act.Fori(0, GROUPS) as i:
                act.preload_act_table_set("natural_log_exp_and_others")
                link = linker(act, "act_chain")
                l0a_act(act, link)
                for s in act_stages:
                    s(act, link)
                l3a_first_act(act, i)
                turn_around(act, i, 0)
            norm_channels_act(act)
            with act.Fori(0, GROUPS) as i:
                act.preload_act_table_set("natural_log_exp_and_others")
                second_act(act, linker(act, "act_chain"), i)
                turn_around(act, i, GROUPS)

        @block.vector
        def _(dve):
            once_dve(dve)
            prepare_l3_dve(dve)
            with dve.Fori(0, GROUPS) as i:
                link = linker(dve, "dve_chain")
                l0a_dve(dve, link, i)
                for s in dve_stages:
                    s(dve, link)
                dve.wait_ge(sem("x_ready"), GROUP * 10)
                nc.vector.tensor_copy(x_all[:, bass.ds(i * GT, GT)],
                                      X[:].rearrange("p g d -> p (g d)")).then_inc(once("x_kept"), 1)
                turn_around(dve, i, 0)
            norm_channels_dve(dve)
            with dve.Fori(0, GROUPS) as i:
                second_dve(dve, linker(dve, "dve_chain2"), i)
                turn_around(dve, i, GROUPS)

        @block.tensor
        def _(pe):
            prepare_l3_pe(pe)
            with pe.Fori(0, GROUPS) as i:
                l0a_pe(pe)
                for s in pe_stages:
                    s(pe)
                l3a_first_pe(pe)
                turn_around(pe, i, 0)
            turn_quantised(pe)
            with pe.Fori(0, GROUPS) as i:
                second_pe(pe)
                turn_around(pe, i, GROUPS)

        @block.sync
        def _(sp):
            load_all(sp)
            numbers = sorted(s.num for s in body_sems.values())
            ends = [i for i in range(1, len(numbers) + 1) if i == len(numbers) or numbers[i] > numbers[i - 1] + 1]
            runs = [range(numbers[i], numbers[j - 1] + 1) for i, j in zip([0] + ends[:-1], ends)]
            for turn in range(2 * GROUPS):
                sp.wait_ge(once("iteration_done"), 4 * (turn + 1))
                for numbers_of_run in runs:
                    last = sp.sem_clear(numbers_of_run)
                last.then_inc(once("iteration_go"), 1)
            sp.wait_ge(once("x_kept"), 2 * GROUPS)
            sp.dma_start(out, x_all[:, :]).then_inc(once("stored"), 16)
            sp.wait_ge(once("stored"), 16)


def _pack(pieces, rows):
    return np.ascontiguousarray(np.concatenate([np.asarray(p).reshape(rows, -1) for p in pieces], axis=1))


def kernel(**t):
    import concourse.bacc as _bacc
    from concourse.bass_utils import run_bass_kernel_spmd as _run

    a = {k: np.asarray(v) for k, v in t.items()}
    wqkv = a["L2_attn_W_qkv"]
    swap = np.arange(128) ^ 1
    wkv = a["L2_xattn_w_kv"]
    w128 = {
        "l0a_gamma": a["L0_attn_gamma"], "l0a_beta": a["L0_attn_beta"],
        "l0a_wk": a["L0_attn_Wk"].T, "l0a_wq": a["L0_attn_Wq"].T, "l0a_wv": a["L0_attn_Wv"].T,
        "l0x_wq": a["L0_xattn_wq"], "l0x_wk": a["L0_xattn_wk"], "l0x_wv": a["L0_xattn_wv"],
        "l0x_wo": a["L0_xattn_wo"], "l0x_bq": a["L0_xattn_bq"], "l0x_bk": a["L0_xattn_bk"],
        "l0f_wg": a["L0_ffn_Wg"],
        "l0f_b1": a["L0_ffn_b1"].reshape(8, 4, 128).transpose(2, 0, 1),
        "l0f_w1": a["L0_ffn_W1"].transpose(1, 0, 2),
        "l0f_w2": a["L0_ffn_W2"].reshape(8, 4, 128, 128).transpose(2, 0, 1, 3),
        "l1a_wq": a["L1_attn_Wq"], "l1a_wk": a["L1_attn_Wk"], "l1a_wv": a["L1_attn_Wv"],
        "l1a_wg": a["L1_attn_Wg"], "l1a_w1": a["L1_attn_gk_w1"], "l1a_b2": a["L1_attn_gk_b2"],
        "l1a_wo": a["L1_attn_Wo"].reshape(2, 128, 128).transpose(1, 0, 2),
        "l1x_wq": a["L1_xattn_Wq"].T, "l1x_wk": a["L1_xattn_Wk"].T, "l1x_wv": a["L1_xattn_Wv"].T,
        "l1x_wo": a["L1_xattn_Wo"].T, "l1x_bq": a["L1_xattn_bq"], "l1x_bk": a["L1_xattn_bk"],
        "l1f_wg": a["L1_ffn_gate_w"].T, "l1f_b1": a["L1_ffn_b1"].T, "l1f_b2": a["L1_ffn_b2"].T,
        "l1f_w1": a["L1_ffn_w1"].transpose(1, 0, 2), "l1f_w2": a["L1_ffn_w2"].transpose(1, 0, 2),
        "l1f_w3": a["L1_ffn_w3"].transpose(1, 0, 2),
        "l2a_wq": wqkv[:, 0:128], "l2a_wk": wqkv[:, 128:256],
        "l2a_wqs": wqkv[:, 0:128][:, swap], "l2a_wks": wqkv[:, 128:256][:, swap],
        "l2a_wv": wqkv[:, 256:384], "l2a_wo": a["L2_attn_W_out"],
        "l2x_wk": wkv[:, 0:128], "l2x_wv": wkv[:, 128:256], "l2x_wq": a["L2_xattn_w_q"],
        "l2x_wla": a["L2_xattn_w_la"], "l2x_wo": a["L2_xattn_w_proj"],
        "l2f_wq": a["L2_ffn_Wq"], "l2f_wk": a["L2_ffn_Wk"],
        "l2f_wg": np.concatenate([a["L2_ffn_Ws"], a["L2_ffn_Wd"]], axis=1),
        "l2f_wv": a["L2_ffn_Wv"].transpose(1, 0, 2),
        "l2f_wo": a["L2_ffn_Wo"].reshape(320, 128)[:256].reshape(2, 128, 128).transpose(1, 0, 2),
        "l3a_w": a["L3_attn_W_attn"].reshape(128, 3, 128).transpose(2, 1, 0),
        "l3a_wp": a["L3_attn_W_proj"], "l3a_wpT": a["L3_attn_W_proj"].T,
        "l3a_gamma": a["L3_attn_bn_gamma"].reshape(3, 128).T, "l3a_beta": a["L3_attn_bn_beta"].reshape(3, 128).T,
        "l3x_wq": a["L3_xattn_Wq"], "l3x_wo": a["L3_xattn_Wo"], "l3x_bq": a["L3_xattn_bq"],
        "l3f_w": a["L3_ffn_weight"],
    }
    w64 = {
        "l0a_bk": a["L0_attn_bk"], "l0a_bq": a["L0_attn_bq"], "l1x_w2": a["L1_xattn_w2"].T,
        "l1x_w3": a["L1_xattn_w3"].T, "l1x_b1": a["L1_xattn_b1"], "l1x_b2": a["L1_xattn_b2"],
        "l2f_wo2": a["L2_ffn_Wo"].reshape(320, 128)[256:],
        "l3a_A": a["L3_attn_lora_attn_A"].T, "l3a_B": a["L3_attn_lora_attn_B"],
        "l3a_pA": a["L3_attn_lora_proj_A"].T, "l3a_pB": a["L3_attn_lora_proj_B"],
    }
    row = {
        "l0a_bv": a["L0_attn_bv"], "l0x_bv": a["L0_xattn_bv"], "l0x_bo": a["L0_xattn_bo"], "l0f_bg": a["L0_ffn_bg"],
        "l1a_gn": a["L1_attn_g_norm_w"], "l1x_bv": a["L1_xattn_bv"], "l1x_bo": a["L1_xattn_bo"],
        "l1x_w1": a["L1_xattn_w1"].T, "l1x_b3": a["L1_xattn_b3"], "l1f_bg": a["L1_ffn_gate_b"],
        "l2a_bo": a["L2_attn_b_out"], "l2x_bo": a["L2_xattn_b_proj"], "l2x_w": a["L2_xattn_att_weight"],
        "l3x_bv": a["L3_xattn_bq"], "l3x_bo": a["L3_xattn_bo"], "l3f_b": a["L3_ffn_bias"],
    }
    arrays = {
        "x_in": np.ascontiguousarray(a["x"].transpose(1, 0, 2)).reshape(128, BATCH * DIM),
        "ctx_in": np.ascontiguousarray(a["ctx_1024"].transpose(2, 0, 1)).reshape(128, BATCH * CTX),
        "mask_in": np.ascontiguousarray(a["mask_BxS2_bk0"]).reshape(1, BATCH * CTX),
        "w128_in": _pack([w128[n] for n in W128], 128),
        "w64_in": _pack([w64[n] for n in W64], 64),
        "w16_in": np.ascontiguousarray(a["L1_attn_gk_w2"]),
        "w8_in": _pack([a["L0_ffn_b2"], a["L1_ffn_b3"]], 8),
        "row_in": _pack([row[n] for n in ROW], 1),
        "con_in": constants(),
    }
    nc = _bacc.Bacc("TRN2", target_bir_lowering=False, num_devices=1)
    args = [nc.dram_tensor(n, v.shape, mybir.dt.from_np(v.dtype), kind="ExternalInput").ap()
            for n, v in arrays.items()]
    out = nc.dram_tensor("out", (128, BATCH * DIM), F32, kind="ExternalOutput").ap()
    decoder(nc, *args, out)
    r = _run(nc, [arrays], core_ids=[0])
    return np.ascontiguousarray(r.results[0]["out"].reshape(TOK, BATCH, DIM).transpose(1, 0, 2))
```

```python
from contextlib import ExitStack

import numpy as np

import concourse.bass as bass
from concourse import mybir

F32 = mybir.dt.float32
BF16 = mybir.dt.bfloat16
U8 = mybir.dt.uint8
ALU = mybir.AluOpType
ACT = mybir.ActivationFunctionType
AX = mybir.AxisListType

BATCH, TOK, DIM, CTX = 8, 128, 128, 77
GROUP = 4
GROUPS = BATCH // GROUP
GT = GROUP * TOK
GC = GROUP * CTX
HEADS, DH = 16, 8
HALF = 8
UNITS = 2 * GROUP
VSTEP = 4 * 32 + DH
VW = 4 * VSTEP
EPS = 1e-5
TTT_LR = 0.01
GATE_NORM = 16.0
CHUNK = 64
MASKED = -1e30
ROUND = 1.5 * 2.0 ** 23


def columns(pieces):
    at, n = {}, 0
    for name, width in pieces:
        at[name] = (n, width)
        n += width
    return at, n


W128_PIECES = [
    ("l0a_gamma", 1), ("l0a_beta", 1), ("l0a_wk", 64), ("l0a_wq", 64), ("l0a_wv", 128),
    ("l0x_wq", 128), ("l0x_wk", 128), ("l0x_wv", 128), ("l0x_wo", 128), ("l0x_bq", 1), ("l0x_bk", 1),
    ("l0f_wg", 8), ("l0f_b1", 32), ("l0f_w1", 4096), ("l0f_w2", 4096),
    ("l1a_wq", 128), ("l1a_wk", 128), ("l1a_wv", 256), ("l1a_wg", 256), ("l1a_w1", 16), ("l1a_b2", 1),
    ("l1a_wo", 256),
    ("l1x_wq", 128), ("l1x_wk", 128), ("l1x_wv", 128), ("l1x_wo", 128), ("l1x_bq", 1), ("l1x_bk", 1),
    ("l1f_wg", 8), ("l1f_b1", 8), ("l1f_b2", 8), ("l1f_w1", 1024), ("l1f_w2", 1024), ("l1f_w3", 1024),
    ("l2a_wq", 128), ("l2a_wk", 128), ("l2a_wqs", 128), ("l2a_wks", 128), ("l2a_wv", 128), ("l2a_wo", 128),
    ("l2x_wk", 128), ("l2x_wv", 128), ("l2x_wq", 128), ("l2x_wla", 16), ("l2x_wo", 128),
    ("l2f_wq", 512), ("l2f_wk", 512), ("l2f_wg", 80), ("l2f_wv", 320), ("l2f_wo", 256),
    ("l3a_w", 384), ("l3a_wp", 128), ("l3a_wpT", 128), ("l3a_gamma", 3), ("l3a_beta", 3),
    ("l3x_wq", 128), ("l3x_wo", 128), ("l3x_bq", 1), ("l3f_w", 128),
]
W128, W128_N = columns(W128_PIECES)
W128_CUTS = ["l0f_w1", "l0f_w2", "l1a_wq", "l2a_wq"]
W64, W64_N = columns([("l0a_bk", 1), ("l0a_bq", 1), ("l1x_w2", 64), ("l1x_w3", 1), ("l1x_b1", 1), ("l1x_b2", 1),
                      ("l2f_wo2", 128), ("l3a_A", 128), ("l3a_B", 384), ("l3a_pA", 128), ("l3a_pB", 128)])
ROW, ROW_N = columns([("l0a_bv", 128), ("l0x_bv", 128), ("l0x_bo", 128), ("l0f_bg", 8), ("l1a_gn", 64),
                      ("l1x_bv", 128), ("l1x_bo", 128), ("l1x_w1", 192), ("l1x_b3", 1), ("l1f_bg", 8),
                      ("l2a_bo", 128), ("l2x_bo", 128), ("l2x_w", 1), ("l3x_bv", 128), ("l3x_bo", 128),
                      ("l3f_b", 128)])
CON, CON_N = columns([("ident", 128), ("row0", 128), ("hm16", 16), ("hm4", 4), ("low", 128), ("up", 128),
                      ("sup", 128), ("incl", 128), ("causal", 128), ("scan", 512), ("tie8", 64), ("tie5", 25),
                      ("cos", 128), ("sin", 128), ("ones", 128)])


def constants():
    c = np.zeros((128, CON_N), np.float32)

    def put(name, a):
        o, w = CON[name]
        c[:, o:o + w] = np.asarray(a, np.float32).reshape(-1, w)

    d = np.arange(128)
    put("ident", np.eye(128))
    put("row0", np.repeat(d[:, None] == 0, 128, axis=1))
    put("hm16", d[:, None] // DH == np.arange(16))
    put("hm4", d[:, None] // 32 == np.arange(4))
    put("low", -TTT_LR * (d[:, None] > d[None, :]))
    put("up", -TTT_LR * (d[:, None] < d[None, :]))
    put("sup", d[:, None] < d[None, :])
    put("incl", d[:, None] <= d[None, :])
    put("causal", np.where(d[None, :] > d[:, None], MASKED, 0.0))
    put("scan", np.tile((np.arange(512) % CHUNK != 0), (128, 1)))
    put("tie8", np.tile((np.arange(8)[None, :] < np.arange(8)[:, None]).reshape(1, 64), (128, 1)))
    put("tie5", np.tile((np.arange(5)[None, :] < np.arange(5)[:, None]).reshape(1, 25), (128, 1)))
    half = DH // 2
    inv = (1.0 / 10000.0 ** (np.arange(half, dtype=np.float32) / half)).astype(np.float32)
    ang = d.astype(np.float32)[None, :] * inv[(d % DH) // 2][:, None]
    put("cos", np.cos(ang))
    put("sin", np.sin(ang) * np.where(d % 2 == 0, -1.0, 1.0)[:, None])
    put("ones", np.ones((128, 128)))
    return c


def decoder(nc, x_in, ctx_in, mask_in, w128_in, w64_in, w16_in, w8_in, row_in, con_in, out):
    with ExitStack() as ctx:
        def sb(name, shape, dt=F32):
            return ctx.enter_context(nc.sbuf_tensor(name, shape, dt))

        body_sems, once_sems = {}, {}

        shared = {"l3a_normed": "l0a_kT", "l3a_v": "l0a_v", "l3a_v_kept": "l0a_qT", "l3a_scores": "l0a_kk",
                  "l3a_shifted": "l0a_masked", "l3a_exp": "l0a_k_kept", "l3a_pT": "l0a_kq", "l3a_pT_kept": "l0a_q_kept",
                  "l3a_o": "l0a_level", "l3f_quantised": "l0a_u", "l3f_turned": "l0a_step", "l3f_kept": "l0a_powers",
                  "l3f_y": "l0a_y", "dve_chain2": "dve_chain"}

        def sem(name):
            name = shared.get(name, name)
            if name not in body_sems:
                body_sems[name] = ctx.enter_context(nc.semaphore(name))
            return body_sems[name]

        def once(name):
            if name not in once_sems:
                once_sems[name] = ctx.enter_context(nc.semaphore(name))
            return once_sems[name]

        def bc(ap, axis, n):
            a = ap.unsqueeze(axis)
            shape = list(a.shape)
            shape[axis] = n
            return a.to_broadcast(shape)

        w128 = sb("w128", [128, W128_N])
        w64 = sb("w64", [64, W64_N])
        w16 = sb("w16", [16, 128])
        w8 = sb("w8", [8, 256])
        row = sb("row", [128, ROW_N])
        con = sb("con", [128, CON_N])
        ident_bf = sb("ident_bf", [128, 128], BF16)
        causal_bf = sb("causal_bf", [128, 4, 128], BF16)
        row0_bf = sb("row0_bf", [128, 128], BF16)
        eps_col = sb("eps_col", [128, 1])
        one_col = sb("one_col", [128, 1])
        w3_rep = sb("w3_rep", [64, 128])
        att_mix = sb("att_mix", [128, 1])
        l3_wT = sb("l3_wT", [128, 384])
        l3_proj = sb("l3_proj", [128, 128])
        l3_wpT = sb("l3_wpT", [128, 128])
        x_all = sb("x_all", [128, BATCH * DIM])
        ctx_all = sb("ctx_all", [128, BATCH * CTX])
        mask_u8 = sb("mask_u8", [128, BATCH * CTX], U8)
        qkv_all = sb("qkv_all", [128, 3, BATCH * TOK])

        X = sb("X", [128, GROUP, DIM])
        XR = sb("XR", [128, GROUP, DIM])
        Y = sb("Y", [128, GROUP, DIM])
        XT = sb("XT", [128, GT])
        CT = sb("CT", [128, GC])
        stats = sb("stats", [128, GROUP, 6])
        mv = sb("mv", [128, GROUP, 2])
        rstd = sb("rstd", [128, GROUP])

        QT = sb("QT", [128, 1, GT])
        KT = sb("KT", [128, 1, GT])
        VS = sb("VS", [128, GROUP, VW])
        VB = sb("VB", [128, GROUP, 4, 128])
        KB = sb("KB", [128, 2, 4, 128])
        E = sb("E", [128, 3, HALF * 128])
        E2 = sb("E2", [128, 2, HALF * 128])
        PT = sb("PT", [128, 2, HALF * 128])
        mx = sb("mx", [128, UNITS, HALF])
        sums = sb("sums", [128, GROUP, HEADS])
        RX = sb("RX", [128, 2, 128])
        flat_VS = VS[:].rearrange("p g k -> p (g k)")
        ON = flat_VS[:, 0:GROUP * 256].rearrange("p (g k) -> p g k", g=GROUP)
        ONT = sb("ONT", [128, 2, 2, 128])
        mask_b = sb("mask_b", [128, GROUP, 4, CTX], BF16)
        big = sb("big", [128, UNITS, HALF * CTX])
        big2 = big[:].rearrange("p u k -> p (u k)")[:, 0:4096]
        small = sb("small", [128, 2048])

        def w(name, a=0, n=None):
            o, width = W128[name]
            return w128[:, o + a:o + a + (width if n is None else n)]

        def h64(name, a=0, n=None):
            o, width = W64[name]
            return w64[:, o + a:o + a + (width if n is None else n)]

        def r(name, a=0, n=None):
            o, width = ROW[name]
            return row[:, o + a:o + a + (width if n is None else n)]

        def c(name, a=0, n=None):
            o, width = CON[name]
            return con[:, o + a:o + a + (width if n is None else n)]

        ident = c("ident")

        PS = ctx.enter_context(nc.psum_tensor("PS", [128, 8, 512], F32))

        def bank(b, n=512):
            return PS[:, b, 0:n]

        y_ps = PS[:, 7, 0:128]
        ont_ps = PS[:, 7, 256:384]
        xt_ps = PS[:, 7, 384:512]

        block = ctx.enter_context(nc.Block())

        def linker(eng, name):
            count = [0]

            def link(ins, wait=True):
                count[0] += 1
                ins.then_inc(sem(name), 1)
                if wait:
                    eng.wait_ge(sem(name), count[0])
            return link

        def norm_stats(dve, link, n, g, y, res):
            link(nc.vector.tensor_tensor(Y[:, g], y, res[:, g], ALU.add))
            link(nc.vector.bn_stats(stats[:, g], Y[:, g]))
            nc.vector.bn_aggr(mv[:, g], stats[:, g]).then_inc(sem("norm_var"), 1)

        def norm_rstd(act, link, n, g):
            act.wait_ge(sem("norm_var"), n * GROUP + g + 1)
            link(nc.scalar.activation(rstd[:, g:g + 1], mv[:, g, 1:2], ACT.Ln, bias=eps_col[:, 0:1]))
            nc.scalar.activation(rstd[:, g:g + 1], rstd[:, g:g + 1], ACT.Exp, scale=-0.5).then_inc(sem("norm_rstd"), 1)

        def norm_apply(dve, n, g, src, dst):
            dve.wait_ge(sem("norm_var"), n * GROUP + g + 1)
            dve.wait_ge(sem("norm_rstd"), n * GROUP + g + 1)
            nc.vector.tensor_scalar(dst, src, mv[:, g, 0:1], rstd[:, g:g + 1],
                                    ALU.subtract, ALU.mult).then_inc(sem("x_ready"), 1)

        def turn_x(pe, n, g, src):
            pe.wait_ge(sem("x_ready"), n * GROUP + g + 1)
            if n * GROUP + g > 0:
                pe.wait_ge(sem("xT_ready"), n * GROUP + g)
            nc.tensor.transpose(xt_ps, src, ident).then_inc(sem("xT_turned"), 1)

        def keep_xT(act, n, g):
            act.wait_ge(sem("xT_turned"), n * GROUP + g + 1)
            nc.scalar.activation(XT[:, g * 128:(g + 1) * 128], xt_ps, ACT.Copy).then_inc(sem("xT_ready"), 1)

        def norms_dve(dve, link, n, ready, y, res, outs=None):
            for g in range(GROUP + 1):
                if g < GROUP:
                    dve.wait_ge(sem(ready), g + 1)
                    norm_stats(dve, link, n, g, y(g), res)
                if g >= 1:
                    norm_apply(dve, n, g - 1, Y[:, g - 1], X[:, g - 1] if outs is None else outs(g - 1))

        def norms_act(act, link, n):
            for g in range(GROUP + 1):
                if g < GROUP:
                    norm_rstd(act, link, n, g)
                if g >= 1:
                    keep_xT(act, n, g - 1)

        def norms_pe(pe, n):
            for g in range(GROUP):
                turn_x(pe, n, g, X[:, g])

        def add_bias(pool, n, bias):
            pool.wait_ge(sem("x_ready"), (n + 1) * GROUP)
            nc.gpsimd.tensor_tensor(XR[:], X[:], bc(bias, 1, GROUP), ALU.add).then_inc(sem("residual"), 1)

        def spread(a, g, K):
            if g % 2 == 0:
                buf = VB[:].rearrange("p g c d -> p (g c d)")
            else:
                buf = PT[:].rearrange("p n k -> p (n k)") if a == 1 else big2[:, 0:2048]
            return buf[:, 0:HEADS * K].rearrange("p (h k) -> p h k", h=HEADS)

        def spread_keys(pool, a, g, K):
            if g >= 2:
                pool.wait_ge(sem("scores"), (a * GROUP + g - 2) * 2 + 2)
            for half in range(2):
                heads = slice(half * HALF, (half + 1) * HALF)
                nc.gpsimd.tensor_tensor(spread(a, g, K)[:, heads], bc(KT[:, 0, g * K:(g + 1) * K], 1, HALF),
                                        bc(c("hm16")[:, heads], 2, K), ALU.mult).then_inc(sem("keys_spread"), 1)

        def s_view(u, K):
            b = 2 * (u % 2)
            return PS[:, b:b + 2, 0:4 * K].rearrange("p b (h k) -> p b h k", h=4)

        def scores(pe, a, u, K, extra=None):
            g = u // 2
            pe.wait_ge(sem("keys_spread"), a * UNITS + u + 1)
            if a * UNITS + u >= 2:
                pe.wait_ge(sem("shifted"), a * UNITS + u - 1)
            for j in range(2):
                h = HALF * (u % 2) + 4 * j
                m = nc.tensor.matmul(PS[:, 2 * (u % 2) + j, 0:4 * K], QT[:, 0, g * 128:(g + 1) * 128],
                                     spread(a, g, K)[:, h:h + 4], start=True, stop=extra is None)
                if extra is not None:
                    m = nc.tensor.matmul(PS[:, 2 * (u % 2) + j, 0:4 * K], *extra(g), start=False, stop=True)
            m.then_inc(sem("scores"), 1)

        def shift(dve, link, a, u, K, dst):
            dve.wait_ge(sem("scores"), a * UNITS + u + 1)
            s = s_view(u, K)
            m = mx[:, u].rearrange("p (b h) -> p b h", b=2)
            link(nc.vector.tensor_reduce(m, s, AX.X, ALU.max))
            nc.vector.tensor_tensor(dst.rearrange("p (b h k) -> p b h k", b=2, h=4), s, bc(m, 3, K),
                                    ALU.subtract).then_inc(sem("shifted"), 1)

        def turn_probs(pe, m, K, src):
            if m >= 1:
                pe.wait_ge(sem("probs_kept"), m)
            for h in range(HALF):
                t = nc.tensor.transpose(PS[0:K, 4 + h // 4, (h % 4) * 128:(h % 4) * 128 + 128],
                                        src[:, h * K:(h + 1) * K], ident)
            t.then_inc(sem("probs_turned"), 1)

        def keep_probs(act, m, K):
            act.wait_ge(sem("probs_turned"), m + 1)
            if m >= 2:
                act.wait_ge(sem("values_done"), m - 1)
            nc.scalar.activation(PT[0:K, m % 2, :].rearrange("p (b k) -> p b k", b=2), PS[0:K, 4:6, :],
                                 ACT.Copy).then_inc(sem("probs_kept"), 1)

        def v_spread(rows):
            return VS[rows].rearrange("p g (s x) -> p g s x", s=4)[:, :, :, 0:128].rearrange(
                "p g s (c e) -> p g s c e", c=4)[:, :, :, :, 0:DH]

        o_ps = PS[:, 6, 0:128]
        rec_ps = PS[:, 6, 128:256]

        def values(pe, m, u, K):
            pe.wait_ge(sem("probs_kept"), m + 1)
            g, half = u // 2, u % 2
            for s in range(2):
                for col in range(4):
                    h = 4 * s + col
                    t = nc.tensor.matmul(PS[32 * col:32 * col + 32, 6, 0:128],
                                         VS[0:K, g, 32 * (half * HALF + h):32 * (half * HALF + h) + 32],
                                         PT[0:K, m % 2, h * 128:(h + 1) * 128],
                                         start=half == 0 and s == 0, stop=half == 1 and s == 1)
            t.then_inc(sem("values_done"), 1)

        def sum_unit(dve, link, u, e, done, count, K):
            g, half = u // 2, u % 2
            dve.wait_ge(sem(done), count)
            m = nc.vector.tensor_reduce(sums[:, g, half * HALF:(half + 1) * HALF],
                                        e[:, 0:HALF * K].rearrange("p (h k) -> p h k", h=HALF), AX.X, ALU.add)
            link(m, wait=half == 1)
            if half == 1:
                nc.vector.reciprocal(RX[:, g % 2].rearrange("p (c s d) -> p s c d", c=4, s=4),
                                     bc(sums[:, g].rearrange("p (s c) -> p s c", s=4), 3, DH)
                                     ).then_inc(sem("attended"), 1)

        def turn_sums(pe, o, g):
            pe.wait_ge(sem("attended"), o + 1)
            nc.tensor.transpose(rec_ps, RX[:, g % 2], ident).then_inc(sem("sums_turned"), 1)

        def normalise(dve, m, g):
            dve.wait_ge(sem("values_done"), m + 1)
            dve.wait_ge(sem("rec_kept"), m // 2 + 1)
            nc.vector.tensor_tensor(ONT[:, g % 2, 0], o_ps, ONT[:, g % 2, 1], ALU.mult).then_inc(sem("out_kept"), 1)

        def keep_rec(act, m, g):
            act.wait_ge(sem("sums_turned"), m // 2 + 1)
            nc.scalar.activation(ONT[:, g % 2, 1], rec_ps, ACT.Copy).then_inc(sem("rec_kept"), 1)

        def project_out(pe, o, g, n, weights):
            pe.wait_ge(sem("out_kept"), o + 1)
            pe.wait_ge(sem("xT_ready"), n * GROUP + g)
            nc.tensor.matmul(y_ps, ONT[:, g % 2, 0], weights, start=True, stop=True).then_inc(sem("y_done"), 1)

        STEPS = 2 * GROUP + 6

        def attend_pe(pe, a, m0, o0, n, K, weights, extra=None, scored=False, probs="exps", probs0=0):
            for i in range(STEPS):
                if 2 <= i < UNITS + 2:
                    pe.wait_ge(sem(probs), probs0 + i - 1)
                    turn_probs(pe, m0 + i - 2, K, E[:, (i - 2) % 3])
                if i < UNITS and not scored:
                    scores(pe, a, i, K, extra)
                if 2 <= i < UNITS + 2:
                    if i % 2 == 0 and i > 2:
                        pe.wait_ge(sem("out_kept"), o0 + (i - 2) // 2)
                    values(pe, m0 + i - 2, i - 2, K)
                    if i % 2:
                        turn_sums(pe, o0 + (i - 3) // 2, (i - 3) // 2)
                if i >= 7 and i % 2:
                    turn_x(pe, n, (i - 7) // 2, X[:, (i - 7) // 2])
                if i >= 5 and i % 2 and (i - 5) // 2 < GROUP:
                    g = (i - 5) // 2
                    project_out(pe, o0 + g, g, n, weights)

        def attend_act(act, link, m0, n, K, exp):
            for i in range(STEPS):
                if i >= 4 and i % 2 == 0 and (i - 4) // 2 < GROUP:
                    keep_rec(act, m0 + i - 3, (i - 4) // 2)
                if 2 <= i < UNITS + 2:
                    keep_probs(act, m0 + i - 2, K)
                if i < UNITS:
                    exp(i)
                if i >= 7 and i % 2:
                    keep_xT(act, n, (i - 7) // 2)
                if i >= 6 and i % 2 == 0:
                    norm_rstd(act, link, n, (i - 6) // 2)

        def attend_dve(dve, link, m0, o0, n, K, res, unit, exp0=0):
            for i in range(STEPS):
                if i >= 4 and i % 2 == 0 and (i - 4) // 2 < GROUP:
                    normalise(dve, m0 + i - 3, (i - 4) // 2)
                if i < UNITS:
                    unit(i)
                if 1 <= i <= UNITS:
                    sum_unit(dve, link, i - 1, E[:, (i - 1) % 3], "exps", exp0 + i, K)
                if i >= 6 and i % 2 == 0:
                    g = (i - 6) // 2
                    dve.wait_ge(sem("y_done"), o0 + g + 1)
                    norm_stats(dve, link, n, g, y_ps, res)
                if i >= 7 and i % 2:
                    norm_apply(dve, n, (i - 7) // 2, Y[:, (i - 7) // 2], X[:, (i - 7) // 2])

        def project_ctx(pe, a, n, wq, wk, wv, bv=None):
            pe.wait_ge(sem("xT_ready"), (n + 1) * GROUP)
            nc.tensor.matmul(bank(0), wq, XT[:, :], start=True, stop=True).then_inc(sem("q_psum"), 1)
            nc.tensor.matmul(bank(1, GC), wk, CT[:, :], start=True, stop=True).then_inc(sem("k_psum"), 1)
            for g in range(GROUP):
                m = nc.tensor.matmul(PS[0:CTX, 2, g * 128:(g + 1) * 128], CT[:, g * CTX:(g + 1) * CTX], wv,
                                     start=True, stop=True)
            m.then_inc(sem("v_psum"), 1)
            pe.wait_ge(sem("q_kept"), a + 1)
            pe.wait_ge(sem("v_kept"), a + 1)

        def keep_qk(act, a, bq, bk):
            act.wait_ge(sem("k_psum"), a + 1)
            nc.scalar.activation(KT[:, 0, 0:GC], bank(1, GC), ACT.Identity, bias=bk).then_inc(sem("k_kept"), 1)
            nc.scalar.activation(QT[:, 0, :], bank(0), ACT.Identity, bias=bq).then_inc(sem("q_kept"), 1)

        def keep_v(dve, a, bv):
            dve.wait_ge(sem("v_psum"), a + 1)
            dve.wait_ge(sem("v_cleared"), a + 1 if a < 2 else 2)
            dst = v_spread(slice(0, CTX))
            for g in range(GROUP):
                src = PS[0:CTX, 2, g * 128:(g + 1) * 128].rearrange("p (s c d) -> p s c d", s=4, c=4)
                if bv is None:
                    m = nc.vector.tensor_copy(dst[:, g], src)
                else:
                    m = nc.vector.tensor_tensor(dst[:, g], src, bv[0:CTX].rearrange("p (s c d) -> p s c d", s=4, c=4),
                                                ALU.add)
            m.then_inc(sem("v_kept"), 1)

        def spread_all(pool, a, K, ready, count):
            pool.wait_ge(sem(ready), count)
            for g in range(GROUP):
                spread_keys(pool, a, g, K)

        def plain_exp(act, a, scale, base):
            def exp(u):
                act.wait_ge(sem("shifted"), a * UNITS + u + 1)
                nc.scalar.activation(E[:, u % 3], E[:, u % 3], ACT.Exp, scale=scale).then_inc(sem("exps"), 1)
            return exp

        def exp_unit(act, a, u, K, scale):
            act.wait_ge(sem("shifted"), a * UNITS + u + 1)
            nc.scalar.activation(E[:, u % 3, 0:HALF * K], E[:, u % 3, 0:HALF * K], ACT.Exp,
                                 scale=scale).then_inc(sem("exps"), 1)

        def clear_values(pool, lo, hi):
            nc.gpsimd.memset(flat_VS[:, lo:hi], 0.0).then_inc(sem("v_cleared"), 1)

        def shift_unit(dve, link, a, u, K, m0):
            if u >= 3:
                dve.wait_ge(sem("probs_turned"), m0 + u - 2)
            shift(dve, link, a, u, K, E[:, u % 3, 0:HALF * K])

        SCALE = DH ** -0.5

        LEVELS = 7
        powers = big2[:, 0:2048].rearrange("p (l g k) -> p l g k", l=2, g=GROUP)
        attT = small[:, GT:2 * GT]
        kmat = KT[0:64, 0, :]
        qmat = QT[0:64, 0, :]

        def l0a_pe(pe):
            pe.wait_ge(once("con_loaded"), 16)
            pe.wait_ge(once("w64_loaded"), 48)
            for g in range(GROUP):
                turn_x(pe, 0, g, ON[:, g, 0:128])
            pe.wait_ge(once("weights0"), 16)
            pe.wait_ge(sem("xT_ready"), GROUP)
            nc.tensor.matmul(PS[0:64, 0, :], w("l0a_wk"), XT[:, :], start=True, stop=True).then_inc(sem("l0a_kT"), 1)
            nc.tensor.matmul(PS[0:64, 1, :], w("l0a_wq"), XT[:, :], start=True, stop=True).then_inc(sem("l0a_qT"), 1)
            for g in range(GROUP):
                m = nc.tensor.matmul(PS[:, 2, g * 128:(g + 1) * 128], XT[:, g * 128:(g + 1) * 128], w("l0a_wv"),
                                     start=True, stop=True)
            m.then_inc(sem("l0a_v"), 1)
            pe.wait_ge(sem("l0a_k_kept"), 1)
            for g in range(GROUP):
                k = kmat[:, g * 128:(g + 1) * 128]
                m = nc.tensor.matmul(PS[:, 4, g * 128:(g + 1) * 128], k, k, start=True, stop=True)
            m.then_inc(sem("l0a_kk"), 1)
            pe.wait_ge(sem("l0a_q_kept"), 1)
            for g in range(GROUP):
                m = nc.tensor.matmul(PS[:, 5, g * 128:(g + 1) * 128], kmat[:, g * 128:(g + 1) * 128],
                                     qmat[:, g * 128:(g + 1) * 128], start=True, stop=True)
            m.then_inc(sem("l0a_kq"), 1)
            pe.wait_ge(sem("l0a_masked"), 3)
            pe.wait_ge(sem("l0a_u0"), 1)
            for l in range(LEVELS):
                for g in range(GROUP):
                    if l >= 1:
                        pe.wait_ge(sem("l0a_u"), (l - 1) * GROUP + g + 1)
                        pe.wait_ge(sem("l0a_powers"), (l - 1) * GROUP + g + 1)
                    p, pt = powers[:, l % 2, g, 0:128], powers[:, l % 2, g, 128:256]
                    nc.tensor.matmul(PS[:, 4 + g, 0:128], pt, VB[:, g, l % 2],
                                     start=True, stop=True).then_inc(sem("l0a_step"), 1)
                    if l < LEVELS - 1:
                        nc.tensor.matmul(PS[:, g, 0:128], pt, p, start=True, stop=True)
                        nc.tensor.matmul(PS[:, g, 128:256], p, pt, start=True, stop=True).then_inc(sem("l0a_level"), 1)
            for g in range(GROUP):
                pe.wait_ge(sem("l0a_u"), (LEVELS - 1) * GROUP + g + 1)
                nc.tensor.matmul(PS[:, g, 0:128], attT[:, g * 128:(g + 1) * 128],
                                 VB[:, g, LEVELS % 2], start=True, stop=True).then_inc(sem("l0a_y"), 1)
            norms_pe(pe, 1)

        def l0a_act(act, link):
            act.wait_ge(once("consts"), 2)
            act.wait_ge(once("weights0"), 16)
            act.wait_ge(once("w64_loaded"), 48)
            for g in range(GROUP + 1):
                if g < GROUP:
                    norm_rstd(act, link, 0, g)
                if g >= 1:
                    act.wait_ge(sem("xT_turned"), g)
                    nc.scalar.activation(XT[:, (g - 1) * 128:g * 128], xt_ps, ACT.Identity, scale=w("l0a_gamma"),
                                         bias=w("l0a_beta")).then_inc(sem("xT_ready"), 1)
            act.wait_ge(sem("l0a_kT"), 1)
            nc.scalar.activation(kmat, PS[0:64, 0, :], ACT.Identity, bias=h64("l0a_bk")).then_inc(sem("l0a_k_kept"), 1)
            act.wait_ge(sem("l0a_qT"), 1)
            nc.scalar.activation(qmat, PS[0:64, 1, :], ACT.Identity, bias=h64("l0a_bq")).then_inc(sem("l0a_q_kept"), 1)
            for l in range(LEVELS - 1):
                for g in range(GROUP):
                    act.wait_ge(sem("l0a_level"), l * GROUP + g + 1)
                    nc.scalar.activation(powers[:, (l + 1) % 2, g], PS[:, g, 0:256],
                                         ACT.Copy).then_inc(sem("l0a_powers"), 1)
            norms_act(act, link, 1)

        def l0a_dve(dve, link, i):
            dve.wait_ge(once("x_loaded"), 16)
            dve.wait_ge(once("row_loaded"), 16)
            dve.wait_ge(once("con_loaded"), 16)
            dve.wait_ge(once("consts"), 2)
            link(nc.vector.tensor_copy(X[:].rearrange("p g d -> p (g d)"), x_all[:, bass.ds(i * GT, GT)]))
            for g in range(GROUP):
                link(nc.vector.bn_stats(stats[:, g], X[:, g]))
                nc.vector.bn_aggr(mv[:, g], stats[:, g]).then_inc(sem("norm_var"), 1)
            for g in range(GROUP):
                norm_apply(dve, 0, g, X[:, g], ON[:, g, 0:128])
            dve.wait_ge(sem("l0a_v"), 1)
            link(nc.vector.tensor_tensor(VB[:, :, 1], PS[:, 2].rearrange("p (g d) -> p g d", g=GROUP),
                                         bc(r("l0a_bv"), 1, GROUP), ALU.add))
            nc.vector.tensor_scalar(VB[:, :, 0], VB[:, :, 1], TTT_LR, None, ALU.mult).then_inc(sem("l0a_u0"), 1)
            dve.wait_ge(sem("l0a_kk"), 1)
            kk = PS[:, 4].rearrange("p (g d) -> p g d", g=GROUP)
            nc.vector.tensor_tensor(powers[:, 0, :, 0:128], kk, bc(c("low"), 1, GROUP),
                                    ALU.mult).then_inc(sem("l0a_masked"), 1)
            nc.vector.tensor_tensor(powers[:, 0, :, 128:256], kk, bc(c("up"), 1, GROUP),
                                    ALU.mult).then_inc(sem("l0a_masked"), 1)
            dve.wait_ge(sem("l0a_kq"), 1)
            nc.vector.tensor_tensor(attT.rearrange("p (g d) -> p g d", g=GROUP),
                                    PS[:, 5].rearrange("p (g d) -> p g d", g=GROUP), bc(c("sup"), 1, GROUP),
                                    ALU.mult).then_inc(sem("l0a_masked"), 1)
            dve.wait_ge(sem("l0a_u0"), 1)
            for l in range(LEVELS):
                for g in range(GROUP):
                    dve.wait_ge(sem("l0a_step"), l * GROUP + g + 1)
                    if l >= 1:
                        dve.wait_ge(sem("l0a_u"), (l - 1) * GROUP + g + 1)
                    nc.vector.tensor_tensor(VB[:, g, (l + 1) % 2], VB[:, g, l % 2], PS[:, 4 + g, 0:128],
                                            ALU.add).then_inc(sem("l0a_u"), 1)
            dve.wait_ge(sem("l0a_doubled"), 1)
            norms_dve(dve, link, 1, "l0a_y", lambda g: PS[:, g, 0:128], XR)

        def l0a_pool(pool, i):
            pool.wait_ge(once("ctx_loaded"), 32)
            nc.gpsimd.tensor_copy(CT[:, :], ctx_all[:, bass.ds(i * GC, GC)]).then_inc(sem("ctx_ready"), 1)
            nc.gpsimd.tensor_copy(small[:, 0:GC], mask_u8[:, bass.ds(i * GC, GC)]).then_inc(sem("ctx_ready"), 1)
            pool.wait_ge(sem("ctx_ready"), 2)
            nc.gpsimd.tensor_scalar(mask_b[:], bc(small[:, 0:GC].rearrange("p (g k) -> p g k", g=GROUP), 2, 4),
                                    MASKED, None, ALU.mult).then_inc(sem("ctx_ready"), 1)
            pool.wait_ge(sem("norm_var"), GROUP)
            nc.gpsimd.tensor_scalar(XR[:], X[:], 2.0, None, ALU.mult).then_inc(sem("l0a_doubled"), 1)
            pool.wait_ge(sem("xT_ready"), GROUP)
            clear_values(pool, 0, GROUP * VW)

        def l0x_pe(pe):
            pe.wait_ge(sem("ctx_ready"), 3)
            pe.wait_ge(once("casts"), 3)
            project_ctx(pe, 0, 1, w("l0x_wq"), w("l0x_wk"), w("l0x_wv"))
            attend_pe(pe, 0, 0, 0, 2, CTX, w("l0x_wo"),
                      lambda g: (row0_bf[:, :], mask_b[:, g].rearrange("p h k -> p (h k)")))

        def l0x_act(act, link):
            keep_qk(act, 0, w("l0x_bq"), w("l0x_bk"))
            attend_act(act, link, 0, 2, CTX, lambda u: exp_unit(act, 0, u, CTX, SCALE))

        def l0x_dve(dve, link):
            dve.wait_ge(once("consts"), 2)
            keep_v(dve, 0, r("l0x_bv"))
            dve.wait_ge(sem("residual"), 1)
            attend_dve(dve, link, 0, 0, 2, CTX, XR, lambda u: shift_unit(dve, link, 0, u, CTX, 0))

        def l0x_pool(pool):
            add_bias(pool, 1, r("l0x_bo"))
            spread_all(pool, 0, CTX, "k_kept", 1)

        def ranks(dve, link, logits, M, n, tie, rank, t1, t2):
            other, own = bc(logits, 2, n), bc(logits, 3, n)
            link(nc.vector.tensor_tensor(t1, other, own, ALU.is_gt))
            link(nc.vector.tensor_tensor(t2, other, own, ALU.is_equal))
            link(nc.vector.tensor_tensor(t2, t2, bc(tie.rearrange("p (e f) -> p e f", e=n), 1, M), ALU.mult))
            link(nc.vector.tensor_tensor(t1, t1, t2, ALU.add))
            link(nc.vector.tensor_reduce(rank, t1, AX.X, ALU.add))

        EXPERTS = 8
        g8 = lambda k: small[:, 32 * k:32 * k + 32].rearrange("p (g e) -> p g e", g=GROUP)
        logits, shifted8, probs, rank8, weight, tmp8 = (g8(k) for k in range(6))
        route_max = small[:, 192:192 + GROUP]
        route_sum = small[:, 200:200 + GROUP]
        pair1 = small[:, 256:512].rearrange("p (g e f) -> p g e f", g=GROUP, e=8)
        pair2 = small[:, 512:768].rearrange("p (g e f) -> p g e f", g=GROUP, e=8)
        weightT = small[0:8, 768:768 + GT]

        def route_pe(pe, tag, n, wg, b2):
            pe.wait_ge(sem("xT_ready"), (n + 1) * GROUP)
            for g in range(GROUP):
                m = nc.tensor.matmul(PS[:, 6, g * 8:(g + 1) * 8], XT[:, g * 128:(g + 1) * 128], wg,
                                     start=True, stop=True)
            m.then_inc(sem(tag + "_logits"), 1)

        def route_bias_pe(pe, tag, b2):
            pe.wait_ge(sem(tag + "_weights"), 1)
            for g in range(GROUP):
                m = nc.tensor.transpose(PS[0:8, 6, g * 128:(g + 1) * 128], weight[:, g], ident)
            m.then_inc(sem(tag + "_wT"), 1)
            pe.wait_ge(sem(tag + "_wT_kept"), 1)
            for g in range(GROUP):
                m = nc.tensor.matmul(PS[:, 7, g * 128:(g + 1) * 128], weightT[:, g * 128:(g + 1) * 128], b2,
                                     start=True, stop=True)
            m.then_inc(sem(tag + "_bias"), 1)

        def route_dve(dve, link, tag, bias, combine):
            dve.wait_ge(sem(tag + "_logits"), 1)
            link(nc.vector.tensor_tensor(logits, PS[:, 6, 0:32].rearrange("p (g e) -> p g e", g=GROUP),
                                         bc(bias, 1, GROUP), ALU.add))
            link(nc.vector.tensor_reduce(route_max, logits, AX.X, ALU.max))
            nc.vector.tensor_tensor(shifted8, logits, bc(route_max, 2, EXPERTS),
                                    ALU.subtract).then_inc(sem(tag + "_shifted"), 1)
            ranks(dve, link, logits, GROUP, EXPERTS, c("tie8"), rank8, pair1, pair2)
            dve.wait_ge(sem(tag + "_exp"), 1)
            link(nc.vector.tensor_reduce(route_sum, probs, AX.X, ALU.add))
            link(nc.vector.reciprocal(route_sum, route_sum))
            link(nc.vector.tensor_tensor(probs, probs, bc(route_sum, 2, EXPERTS), ALU.mult))
            combine(link).then_inc(sem(tag + "_weights"), 1)

        def route_act(act, tag):
            act.wait_ge(sem(tag + "_shifted"), 1)
            nc.scalar.activation(probs, shifted8, ACT.Exp).then_inc(sem(tag + "_exp"), 1)
            act.wait_ge(sem(tag + "_wT"), 1)
            nc.scalar.activation(weightT, PS[0:8, 6, :], ACT.Copy).then_inc(sem(tag + "_wT_kept"), 1)

        def start_sum(dve, link, tag):
            dve.wait_ge(sem(tag + "_bias"), 1)
            link(nc.vector.tensor_tensor(Y[:], X[:], PS[:, 7].rearrange("p (g d) -> p g d", g=GROUP), ALU.add))

        def add_expert(dve, tag, down, e):
            dve.wait_ge(sem(down), e + 1)
            if e >= 1:
                dve.wait_ge(sem(tag + "_added"), e)
            for g in range(GROUP):
                m = nc.vector.scalar_tensor_tensor(Y[:, g], PS[:, 4 + e % 2, g * 128:(g + 1) * 128],
                                                   weight[:, g, e:e + 1], Y[:, g], ALU.mult, ALU.add)
            m.then_inc(sem(tag + "_added"), 1)

        def norms_of_sum(dve, link, n, summed):
            dve.wait_ge(sem(summed[0]), summed[1])
            for g in range(GROUP):
                link(nc.vector.bn_stats(stats[:, g], Y[:, g]))
                nc.vector.bn_aggr(mv[:, g], stats[:, g]).then_inc(sem("norm_var"), 1)
            for g in range(GROUP):
                norm_apply(dve, n, g, Y[:, g], X[:, g])

        TILES = 4
        hidden = big2.rearrange("p (i t) -> p i t", i=8)

        def l0f_pe(pe):
            route_pe(pe, "l0f", 2, w("l0f_wg"), None)

            pe.wait_ge(once("weights1"), 16)
            pe.wait_ge(once("weights2"), 16)

            def up(e):
                for t in range(TILES):
                    i = e * TILES + t
                    if i >= 4:
                        pe.wait_ge(sem("l0f_gelu"), i - 3)
                    nc.tensor.matmul(bank(i % 4), w("l0f_w1", e * 512 + t * 128, 128), XT[:, :],
                                     start=True, stop=True).then_inc(sem("l0f_up"), 1)

            def down(e):
                pe.wait_ge(sem("l0f_gelu"), (e + 1) * TILES)
                if e >= 2:
                    pe.wait_ge(sem("l0f_added"), e - 1)
                for g in range(GROUP):
                    for t in range(TILES):
                        m = nc.tensor.matmul(PS[:, 4 + e % 2, g * 128:(g + 1) * 128],
                                             hidden[:, (e * TILES + t) % 8, g * 128:(g + 1) * 128],
                                             w("l0f_w2", e * 512 + t * 128, 128), start=t == 0, stop=t == TILES - 1)
                m.then_inc(sem("l0f_down"), 1)

            up(0)
            route_bias_pe(pe, "l0f", w8[:, 0:128])
            for e in range(EXPERTS):
                if e + 1 < EXPERTS:
                    up(e + 1)
                down(e)
            norms_pe(pe, 3)

        def l0f_act(act, link):
            route_act(act, "l0f")
            act.preload_act_table_set("gelu_and_others")
            for i in range(EXPERTS * TILES):
                act.wait_ge(sem("l0f_up"), i + 1)
                if i >= 8:
                    act.wait_ge(sem("l0f_down"), i // TILES - 1)
                nc.scalar.activation(hidden[:, i % 8], bank(i % 4), ACT.Gelu,
                                     bias=w("l0f_b1", i, 1)).then_inc(sem("l0f_gelu"), 1)
            act.preload_act_table_set("natural_log_exp_and_others")
            norms_act(act, link, 3)

        def l0f_dve(dve, link):
            route_dve(dve, link, "l0f", r("l0f_bg"), lambda link: nc.vector.scalar_tensor_tensor(
                weight, rank8, 2.0, probs, ALU.is_lt, ALU.mult))
            start_sum(dve, link, "l0f")
            for e in range(EXPERTS):
                add_expert(dve, "l0f", "l0f_down", e)
            norms_of_sum(dve, link, 3, ("l0f_added", EXPERTS))

        def l0f_pool(pool):
            pass

        GH, GK, GV = 4, 32, 64
        gate_abs = E[:, 0, 0:GT]
        gate_min = E[:, 1, 0:GT]
        gate = E[:, 2, 0:GT]
        run_sum = E2[:, 1, 0:GT]
        low_rank = E2[0:16, 0, 0:GT]
        exp_b, exp_nb = gate_abs, gate_min
        tail_b = PT[:, 0, 0:GROUP * CHUNK].rearrange("p (g t) -> p g t", g=GROUP)
        k_carry = small[:, 0:GT].rearrange("p (g c t) -> p g c t", g=GROUP, c=2)
        gla_v = VB[:, :, 0:2]
        gla_g = VB[:, :, 2:4]
        rms = small[:, 600:600 + 4 * GROUP].rearrange("p (g h) -> p g h", g=GROUP)

        def wide(b):
            return PS[:, b:b + 2, :].rearrange("p b (g d) -> p (b g) d", g=2)

        def l1a_pe(pe):
            pe.wait_ge(once("weights3"), 16)
            pe.wait_ge(sem("xT_ready"), 4 * GROUP)
            nc.tensor.matmul(PS[0:16, 2, :], w("l1a_w1"), XT[:, :], start=True, stop=True).then_inc(sem("l1a_low"), 1)
            nc.tensor.matmul(bank(0), w("l1a_wq"), XT[:, :], start=True, stop=True)
            nc.tensor.matmul(bank(1), w("l1a_wk"), XT[:, :], start=True, stop=True).then_inc(sem("l1a_qk"), 1)
            pe.wait_ge(sem("l1a_low_kept"), 1)
            nc.tensor.matmul(bank(3), w16[:, :], low_rank, start=True, stop=True).then_inc(sem("l1a_z"), 1)
            for b, name, s in ((4, "l1a_wv", "l1a_v"), (6, "l1a_wg", "l1a_g")):
                for g in range(GROUP):
                    m = nc.tensor.matmul(wide(b)[:, g], XT[:, g * 128:(g + 1) * 128], w(name), start=True, stop=True)
                m.then_inc(sem(s), 1)
            pe.wait_ge(sem("l1a_v_kept"), 1)
            pe.wait_ge(sem("l1a_gated"), 1)
            pe.wait_ge(sem("l1a_keys"), 3)
            for i in range(GROUP + 3):
                if i < GROUP:
                    pe.wait_ge(sem("l1a_spread"), i + 1)
                    if i >= 2:
                        pe.wait_ge(sem("l1a_masked"), i - 1)
                    kb = KB[:, i % 2].rearrange("p h k -> p (h k)")
                    nc.tensor.matmul(PS[:, i % 2, 0:256], KT[:, 0, i * 128:(i + 1) * 128], kb[:, 0:256],
                                     start=True, stop=True)
                    nc.tensor.matmul(PS[:, i % 2, 256:512], k_carry[:, i], kb[:, 256:512],
                                     start=True, stop=True).then_inc(sem("l1a_scores"), 1)
                if i >= 3:
                    turn_x(pe, 4, i - 3, X[:, i - 3])
                if 1 <= i <= GROUP:
                    g = i - 1
                    pe.wait_ge(sem("l1a_masked"), g + 1)
                    if g >= 2:
                        pe.wait_ge(sem("attended"), O_L1A + g - 1)
                    at = E2[:, g % 2, 0:512].rearrange("p (h t) -> p h t", h=GH)
                    for h in range(GH):
                        m = nc.tensor.matmul(PS[:, 2 + g % 2, h * GV:(h + 1) * GV], at[:, h],
                                             VB[:, g, h // 2, (h % 2) * GV:(h % 2) * GV + GV], start=True, stop=True)
                    m.then_inc(sem("l1a_o"), 1)
                if 2 <= i <= GROUP + 1:
                    g = i - 2
                    pe.wait_ge(sem("attended"), O_L1A + g + 1)
                    for k in range(2):
                        m = nc.tensor.transpose(PS[:, 4 + g % 2, 128 * k:128 * k + 128],
                                                ON[:, g, 128 * k:128 * k + 128], ident)
                    m.then_inc(sem("out_turned"), 1)
                    pe.wait_ge(sem("out_kept"), O_L1A + g + 1)
                    if g >= 1:
                        pe.wait_ge(sem("x_ready"), 4 * GROUP + g)
                    for k in range(2):
                        m = nc.tensor.matmul(PS[:, 6, 0:128], ONT[:, g % 2, k], w("l1a_wo", 128 * k, 128),
                                             start=k == 0, stop=k == 1)
                    m.then_inc(sem("y_done"), 1)

        def l1a_act(act, link):
            act.wait_ge(once("weights3"), 16)
            act.wait_ge(sem("l1a_low"), 1)
            nc.scalar.activation(low_rank, PS[0:16, 2, :], ACT.Copy).then_inc(sem("l1a_low_kept"), 1)
            act.wait_ge(sem("l1a_z"), 1)
            nc.scalar.activation(gate_abs, bank(3), ACT.Abs, bias=w("l1a_b2")).then_inc(sem("l1a_abs"), 1)
            act.wait_ge(sem("l1a_abs"), 1)
            link(nc.scalar.activation(gate_abs, gate_abs, ACT.Exp, scale=-1.0))
            nc.scalar.activation(gate_abs, gate_abs, ACT.Ln, bias=one_col[:, 0:1]).then_inc(sem("l1a_softplus"), 1)
            act.wait_ge(sem("l1a_v"), 1)
            nc.scalar.activation(gla_v.rearrange("p g c d -> p g (c d)"), wide(4), ACT.Copy).then_inc(sem("l1a_v_kept"), 1)
            act.wait_ge(sem("l1a_g"), 1)
            nc.scalar.activation(gla_g.rearrange("p g c d -> p g (c d)"), wide(6), ACT.Exp,
                                 scale=-1.0).then_inc(sem("l1a_expg"), 1)
            act.wait_ge(sem("l1a_run"), 1)
            nc.scalar.activation(exp_b, run_sum, ACT.Exp, scale=1.0 / GATE_NORM).then_inc(sem("l1a_expb"), 1)
            nc.scalar.activation(exp_nb, run_sum, ACT.Exp, scale=-1.0 / GATE_NORM).then_inc(sem("l1a_expb"), 1)
            act.wait_ge(sem("l1a_tail"), 1)
            nc.scalar.activation(tail_b, tail_b, ACT.Exp, scale=1.0 / GATE_NORM).then_inc(sem("l1a_expb"), 1)
            for i in range(GROUP + 3):
                if i >= 3:
                    keep_xT(act, 4, i - 3)
                if 1 <= i <= GROUP:
                    g = i - 1
                    act.wait_ge(sem("l1a_o"), g + 1)
                    nc.scalar.activation(PT[:, g % 2, 0:256], PS[:, 2 + g % 2, 0:256],
                                         ACT.Square).then_inc(sem("l1a_square"), 1)
                    act.wait_ge(sem("l1a_ms"), g + 1)
                    link(nc.scalar.activation(rms[:, g], rms[:, g], ACT.Ln, bias=eps_col[:, 0:1], scale=1.0 / GV))
                    nc.scalar.activation(rms[:, g], rms[:, g], ACT.Exp, scale=-0.5).then_inc(sem("l1a_rms"), 1)
                if 2 <= i <= GROUP + 1:
                    g = i - 2
                    act.wait_ge(sem("out_turned"), g + 1)
                    nc.scalar.activation(ONT[:, g % 2].rearrange("p k t -> p (k t)"), PS[:, 4 + g % 2, 0:256],
                                         ACT.Copy).then_inc(sem("out_kept"), 1)
                    norm_rstd(act, link, 4, g)

        def l1a_dve(dve, link):
            dve.wait_ge(once("weights3"), 16)
            dve.wait_ge(sem("l1a_abs"), 1)
            nc.vector.tensor_scalar(gate_min, bank(3), w("l1a_b2"), 0.0, ALU.add, ALU.min).then_inc(sem("l1a_min"), 1)
            dve.wait_ge(sem("l1a_softplus"), 1)
            dve.wait_ge(sem("l1a_min"), 1)
            link(nc.vector.tensor_tensor(gate, gate_min, gate_abs, ALU.subtract))
            nc.vector.tensor_tensor_scan(run_sum, c("scan"), gate, 0.0, ALU.mult, ALU.add).then_inc(sem("l1a_run"), 1)
            dve.wait_ge(sem("l1a_run"), 1)
            b0 = run_sum.rearrange("p (g c t) -> p g c t", g=GROUP, c=2)[:, :, 0]
            nc.vector.tensor_tensor(tail_b, b0[:, :, CHUNK - 1:CHUNK].to_broadcast([128, GROUP, CHUNK]), b0,
                                    ALU.subtract).then_inc(sem("l1a_tail"), 1)
            dve.wait_ge(sem("l1a_expg"), 1)
            gg = gla_g.rearrange("p g c d -> p g (c d)")
            link(nc.vector.tensor_scalar(gg, gg, 1.0, None, ALU.add))
            link(nc.vector.reciprocal(gg, gg))
            link(nc.vector.tensor_tensor(gg, gg, wide(6), ALU.mult))
            g4 = gg.rearrange("p g (h d) -> p g h d", h=GH)
            for g in range(GROUP):
                m = nc.vector.tensor_tensor(g4[:, g], g4[:, g], bc(r("l1a_gn"), 1, GH), ALU.mult)
            m.then_inc(sem("l1a_gated"), 1)
            dve.wait_ge(sem("l1a_qk"), 1)
            dve.wait_ge(sem("l1a_expb"), 3)
            nc.vector.scalar_tensor_tensor(QT[:, 0], bank(0), GK ** -0.5, exp_b,
                                           ALU.mult, ALU.mult).then_inc(sem("l1a_keys"), 1)
            nc.vector.tensor_tensor(KT[:, 0], bank(1), exp_nb, ALU.mult).then_inc(sem("l1a_keys"), 1)
            kk = bank(1).rearrange("p (g c t) -> p g c t", g=GROUP, c=2)
            link(nc.vector.tensor_tensor(k_carry[:, :, 0], kk[:, :, 0], tail_b, ALU.mult))
            dve.wait_ge(sem("l1a_keys"), 2)
            nc.vector.tensor_copy(k_carry[:, :, 1], KT[:, 0].rearrange("p (g c t) -> p g c t", g=GROUP, c=2)[:, :, 1]
                                  ).then_inc(sem("l1a_keys"), 1)
            dve.wait_ge(sem("l1a_gated"), 1)
            for i in range(GROUP + 3):
                if i < GROUP:
                    dve.wait_ge(sem("l1a_scores"), i + 1)
                    if i >= 2:
                        dve.wait_ge(sem("l1a_o"), i - 1)
                    mask = bc(c("incl").rearrange("p (c t) -> p c t", c=2), 2, GH)
                    nc.vector.tensor_tensor(E2[:, i % 2, 0:512].rearrange("p (h c t) -> p c h t", c=2, h=GH),
                                            bank(i % 2).rearrange("p (c h t) -> p c h t", c=2, h=GH), mask,
                                            ALU.mult).then_inc(sem("l1a_masked"), 1)
                if i >= 3:
                    norm_apply(dve, 4, i - 3, Y[:, i - 3], X[:, i - 3])
                if 1 <= i <= GROUP:
                    g = i - 1
                    dve.wait_ge(sem("l1a_square"), g + 1)
                    nc.vector.tensor_reduce(rms[:, g], PT[:, g % 2, 0:256].rearrange("p (h d) -> p h d", h=GH),
                                            AX.X, ALU.add).then_inc(sem("l1a_ms"), 1)
                    dve.wait_ge(sem("l1a_rms"), g + 1)
                    o4 = ON[:, g].rearrange("p (h d) -> p h d", h=GH)
                    link(nc.vector.tensor_tensor(o4, PS[:, 2 + g % 2, 0:256].rearrange("p (h d) -> p h d", h=GH),
                                                 bc(rms[:, g], 2, GV), ALU.mult))
                    nc.vector.tensor_tensor(ON[:, g], ON[:, g], gg[:, g], ALU.mult).then_inc(sem("attended"), 1)
                if 2 <= i <= GROUP + 1:
                    g = i - 2
                    dve.wait_ge(sem("y_done"), O_L1A + g + 1)
                    norm_stats(dve, link, 4, g, PS[:, 6, 0:128], X)

        def l1a_pool(pool):
            pool.wait_ge(sem("l1a_keys"), 3)
            for g in range(GROUP):
                if g >= 2:
                    pool.wait_ge(sem("l1a_scores"), g - 1)
                q = QT[:, 0, g * 128:(g + 1) * 128].rearrange("p (c t) -> p c t", c=2)
                for ch in range(2):
                    m = nc.gpsimd.tensor_tensor(
                        KB[:, g % 2].rearrange("p h k -> p (h k)")[:, 256 * ch:256 * ch + 256].rearrange(
                            "p (h t) -> p h t", h=GH),
                        bc(q[:, ch], 1, GH), bc(c("hm4"), 2, CHUNK), ALU.mult)
                m.then_inc(sem("l1a_spread"), 1)

        O_L1A = GROUP

        NH = GROUP * HEADS
        LOG_T_MIN, LOG_T_MAX = float(np.log(0.1)), float(np.log(10.0))
        flat_mx = mx[:].rearrange("p u h -> p (u h)")
        sum1, sum2, feat_max, feat_var, feat_mean, half_t = (small[:, NH * k:NH * k + NH] for k in range(6))
        q_sum = small[:, 400:400 + GROUP]
        k_sum = small[:, 408:408 + GROUP]
        mlp1, mlp2 = small[0:64, 420:420 + NH], small[0:64, 484:484 + NH]

        def l1x_pe(pe):
            project_ctx(pe, 1, 4, w("l1x_wq"), w("l1x_wk"), w("l1x_wv"))
            for u in range(UNITS):
                scores(pe, 1, u, CTX)
            pe.wait_ge(sem("l1x_feats"), 3)
            pe.wait_ge(once("casts"), 5)
            feats = (feat_mean, feat_max, feat_var)
            for j in range(3):
                m = nc.tensor.matmul(PS[0:64, 3, 0:NH], r("l1x_w1", 64 * j, 64), feats[j], start=j == 0, stop=j == 2)
            m.then_inc(sem("l1x_mlp"), 1)
            pe.wait_ge(sem("l1x_gelu"), 1)
            nc.tensor.matmul(PS[0:64, 2, 0:NH], h64("l1x_w2"), mlp1, start=True, stop=True).then_inc(sem("l1x_mlp"), 1)
            pe.wait_ge(sem("l1x_gelu"), 2)
            nc.tensor.matmul(PS[:, 3, 0:NH], w3_rep[:, :], mlp2, start=True, stop=True).then_inc(sem("l1x_mlp"), 1)
            attend_pe(pe, 1, UNITS, 2 * GROUP, 5, CTX, w("l1x_wo"), scored=True, probs0=UNITS)

        def l1x_act(act, link):
            keep_qk(act, 1, w("l1x_bq"), w("l1x_bk"))

            def square(v):
                act.wait_ge(sem("l1x_exp"), v + 1)
                if v >= 2:
                    act.wait_ge(sem("l1x_sums"), v - 1)
                nc.scalar.activation(E2[:, v % 2, 0:HALF * CTX], E[:, v % 3, 0:HALF * CTX],
                                     ACT.Square).then_inc(sem("l1x_square"), 1)

            for u in range(UNITS):
                act.wait_ge(sem("shifted"), UNITS + u + 1)
                if u >= 3:
                    act.wait_ge(sem("l1x_sums"), u - 2)
                nc.scalar.activation(E[:, u % 3, 0:HALF * CTX], big[:, u], ACT.Exp,
                                     scale=SCALE).then_inc(sem("l1x_exp"), 1)
                if u >= 1:
                    square(u - 1)
            square(UNITS - 1)
            act.preload_act_table_set("gelu_and_others")
            act.wait_ge(sem("l1x_mlp"), 1)
            nc.scalar.activation(mlp1, PS[0:64, 3, 0:NH], ACT.Gelu, bias=h64("l1x_b1")).then_inc(sem("l1x_gelu"), 1)
            act.wait_ge(sem("l1x_mlp"), 2)
            nc.scalar.activation(mlp2, PS[0:64, 2, 0:NH], ACT.Gelu, bias=h64("l1x_b2")).then_inc(sem("l1x_gelu"), 1)
            act.preload_act_table_set("natural_log_exp_and_others")
            act.wait_ge(sem("l1x_logt"), 1)
            nc.scalar.activation(half_t, half_t, ACT.Exp, scale=-1.0).then_inc(sem("l1x_t"), 1)

            def exp(u):
                act.wait_ge(sem("l1x_scaled"), u + 1)
                nc.scalar.activation(E[:, u % 3, 0:HALF * CTX], E[:, u % 3, 0:HALF * CTX], ACT.Exp,
                                     scale=0.5).then_inc(sem("exps"), 1)

            attend_act(act, link, UNITS, 5, CTX, exp)

        def l1x_dve(dve, link):
            keep_v(dve, 1, r("l1x_bv"))

            def sums(u):
                dve.wait_ge(sem("l1x_exp"), u + 1)
                nc.vector.tensor_reduce(sum1[:, u * HALF:(u + 1) * HALF], E[:, u % 3, 0:HALF * CTX].rearrange(
                    "p (h k) -> p h k", h=HALF), AX.X, ALU.add)
                dve.wait_ge(sem("l1x_square"), u + 1)
                nc.vector.tensor_reduce(sum2[:, u * HALF:(u + 1) * HALF], E2[:, u % 2, 0:HALF * CTX].rearrange(
                    "p (h k) -> p h k", h=HALF), AX.X, ALU.add).then_inc(sem("l1x_sums"), 1)

            for u in range(UNITS + 2):
                if u < UNITS:
                    shift(dve, link, 1, u, CTX, big[:, u])
                if u >= 2:
                    sums(u - 2)
            nc.vector.tensor_scalar(feat_max, flat_mx, SCALE / TOK, None, ALU.mult).then_inc(sem("l1x_feats"), 1)
            dve.wait_ge(sem("l1x_sums"), UNITS)
            link(nc.vector.reciprocal(sum1, sum1))
            link(nc.vector.tensor_tensor(sum2, sum2, sum1, ALU.mult))
            link(nc.vector.tensor_tensor(sum2, sum2, sum1, ALU.mult))
            nc.vector.tensor_scalar(feat_var, sum2, -1.0 / CTX, 1.0 / ((CTX - 1) * TOK), ALU.add,
                                    ALU.mult).then_inc(sem("l1x_feats"), 1)
            dve.wait_ge(sem("q_kept"), 2)
            link(nc.vector.tensor_reduce(q_sum, QT[:, 0].rearrange("p (g t) -> p g t", g=GROUP), AX.X, ALU.add))
            link(nc.vector.tensor_reduce(k_sum, KT[:, 0, 0:GC].rearrange("p (g k) -> p g k", g=GROUP), AX.X, ALU.add))
            link(nc.vector.scalar_tensor_tensor(q_sum, q_sum, SCALE / (TOK * CTX), k_sum, ALU.mult, ALU.mult))
            nc.vector.tensor_tensor(feat_mean.rearrange("p (g h) -> p g h", g=GROUP), bc(q_sum, 2, HEADS),
                                    bc(c("hm16"), 1, GROUP), ALU.mult).then_inc(sem("l1x_feats"), 1)
            dve.wait_ge(sem("l1x_mlp"), 3)
            link(nc.vector.tensor_scalar(half_t, PS[:, 3, 0:NH], r("l1x_b3"), LOG_T_MIN, ALU.add, ALU.max))
            nc.vector.tensor_scalar(half_t, half_t, LOG_T_MAX, None, ALU.min).then_inc(sem("l1x_logt"), 1)
            dve.wait_ge(sem("l1x_t"), 1)
            dve.wait_ge(sem("residual"), 2)

            def scaled(u):
                if u >= 3:
                    dve.wait_ge(sem("probs_turned"), UNITS + u - 2)
                nc.vector.tensor_tensor(E[:, u % 3, 0:HALF * CTX].rearrange("p (h k) -> p h k", h=HALF),
                                        big[:, u].rearrange("p (h k) -> p h k", h=HALF),
                                        bc(half_t[:, u * HALF:(u + 1) * HALF], 2, CTX),
                                        ALU.mult).then_inc(sem("l1x_scaled"), 1)

            attend_dve(dve, link, UNITS, 2 * GROUP, 5, CTX, XR, scaled, UNITS)

        def l1x_pool(pool):
            add_bias(pool, 4, r("l1x_bo"))
            clear_values(pool, 0, GROUP * 256)
            pool.wait_ge(sem("k_kept"), 2)
            for g in range(GROUP):
                spread_keys(pool, 1, g, CTX)

        first_h = [big2[:, 512 * k:512 * k + 512] for k in range(2)]
        second_h = [big2[:, 1024 + 512 * k:1536 + 512 * k] for k in range(2)]

        def l1f_pe(pe):
            route_pe(pe, "l1f", 5, w("l1f_wg"), None)
            for i in range(EXPERTS + 2):
                if i < EXPERTS:
                    if i >= 2:
                        pe.wait_ge(sem("l1f_relu1"), i - 1)
                    nc.tensor.matmul(bank(i % 2), w("l1f_w1", 128 * i, 128), XT[:, :],
                                     start=True, stop=True).then_inc(sem("l1f_up1"), 1)
                if 1 <= i <= EXPERTS:
                    j = i - 1
                    pe.wait_ge(sem("l1f_relu1"), j + 1)
                    if j >= 2:
                        pe.wait_ge(sem("l1f_relu2"), j - 1)
                    nc.tensor.matmul(bank(2 + j % 2), w("l1f_w2", 128 * j, 128), first_h[j % 2],
                                     start=True, stop=True).then_inc(sem("l1f_up2"), 1)
                if i >= 2:
                    j = i - 2
                    pe.wait_ge(sem("l1f_relu2"), j + 1)
                    if j >= 2:
                        pe.wait_ge(sem("l1f_added"), j - 1)
                    for g in range(GROUP):
                        m = nc.tensor.matmul(PS[:, 4 + j % 2, g * 128:(g + 1) * 128],
                                             second_h[j % 2][:, g * 128:(g + 1) * 128], w("l1f_w3", 128 * j, 128),
                                             start=True, stop=True)
                    m.then_inc(sem("l1f_down"), 1)
                if i == 1:
                    route_bias_pe(pe, "l1f", w8[:, 128:256])
            norms_pe(pe, 6)

        def l1f_act(act, link):
            for i in range(EXPERTS):
                act.wait_ge(sem("l1f_up1"), i + 1)
                if i >= 2:
                    act.wait_ge(sem("l1f_up2"), i - 1)
                nc.scalar.activation(first_h[i % 2], bank(i % 2), ACT.Relu,
                                     bias=w("l1f_b1", i, 1)).then_inc(sem("l1f_relu1"), 1)
                if i == 0:
                    route_act(act, "l1f")
                if i >= 1:
                    relu2(act, i - 1)
            relu2(act, EXPERTS - 1)
            norms_act(act, link, 6)

        def relu2(act, j):
            act.wait_ge(sem("l1f_up2"), j + 1)
            if j >= 2:
                act.wait_ge(sem("l1f_down"), j - 1)
            nc.scalar.activation(second_h[j % 2], bank(2 + j % 2), ACT.Relu,
                                 bias=w("l1f_b2", j, 1)).then_inc(sem("l1f_relu2"), 1)

        def l1f_dve(dve, link):
            def combine(link):
                link(nc.vector.scalar_tensor_tensor(tmp8, rank8, 0.0, probs[:, :, 0:1].to_broadcast([128, GROUP, 8]),
                                                    ALU.is_equal, ALU.mult))
                link(nc.vector.scalar_tensor_tensor(weight, rank8, 1.0, probs[:, :, 1:2].to_broadcast([128, GROUP, 8]),
                                                    ALU.is_equal, ALU.mult))
                return nc.vector.tensor_tensor(weight, weight, tmp8, ALU.add)

            route_dve(dve, link, "l1f", r("l1f_bg"), combine)
            start_sum(dve, link, "l1f")
            for e in range(EXPERTS):
                add_expert(dve, "l1f", "l1f_down", e)
            norms_of_sum(dve, link, 6, ("l1f_added", EXPERTS))

        def l1f_pool(pool):
            pass

        rot = [E[:, 0, 0:GT], E[:, 1, 0:GT], E[:, 2, 0:GT], E2[:, 0, 0:GT]]

        def l2a_pe(pe):
            pe.wait_ge(once("weights4"), 16)
            pe.wait_ge(sem("xT_ready"), 7 * GROUP)
            for b, name in enumerate(("l2a_wk", "l2a_wks", "l2a_wq", "l2a_wqs")):
                nc.tensor.matmul(bank(b), w(name), XT[:, :], start=True, stop=True).then_inc(sem("l2a_qk"), 1)
            for g in range(GROUP):
                m = nc.tensor.matmul(PS[:, 4, g * 128:(g + 1) * 128], XT[:, g * 128:(g + 1) * 128], w("l2a_wv"),
                                     start=True, stop=True)
            m.then_inc(sem("l2a_v"), 1)
            pe.wait_ge(sem("l2a_rotated"), 4)
            pe.wait_ge(sem("l2a_q"), 1)
            pe.wait_ge(sem("l2a_v_kept"), 1)
            causal = causal_bf[:].rearrange("p h k -> p (h k)")
            attend_pe(pe, 2, 2 * UNITS, 3 * GROUP, 7, TOK, w("l2a_wo"), lambda g: (ident_bf[:, :], causal),
                      probs0=2 * UNITS)

        def l2a_act(act, link):
            act.wait_ge(sem("l2a_v"), 1)
            for g in range(GROUP):
                m = nc.scalar.activation(v_spread(slice(0, 128))[:, g], PS[:, 4, g * 128:(g + 1) * 128].rearrange(
                    "p (s c d) -> p s c d", s=4, c=4), ACT.Copy)
            m.then_inc(sem("l2a_v_kept"), 1)
            attend_act(act, link, 2 * UNITS, 7, TOK, lambda u: exp_unit(act, 2, u, TOK, SCALE))

        def l2a_dve(dve, link):
            for b in range(4):
                dve.wait_ge(sem("l2a_qk"), b + 1)
                nc.vector.tensor_tensor(rot[b].rearrange("p (g t) -> p g t", g=GROUP),
                                        bank(b).rearrange("p (g t) -> p g t", g=GROUP),
                                        bc(c("sin" if b % 2 else "cos"), 1, GROUP),
                                        ALU.mult).then_inc(sem("l2a_rotated"), 1)
            dve.wait_ge(sem("l2a_q"), 1)
            dve.wait_ge(sem("residual"), 3)
            attend_dve(dve, link, 2 * UNITS, 3 * GROUP, 7, TOK, XR, lambda u: shift_unit(dve, link, 2, u, TOK, 2 * UNITS),
                       2 * UNITS)

        def l2a_pool(pool):
            pool.wait_ge(sem("l2a_rotated"), 2)
            nc.gpsimd.tensor_tensor(KT[:, 0], rot[0], rot[1], ALU.add).then_inc(sem("l2a_k"), 1)
            pool.wait_ge(sem("l2a_k"), 1)
            spread_keys(pool, 2, 0, TOK)
            pool.wait_ge(sem("l2a_rotated"), 4)
            nc.gpsimd.tensor_tensor(QT[:, 0], rot[2], rot[3], ALU.add).then_inc(sem("l2a_q"), 1)
            spread_keys(pool, 2, 1, TOK)
            add_bias(pool, 6, r("l2a_bo"))
            for g in range(2, GROUP):
                spread_keys(pool, 2, g, TOK)

        gate_hm = small[0:16, 0:NH].rearrange("p (g h) -> p g h", g=GROUP)
        gate_mean, gate_top = small[0:16, 64:64 + GROUP], small[0:16, 72:72 + GROUP]
        gates = small[:, 128:128 + NH]
        scale1 = small[:, 192:192 + NH]
        mx2 = small[:, 256:256 + NH]
        share1 = small[:, 320:320 + NH]
        share2 = small[:, 384:384 + NH]
        X_STEPS = STEPS + 1
        U2 = 3 * UNITS

        def l2x_pe(pe):
            pe.wait_ge(sem("xT_ready"), 8 * GROUP)
            nc.tensor.matmul(PS[0:16, 3, 0:GC], w("l2x_wla"), CT[:, :], start=True, stop=True).then_inc(sem("l2x_la"), 1)
            project_ctx(pe, 2, 7, w("l2x_wq"), w("l2x_wk"), w("l2x_wv"))
            pe.wait_ge(sem("l2x_gate"), 1)
            nc.tensor.matmul(PS[:, 6, 0:NH], c("ones")[0:16], gate_hm.rearrange("p g h -> p (g h)"),
                             start=True, stop=True).then_inc(sem("l2x_gates"), 1)
            pe.wait_ge(sem("l2x_gates_kept"), 1)
            for i in range(X_STEPS):
                if 3 <= i < UNITS + 3:
                    pe.wait_ge(sem("l2x_mixed"), i - 2)
                    turn_probs(pe, U2 + i - 3, CTX, E[:, (i - 3) % 3])
                if i < UNITS:
                    scores(pe, 3, i, CTX)
                if 3 <= i < UNITS + 3:
                    if i % 2 and i > 3:
                        pe.wait_ge(sem("out_kept"), 4 * GROUP + (i - 3) // 2)
                    values(pe, U2 + i - 3, i - 3, CTX)
                if i >= 8 and i % 2 == 0:
                    turn_x(pe, 8, (i - 8) // 2, X[:, (i - 8) // 2])
                if i >= 6 and i % 2 == 0 and (i - 6) // 2 < GROUP:
                    g = (i - 6) // 2
                    project_out(pe, 4 * GROUP + g, g, 8, w("l2x_wo"))

        def l2x_act(act, link):
            act.wait_ge(sem("k_psum"), 3)
            nc.scalar.activation(KT[:, 0, 0:GC], bank(1, GC), ACT.Copy).then_inc(sem("k_kept"), 1)
            nc.scalar.activation(QT[:, 0, :], bank(0), ACT.Copy).then_inc(sem("q_kept"), 1)
            for i in range(X_STEPS):
                if 3 <= i < UNITS + 3:
                    keep_probs(act, U2 + i - 3, CTX)
                if 1 <= i < UNITS + 1:
                    u = i - 1
                    act.wait_ge(sem("l2x_shifted2"), u + 1)
                    nc.scalar.activation(E2[:, u % 2, 0:HALF * CTX], E2[:, u % 2, 0:HALF * CTX],
                                         ACT.Exp).then_inc(sem("l2x_exps2"), 1)
                if i < UNITS:
                    act.wait_ge(sem("shifted"), 3 * UNITS + i + 1)
                    nc.scalar.activation(E[:, i % 3, 0:HALF * CTX], E[:, i % 3, 0:HALF * CTX], ACT.Exp,
                                         scale=SCALE).then_inc(sem("exps"), 1)
                if i >= 8 and i % 2 == 0:
                    keep_xT(act, 8, (i - 8) // 2)
                if i >= 7 and i % 2:
                    norm_rstd(act, link, 8, (i - 7) // 2)

        def l2x_dve(dve, link):
            keep_v(dve, 2, None)
            dve.wait_ge(sem("l2x_la"), 1)
            la = PS[0:16, 3, 0:GC].rearrange("p (g k) -> p g k", g=GROUP)
            link(nc.vector.tensor_reduce(gate_mean, la, AX.X, ALU.add))
            link(nc.vector.tensor_reduce(gate_top, la, AX.X, ALU.max))
            link(nc.vector.tensor_scalar(gate_mean, gate_mean, 0.5 / CTX, None, ALU.mult))
            link(nc.vector.scalar_tensor_tensor(gate_mean, gate_top, 0.5, gate_mean, ALU.mult, ALU.add))
            nc.vector.tensor_tensor(gate_hm, bc(gate_mean, 2, HEADS), bc(ident[0:16, 0:16], 1, GROUP),
                                    ALU.mult).then_inc(sem("l2x_gate"), 1)
            dve.wait_ge(sem("l2x_gates"), 1)
            nc.vector.tensor_copy(gates, PS[:, 6, 0:NH]).then_inc(sem("l2x_gates_kept"), 1)
            dve.wait_ge(sem("l2x_gates_kept"), 1)
            dve.wait_ge(sem("residual"), 4)

            def of_unit(row, u):
                return row[:, u * HALF:(u + 1) * HALF]

            def heads(e):
                return e[:, 0:HALF * CTX].rearrange("p (h k) -> p h k", h=HALF)

            def second(u):
                e1, e2 = heads(E[:, u % 3]), heads(E2[:, u % 2])
                s1, m2 = of_unit(scale1, u), of_unit(mx2, u)
                dve.wait_ge(sem("exps"), U2 + u + 1)
                link(nc.vector.tensor_reduce(s1, e1, AX.X, ALU.add))
                link(nc.vector.reciprocal(s1, s1))
                link(nc.vector.tensor_scalar(of_unit(share1, u), s1, att_mix[:, 0:1], None, ALU.mult), wait=False)
                link(nc.vector.tensor_tensor(s1, s1, of_unit(gates, u), ALU.mult))
                if u >= 2:
                    dve.wait_ge(sem("l2x_mixed"), u - 1)
                link(nc.vector.tensor_tensor(e2, e1, bc(s1, 2, CTX), ALU.mult))
                link(nc.vector.tensor_reduce(m2, e2, AX.X, ALU.max))
                nc.vector.tensor_tensor(e2, e2, bc(m2, 2, CTX), ALU.subtract).then_inc(sem("l2x_shifted2"), 1)

            def third(u):
                e2, s2 = heads(E2[:, u % 2]), of_unit(share2, u)
                dve.wait_ge(sem("l2x_exps2"), u + 1)
                link(nc.vector.tensor_reduce(s2, e2, AX.X, ALU.add))
                link(nc.vector.reciprocal(s2, s2))
                link(nc.vector.tensor_scalar(s2, s2, r("l2x_w"), None, ALU.mult))
                nc.vector.tensor_tensor(e2, e2, bc(s2, 2, CTX), ALU.mult).then_inc(sem("l2x_weighted2"), 1)

            for i in range(X_STEPS):
                if i >= 5 and i % 2 and (i - 5) // 2 < GROUP:
                    g = (i - 5) // 2
                    dve.wait_ge(sem("values_done"), U2 + 2 * g + 2)
                    nc.vector.tensor_copy(ONT[:, g % 2, 0], o_ps).then_inc(sem("out_kept"), 1)
                if 2 <= i < UNITS + 2:
                    third(i - 2)
                if 1 <= i < UNITS + 1:
                    second(i - 1)
                if i < UNITS:
                    if i >= 3:
                        dve.wait_ge(sem("probs_turned"), U2 + i - 2)
                    shift(dve, link, 3, i, CTX, E[:, i % 3, 0:HALF * CTX])
                if i >= 7 and i % 2:
                    g = (i - 7) // 2
                    dve.wait_ge(sem("y_done"), 4 * GROUP + g + 1)
                    norm_stats(dve, link, 8, g, y_ps, XR)
                if i >= 8 and i % 2 == 0:
                    norm_apply(dve, 8, (i - 8) // 2, Y[:, (i - 8) // 2], X[:, (i - 8) // 2])

        def l2x_pool(pool):
            add_bias(pool, 7, r("l2x_bo"))
            pool.wait_ge(sem("k_kept"), 3)
            spread_keys(pool, 3, 0, CTX)
            for u in range(UNITS):
                if u % 2 == 0 and u // 2 + 1 < GROUP:
                    spread_keys(pool, 3, u // 2 + 1, CTX)
                e1, e2 = E[:, u % 3, 0:HALF * CTX], E2[:, u % 2, 0:HALF * CTX]
                pool.wait_ge(sem("l2x_shifted2"), u + 1)
                nc.gpsimd.tensor_tensor(e1.rearrange("p (h k) -> p h k", h=HALF), e1.rearrange("p (h k) -> p h k", h=HALF),
                                        bc(share1[:, u * HALF:(u + 1) * HALF], 2, CTX),
                                        ALU.mult).then_inc(sem("l2x_weighted1"), 1)
                pool.wait_ge(sem("l2x_weighted1"), u + 1)
                pool.wait_ge(sem("l2x_weighted2"), u + 1)
                nc.gpsimd.tensor_tensor(e1, e1, e2, ALU.add).then_inc(sem("l2x_mixed"), 1)

        NE, WH, WD = 5, 8, 64
        wide_q = big2[:, 0:2048].rearrange("p (j t) -> p j t", j=4)
        wide_k = big2[:, 2048:4096].rearrange("p (j t) -> p j t", j=4)
        flatE = E[:].rearrange("p n k -> p (n k)")
        GE = NE * WH * GROUP
        xv = [(flatE[:, 2048 + 320 * g:2368 + 320 * g] if g < 3 else QT[:, 0, 0:320]).rearrange(
            "p (e d) -> p e d", e=NE) for g in range(GROUP)]
        gl = [small[:, GE * s:GE * s + GE] for s in range(2)]
        glrank = [small[:, 320 + GE * s:320 + GE * s + GE] for s in range(2)]
        glsig = small[:, 640:800].rearrange("p (g h e) -> p g h e", g=GROUP, e=NE)
        v_pick = small[:, 800:960].rearrange("p (g h e) -> p g h e", g=GROUP, e=NE)
        o_pick = small[:, 960:1120].rearrange("p (g h e) -> p g h e", g=GROUP, e=NE)
        head_sum = small[:, 1120:1120 + 32].rearrange("p (g h) -> p g h", g=GROUP)
        gl_pairs = [PT[:].rearrange("p n k -> p (n k)")[:, NE * GE * k:NE * GE * (k + 1)].rearrange(
            "p (m e f) -> p m e f", e=NE, f=NE) for k in range(2)]
        v_parts = E2[:].rearrange("p n k -> p (n k)").rearrange("p (e h d) -> p e h d", e=4, h=WH)
        wide_v = VB[:].rearrange("p g c d -> p g (c d)").rearrange("p g (h d) -> p g h d", h=WH)
        o_kept = [KB[:, k].rearrange("p h k -> p (h k)")[:, 0:512].rearrange("p (h d) -> p h d", h=WH) for k in range(2)]
        o_part4 = [flat_VS[:, 1024 + 512 * k:1536 + 512 * k].rearrange("p (h d) -> p h d", h=WH) for k in range(2)]
        o_parts = E2[:].rearrange("p n k -> p (n k)").rearrange("p (e h d) -> p e h d", e=4, h=WH)
        per_expert = [small[:, 1200 + 320 * k:1520 + 320 * k] for k in range(2)]
        per_expertT = [flat_VS[:, 384 * k:384 * k + 384] for k in range(2)]
        M0 = U2 + UNITS
        S0 = 4 * UNITS
        O0 = 5 * GROUP
        A0 = 4 * GROUP

        def slot(h):
            return 4 * (h % 2) + h // 2

        def l2f_pe(pe):
            pe.wait_ge(sem("xT_ready"), 9 * GROUP)
            for g in range(GROUP):
                m = nc.tensor.matmul(PS[:, 0, 80 * g:80 * g + 80], XT[:, g * 128:(g + 1) * 128], w("l2f_wg"),
                                     start=True, stop=True)
            m.then_inc(sem("l2f_gl"), 1)
            for g in range(GROUP):
                nc.tensor.matmul(PS[:, 4 + g, 0:320], XT[:, g * 128:(g + 1) * 128], w("l2f_wv"),
                                 start=True, stop=True).then_inc(sem("l2f_xv"), 1)
            for j in range(8):
                if j >= 3:
                    pe.wait_ge(sem("l2f_qk_kept"), j - 2)
                nc.tensor.matmul(bank(1 + j % 3), w("l2f_wq" if j % 2 == 0 else "l2f_wk", 128 * (j // 2), 128), XT[:, :],
                                 start=True, stop=True).then_inc(sem("l2f_qk"), 1)
            pe.wait_ge(sem("l2f_gl_kept"), 2)
            pe.wait_ge(sem("l2f_qk_kept"), 8)
            for i in range(GROUP + 5):
                if i < GROUP:
                    if i >= 1:
                        pe.wait_ge(sem("shifted"), S0 + i)
                    for h in range(WH):
                        p, t = 64 * (h % 2), slice(i * 128, (i + 1) * 128)
                        m = nc.tensor.matmul(PS[:, h % 2, (h // 2) * 128:(h // 2) * 128 + 128],
                                             wide_q[p:p + 64, h // 2, t], wide_k[p:p + 64, h // 2, t],
                                             start=True, stop=True)
                    m.then_inc(sem("scores"), 1)
                if i == 4:
                    adapt_l3_pe(pe)
                if i == 6:
                    merge_l3_pe(pe)
                if i >= 5:
                    turn_x(pe, 9, i - 5, X[:, i - 5])
                if 4 <= i <= GROUP + 3:
                    g = i - 4
                    pe.wait_ge(sem("attended"), A0 + g + 1)
                    for k, n in ((0, 128), (1, 128), (2, 64)):
                        m = nc.tensor.transpose(PS[0:n, 6, 128 * k:128 * k + 128],
                                                per_expert[g % 2][:, 128 * k:128 * k + n], ident)
                    m.then_inc(sem("out_turned"), 1)
                    pe.wait_ge(sem("out_kept"), O0 + g + 1)
                    pe.wait_ge(sem("xT_ready"), 9 * GROUP + g)
                    a = per_expertT[g % 2]
                    nc.tensor.matmul(y_ps, a[:, 0:128], w("l2f_wo", 0, 128), start=True, stop=False)
                    nc.tensor.matmul(y_ps, a[:, 128:256], w("l2f_wo", 128, 128), start=False, stop=False)
                    nc.tensor.matmul(y_ps, a[0:64, 256:384], h64("l2f_wo2"), start=False,
                                     stop=True).then_inc(sem("y_done"), 1)
                if 1 <= i <= GROUP:
                    g = i - 1
                    if g == 0:
                        pe.wait_ge(sem("l2f_xv_kept"), GROUP)
                    pe.wait_ge(sem("exps"), S0 + g + 1)
                    turn_probs(pe, M0 + g, TOK, E[:, g % 2])
                    pe.wait_ge(sem("probs_kept"), M0 + g + 1)
                    pe.wait_ge(sem("l2f_v"), 4 * (g + 1))
                    pe.wait_ge(sem("l2f_v4"), g + 1)
                    if g >= 2:
                        pe.wait_ge(sem("l2f_o_kept"), g - 1)
                    for h in range(WH):
                        m = nc.tensor.matmul(PS[:, 2 + g % 2, h * WD:(h + 1) * WD],
                                             PT[:, (M0 + g) % 2, slot(h) * 128:slot(h) * 128 + 128], wide_v[:, g, h],
                                             start=True, stop=True)
                    m.then_inc(sem("values_done"), 1)

        def l2f_act(act, link):
            act.wait_ge(sem("l2f_gl_kept"), 1)
            nc.scalar.activation(glsig.rearrange("p g h e -> p (g h e)"), gl[0], ACT.Exp,
                                 scale=-1.0).then_inc(sem("l2f_expg"), 1)
            for g in range(GROUP):
                act.wait_ge(sem("l2f_xv"), g + 1)
                nc.scalar.activation(xv[g].rearrange("p e d -> p (e d)"), PS[:, 4 + g, 0:320],
                                     ACT.Copy).then_inc(sem("l2f_xv_kept"), 1)
            for j in range(8):
                act.wait_ge(sem("l2f_qk"), j + 1)
                nc.scalar.activation((wide_q if j % 2 == 0 else wide_k)[:, j // 2], bank(1 + j % 3),
                                     ACT.Copy).then_inc(sem("l2f_qk_kept"), 1)

            def expert4_values(g):
                act.wait_ge(sem("l2f_picked"), 1)
                act.wait_ge(sem("l2f_xv_kept"), g + 1)
                for h in range(WH):
                    m = nc.scalar.activation(wide_v[:, g, h], xv[g][:, 4], ACT.Identity, scale=v_pick[:, g, h, 4:5])
                m.then_inc(sem("l2f_v4"), 1)

            expert4_values(0)
            for i in range(GROUP + 5):
                if i >= 5:
                    keep_xT(act, 9, i - 5)
                if 4 <= i <= GROUP + 3:
                    g = i - 4
                    act.wait_ge(sem("out_turned"), GROUP + g + 1)
                    a = per_expertT[g % 2]
                    link(nc.scalar.activation(a[:, 0:256], PS[:, 6, 0:256], ACT.Copy))
                    nc.scalar.activation(a[0:64, 256:384], PS[0:64, 6, 256:384], ACT.Copy).then_inc(sem("out_kept"), 1)
                if 1 <= i <= GROUP:
                    keep_probs(act, M0 + i - 1, TOK)
                if i < GROUP:
                    act.wait_ge(sem("shifted"), S0 + i + 1)
                    nc.scalar.activation(E[:, i % 2], E[:, i % 2], ACT.Exp, scale=WD ** -0.5).then_inc(sem("exps"), 1)
                if i < 2:
                    for g in ((1,), (2, 3))[i]:
                        expert4_values(g)
                if 1 <= i <= GROUP:
                    g = i - 1
                    act.wait_ge(sem("values_done"), M0 + g + 1)
                    if g >= 2:
                        act.wait_ge(sem("attended"), A0 + g - 1)
                    nc.scalar.activation(o_kept[g % 2].rearrange("p h d -> p (h d)"), bank(2 + g % 2),
                                         ACT.Copy).then_inc(sem("l2f_o_kept"), 1)
                    act.wait_ge(sem("l2f_o_kept"), g + 1)
                    act.wait_ge(sem("l2f_shares"), g + 1)
                    for h in range(WH):
                        m = nc.scalar.activation(o_part4[g % 2][:, h], o_kept[g % 2][:, h], ACT.Identity,
                                                 scale=o_pick[:, g, h, 4:5])
                    m.then_inc(sem("l2f_o_part4"), 1)
                if 4 <= i <= GROUP + 3:
                    norm_rstd(act, link, 9, i - 4)

        def l2f_dve(dve, link):
            dve.wait_ge(once("weights4"), 16)
            dve.wait_ge(sem("l2f_gl"), 1)
            for s in range(2):
                nc.vector.tensor_copy(gl[s].rearrange("p (g n) -> p g n", g=GROUP), PS[:, 0, 0:320].rearrange(
                    "p (g s n) -> p g s n", g=GROUP, s=2)[:, :, s]).then_inc(sem("l2f_gl_kept"), 1)

            def rank_experts(s):
                ranks(dve, link, gl[s].rearrange("p (m e) -> p m e", e=NE), WH * GROUP, NE, c("tie5"),
                      glrank[s].rearrange("p (m e) -> p m e", e=NE), *gl_pairs)

            dve.wait_ge(sem("l2f_gl_kept"), 2)
            rank_experts(0)
            dve.wait_ge(sem("l2f_expg"), 1)
            flat_sig = small[:, 640:800]
            link(nc.vector.tensor_scalar(flat_sig, flat_sig, 1.0, None, ALU.add))
            link(nc.vector.reciprocal(flat_sig, flat_sig))
            nc.vector.scalar_tensor_tensor(v_pick.rearrange("p g h e -> p (g h e)"), glrank[0], 2.0, flat_sig,
                                           ALU.is_lt, ALU.mult).then_inc(sem("l2f_picked"), 1)
            rank_experts(1)
            nc.vector.tensor_scalar(o_pick.rearrange("p g h e -> p (g h e)"), glrank[1], 2.0, None,
                                    ALU.is_lt).then_inc(sem("l2f_picked"), 1)

            def add_values(g):
                dve.wait_ge(sem("l2f_v4"), g + 1)
                for e in range(4):
                    dve.wait_ge(sem("l2f_parts"), 4 * g + e + 1)
                    if e >= 1:
                        dve.wait_ge(sem("l2f_v"), 4 * g + e)
                    nc.vector.tensor_tensor(wide_v[:, g], wide_v[:, g], v_parts[:, e], ALU.add).then_inc(sem("l2f_v"), 1)

            for i in range(GROUP + 5):
                if i >= 5:
                    norm_apply(dve, 9, i - 5, Y[:, i - 5], X[:, i - 5])
                if i < GROUP:
                    dve.wait_ge(sem("scores"), S0 + i + 1)
                    if i >= 2:
                        dve.wait_ge(sem("probs_turned"), M0 + i - 1)
                    s = s_view(0, TOK)
                    m = mx[:, i].rearrange("p (b h) -> p b h", b=2)
                    link(nc.vector.tensor_reduce(m, s, AX.X, ALU.max))
                    nc.vector.tensor_tensor(E[:, i % 2].rearrange("p (b h k) -> p b h k", b=2, h=4), s, bc(m, 3, TOK),
                                            ALU.subtract).then_inc(sem("shifted"), 1)
                if i < 3:
                    for g in ((0,), (1,), (2, 3))[i]:
                        add_values(g)
                if 1 <= i <= GROUP:
                    g = i - 1
                    dve.wait_ge(sem("exps"), S0 + g + 1)
                    link(nc.vector.tensor_reduce(head_sum[:, g].rearrange("p (j b) -> p b j", b=2),
                                                 E[:, g % 2].rearrange("p (b j k) -> p b j k", b=2, j=4),
                                                 AX.X, ALU.add))
                    link(nc.vector.reciprocal(head_sum[:, g], head_sum[:, g]))
                    if g == 0:
                        dve.wait_ge(sem("l2f_picked"), 2)
                    nc.vector.tensor_tensor(o_pick[:, g], o_pick[:, g], bc(head_sum[:, g], 2, NE),
                                            ALU.mult).then_inc(sem("l2f_shares"), 1)
                if 3 <= i <= GROUP + 2:
                    g = i - 3
                    dve.wait_ge(sem("l2f_o_parts"), g + 1)
                    dve.wait_ge(sem("l2f_o_part4"), g + 1)
                    a = per_expert[g % 2].rearrange("p (e d) -> p e d", e=NE)
                    link(nc.vector.tensor_reduce(a[:, 0:4], o_parts.rearrange("p e h d -> p e d h"), AX.X, ALU.add))
                    nc.vector.tensor_reduce(a[:, 4], o_part4[g % 2].rearrange("p h d -> p d h"), AX.X,
                                            ALU.add).then_inc(sem("attended"), 1)
                if i == 5:
                    adapt_l3_dve(dve)
                if i == 7:
                    merge_l3_dve(dve)
                if 4 <= i <= GROUP + 3:
                    g = i - 4
                    dve.wait_ge(sem("y_done"), O0 + g + 1)
                    norm_stats(dve, link, 9, g, y_ps, X)

        def l2f_pool(pool):
            pool.wait_ge(sem("l2f_picked"), 1)
            for g in range(GROUP):
                pool.wait_ge(sem("l2f_xv_kept"), g + 1)
                for e in range(4):
                    if g >= 1:
                        pool.wait_ge(sem("l2f_v"), 4 * (g - 1) + e + 1)
                    nc.gpsimd.tensor_tensor(v_parts[:, e], bc(xv[g][:, e], 1, WH), bc(v_pick[:, g, :, e], 2, WD),
                                            ALU.mult).then_inc(sem("l2f_parts"), 1)
            pool.wait_ge(sem("l2f_v"), 4 * GROUP)
            for g in range(GROUP):
                pool.wait_ge(sem("l2f_shares"), g + 1)
                pool.wait_ge(sem("l2f_o_kept"), g + 1)
                if g >= 1:
                    pool.wait_ge(sem("attended"), A0 + g)
                for e in range(4):
                    m = nc.gpsimd.tensor_tensor(o_parts[:, e], o_kept[g % 2], bc(o_pick[:, g, :, e], 2, WD), ALU.mult)
                m.then_inc(sem("l2f_o_parts"), 1)

        def adapt_l3_pe(pe):
            pe.wait_ge(sem("shifted"), S0 + GROUP)
            for j in range(3):
                nc.tensor.matmul(PS[:, 0, 128 * j:128 * j + 128], h64("l3a_B", 128 * j, 128), h64("l3a_A"),
                                 start=True, stop=True)
            nc.tensor.matmul(PS[:, 0, 384:512], h64("l3a_pB"), h64("l3a_pA"),
                             start=True, stop=True).then_inc(sem("l3_adapted"), 1)

        def merge_l3_pe(pe):
            pe.wait_ge(sem("l3_weights"), 1)
            nc.tensor.matmul(PS[:, 1, 0:128], w("l3a_wp"), l3_wpT[:, :],
                             start=True, stop=True).then_inc(sem("l3_adapted"), 1)

        def adapt_l3_dve(dve):
            dve.wait_ge(sem("l3_adapted"), 1)
            nc.vector.tensor_tensor(l3_wpT[:, :], PS[:, 0, 384:512], w("l3a_wpT"),
                                    ALU.add).then_inc(sem("l3_weights"), 1)
            for j in range(3):
                nc.vector.tensor_tensor(l3_wT[:, :].rearrange("p (i j) -> p i j", j=3)[:, :, j],
                                        PS[:, 0, 128 * j:128 * j + 128],
                                        w("l3a_w", 128 * j, 128), ALU.add).then_inc(sem("l3_weights"), 1)

        def merge_l3_dve(dve):
            dve.wait_ge(sem("l3_adapted"), 2)
            nc.vector.tensor_copy(l3_proj[:, :], PS[:, 1, 0:128]).then_inc(sem("l3_weights"), 1)

        def l3a_first_pe(pe):
            pe.wait_ge(sem("xT_ready"), 10 * GROUP)
            pe.wait_ge(sem("l3_weights"), 5)
            for j in range(3):
                nc.tensor.matmul(bank(j), l3_wT[:, 128 * j:128 * j + 128], XT[:, :],
                                 start=True, stop=True).then_inc(sem("l3a_qkv"), 1)

        def l3a_first_act(act, i):
            for j in range(3):
                act.wait_ge(sem("l3a_qkv"), j + 1)
                nc.scalar.activation(qkv_all[:, j, bass.ds(i * GT, GT)], bank(j), ACT.Copy).then_inc(once("qkv_kept"), 1)

        ch_stats = small[:, 0:36].rearrange("p (j n s) -> p j n s", j=3, n=2)
        ch_mv = small[:, 40:46].rearrange("p (j s) -> p j s", j=3)
        ch_scale = small[:, 2000:2003]
        ch_shift = small[:, 2004:2007]
        w_quant = small[:, 128:256]
        wqT = l3_wpT

        def norm_channels_dve(dve):
            def link(ins):
                chain[0] += 1
                ins.then_inc(once("between_chain"), 1)
                dve.wait_ge(once("between_chain"), chain[0])

            chain = [0]
            quantise(link, w("l3f_w"), 4, w_quant)
            nc.vector.tensor_copy(ch_scale, w_quant[:, 0:3]).then_inc(once("w_quantised"), 1)
            dve.wait_ge(once("qkv_kept"), 3 * GROUPS)
            for j in range(3):
                for n in range(2):
                    link(nc.vector.bn_stats(ch_stats[:, j, n], qkv_all[:, j, GT * n:GT * n + GT]))
                link(nc.vector.bn_aggr(ch_mv[:, j], ch_stats[:, j].rearrange("p n s -> p (n s)")))
            nc.vector.tensor_copy(ch_shift, ch_mv[:, :, 1]).then_inc(once("channel_var"), 1)
            dve.wait_ge(once("channel_rstd"), 1)
            link(nc.vector.tensor_tensor(ch_scale, ch_shift, w("l3a_gamma"), ALU.mult))
            link(nc.vector.tensor_tensor(ch_shift, ch_mv[:, :, 0], ch_scale, ALU.mult))
            link(nc.vector.tensor_tensor(ch_shift, w("l3a_beta"), ch_shift, ALU.subtract))
            dve.wait_ge(once("wT_turned"), 1)
            nc.vector.tensor_copy(wqT[:, :], PS[:, 0, 0:128]).then_inc(once("wT_kept"), 1)
            dve.wait_ge(once("wT_kept"), 1)

        def norm_channels_act(act):
            act.wait_ge(once("channel_var"), 1)
            nc.scalar.activation(ch_shift, ch_shift, ACT.Ln, bias=eps_col[:, 0:1]).then_inc(once("channel_ln"), 1)
            act.wait_ge(once("channel_ln"), 1)
            nc.scalar.activation(ch_shift, ch_shift, ACT.Exp, scale=-0.5).then_inc(once("channel_rstd"), 1)

        def turn_quantised(pe):
            pe.wait_ge(once("w_quantised"), 1)
            nc.tensor.transpose(PS[:, 0, 0:128], w_quant, ident).then_inc(once("wT_turned"), 1)
            pe.wait_ge(once("wT_kept"), 1)

        def quantise(link, src, blocks, dst):
            n = 32 * blocks
            y, y2, a, b = flatE[:, 0:n], flatE[:, 512:512 + n], flatE[:, 1024:1024 + n], flatE[:, 1536:1536 + n]
            inv, rnd = flatE[:, 2048:2048 + n], flatE[:, 2560:2560 + n]
            top, scale, rs = (small[:, 1024 + 16 * k:1024 + 16 * k + blocks] for k in range(3))

            def blk(ap):
                return ap.rearrange("p (b k) -> p b k", k=32)

            link(nc.vector.tensor_reduce(top, blk(src), AX.X, ALU.max, apply_absolute_value=True))
            link(nc.vector.tensor_scalar(scale, top, 1.0 / 7.5, 1e-30, ALU.mult, ALU.max))
            link(nc.vector.reciprocal(rs, scale))
            link(nc.vector.tensor_tensor(blk(y), blk(src), bc(rs, 2, 32), ALU.mult))
            link(nc.vector.tensor_tensor(y2, y, y, ALU.mult))
            link(nc.vector.tensor_scalar(a, y2, 4.0, -4.0, ALU.is_ge, ALU.mult))
            link(nc.vector.tensor_scalar(b, y2, 16.0, -2.0, ALU.is_ge, ALU.mult))
            link(nc.vector.scalar_tensor_tensor(inv, a, 8.0, b, ALU.add, ALU.add))
            link(nc.vector.tensor_tensor(y, y, inv, ALU.mult))
            link(nc.vector.tensor_scalar(rnd, y, ROUND, ROUND, ALU.add, ALU.subtract))
            link(nc.vector.tensor_tensor(y, y, rnd, ALU.subtract))
            link(nc.vector.scalar_tensor_tensor(y, y, -0.5, rnd, ALU.is_equal, ALU.subtract))
            link(nc.vector.reciprocal(inv, inv))
            link(nc.vector.scalar_tensor_tensor(y, y, -1.0, inv, ALU.mult, ALU.mult))
            link(nc.vector.tensor_tensor(blk(dst), blk(y), bc(scale, 2, 32), ALU.mult))

        qkv = [big2[:, GT * j:GT * j + GT] for j in range(3)]
        vmat = VB[:, :, 0]
        p_sum = small[:, 64:64 + GROUP]

        def l3a_pe(pe):
            pe.wait_ge(sem("l3a_normed"), 3)
            for g in range(GROUP):
                m = nc.tensor.transpose(PS[:, 6, g * 128:(g + 1) * 128], qkv[2][:, g * 128:(g + 1) * 128], ident)
            m.then_inc(sem("l3a_v"), 1)
            for i in range(GROUP + 3):
                if i < GROUP:
                    t = slice(i * 128, (i + 1) * 128)
                    if i >= 2:
                        pe.wait_ge(sem("l3a_shifted"), i - 1)
                    nc.tensor.matmul(PS[:, i % 2, 0:128], qkv[0][:, t], qkv[1][:, t], start=True, stop=False)
                    nc.tensor.matmul(PS[:, i % 2, 0:128], ident_bf[:, :], causal_bf[:, 0], start=False,
                                     stop=True).then_inc(sem("l3a_scores"), 1)
                if i >= 3:
                    turn_x(pe, 0, i - 3, X[:, i - 3])
                if 1 <= i <= GROUP:
                    g = i - 1
                    pe.wait_ge(sem("l3a_exp"), g + 1)
                    nc.tensor.transpose(PS[:, 2 + g % 2, 0:128], E[:, g % 2, 0:128], ident).then_inc(sem("l3a_pT"), 1)
                    pe.wait_ge(sem("l3a_pT_kept"), g + 1)
                    if g == 0:
                        pe.wait_ge(sem("l3a_v_kept"), 1)
                    if g >= 2:
                        pe.wait_ge(sem("attended"), g - 1)
                    nc.tensor.matmul(PS[:, 4 + g % 2, 0:128], PT[:, g % 2, 0:128], vmat[:, g],
                                     start=True, stop=True).then_inc(sem("l3a_o"), 1)
                if 2 <= i <= GROUP + 1:
                    g = i - 2
                    pe.wait_ge(sem("attended"), g + 1)
                    if g >= 1:
                        pe.wait_ge(sem("xT_ready"), g)
                    nc.tensor.transpose(ont_ps, ON[:, g, 0:128], ident).then_inc(sem("out_turned"), 1)
                    project_out(pe, g, g, 0, l3_proj[:, :])

        def l3a_act(act, link):
            act.wait_ge(sem("l3a_v"), 1)
            nc.scalar.activation(vmat, PS[:, 6].rearrange("p (g d) -> p g d", g=GROUP),
                                 ACT.Copy).then_inc(sem("l3a_v_kept"), 1)
            for i in range(GROUP + 3):
                if i >= 3:
                    keep_xT(act, 0, i - 3)
                if 1 <= i <= GROUP:
                    g = i - 1
                    act.wait_ge(sem("l3a_pT"), g + 1)
                    if g >= 2:
                        act.wait_ge(sem("l3a_o"), g - 1)
                    nc.scalar.activation(PT[:, g % 2, 0:128], PS[:, 2 + g % 2, 0:128],
                                         ACT.Copy).then_inc(sem("l3a_pT_kept"), 1)
                if i < GROUP:
                    act.wait_ge(sem("l3a_shifted"), i + 1)
                    nc.scalar.activation(E[:, i % 2, 0:128], E[:, i % 2, 0:128], ACT.Exp,
                                         scale=DIM ** -0.5).then_inc(sem("l3a_exp"), 1)
                if 2 <= i <= GROUP + 1:
                    act.wait_ge(sem("out_turned"), i - 1)
                    nc.scalar.activation(ONT[:, i % 2, 0], ont_ps, ACT.Copy).then_inc(sem("out_kept"), 1)
                    norm_rstd(act, link, 0, i - 2)

        def l3a_dve(dve, link, i):
            link(nc.vector.tensor_copy(X[:].rearrange("p g d -> p (g d)"), x_all[:, bass.ds(i * GT, GT)]))
            for j in range(3):
                nc.vector.tensor_scalar(qkv[j], qkv_all[:, j, bass.ds(i * GT, GT)], ch_scale[:, j:j + 1],
                                        ch_shift[:, j:j + 1], ALU.mult, ALU.add).then_inc(sem("l3a_normed"), 1)
            for i in range(GROUP + 3):
                if i >= 3:
                    norm_apply(dve, 0, i - 3, Y[:, i - 3], X[:, i - 3])
                if i < GROUP:
                    dve.wait_ge(sem("l3a_scores"), i + 1)
                    link(nc.vector.tensor_reduce(mx[:, i, 0:1], PS[:, i % 2, 0:128], AX.X, ALU.max))
                    if i >= 2:
                        dve.wait_ge(sem("l3a_pT"), i - 1)
                    nc.vector.tensor_scalar(E[:, i % 2, 0:128], PS[:, i % 2, 0:128], mx[:, i, 0:1], None,
                                            ALU.subtract).then_inc(sem("l3a_shifted"), 1)
                if 1 <= i <= GROUP:
                    g = i - 1
                    dve.wait_ge(sem("l3a_exp"), g + 1)
                    link(nc.vector.tensor_reduce(p_sum[:, g:g + 1], E[:, g % 2, 0:128], AX.X, ALU.add))
                    link(nc.vector.reciprocal(p_sum[:, g:g + 1], p_sum[:, g:g + 1]))
                    dve.wait_ge(sem("l3a_o"), g + 1)
                    nc.vector.tensor_scalar(ON[:, g, 0:128], PS[:, 4 + g % 2, 0:128], p_sum[:, g:g + 1], None,
                                            ALU.mult).then_inc(sem("attended"), 1)
                if 2 <= i <= GROUP + 1:
                    g = i - 2
                    dve.wait_ge(sem("y_done"), g + 1)
                    norm_stats(dve, link, 0, g, y_ps, X)

        x_quant = flat_VS[:, 0:GT]
        x_quantT = E2[:, 0, 0:GT]

        def second_pe(pe):
            l3a_pe(pe)
            pe.wait_ge(sem("ctx_ready"), 1)
            project_ctx(pe, 0, 0, w("l3x_wq"), w("l3x_wq"), w("l3x_wq"))
            attend_pe(pe, 0, 0, GROUP, 1, CTX, w("l3x_wo"))
            for g in range(GROUP):
                pe.wait_ge(sem("l3f_quantised"), 1)
                nc.tensor.transpose(PS[:, g, 0:128], x_quant[:, g * 128:(g + 1) * 128],
                                    ident).then_inc(sem("l3f_turned"), 1)
            for g in range(GROUP):
                pe.wait_ge(sem("l3f_kept"), g + 1)
                nc.tensor.matmul(PS[:, 4 + g % 3, 0:128] if g < 3 else PS[:, 0, 0:128],
                                 x_quantT[:, g * 128:(g + 1) * 128], wqT[:, :],
                                 start=True, stop=True).then_inc(sem("l3f_y"), 1)

        def second_act(act, link, i):
            l3a_act(act, link)
            act.wait_ge(once("weights4"), 16)
            keep_qk(act, 0, w("l3x_bq"), w("l3x_bq"))
            attend_act(act, link, 0, 1, CTX, lambda u: exp_unit(act, 0, u, CTX, SCALE))
            for g in range(GROUP):
                act.wait_ge(sem("l3f_turned"), g + 1)
                nc.scalar.activation(x_quantT[:, g * 128:(g + 1) * 128], PS[:, g, 0:128],
                                     ACT.Copy).then_inc(sem("l3f_kept"), 1)
            for g in range(GROUP):
                norm_rstd(act, link, 2, g)

        def second_dve(dve, link, i):
            l3a_dve(dve, link, i)
            keep_v(dve, 0, r("l3x_bv"))
            dve.wait_ge(sem("residual"), 1)
            attend_dve(dve, link, 0, GROUP, 1, CTX, XR, lambda u: shift_unit(dve, link, 0, u, CTX, 0))
            dve.wait_ge(sem("x_ready"), 2 * GROUP)
            quantise(link, X[:].rearrange("p g d -> p (g d)"), 4 * GROUP, x_quant)
            nc.vector.tensor_copy(small[:, 1100:1101], x_quant[:, 0:1]).then_inc(sem("l3f_quantised"), 1)
            dve.wait_ge(sem("residual"), 2)
            norms_dve(dve, link, 2, "l3f_y", lambda g: PS[:, 4 + g, 0:128] if g < 3 else PS[:, 0, 0:128], XR)
            dve.wait_ge(sem("x_ready"), 3 * GROUP)
            nc.vector.tensor_copy(x_all[:, bass.ds(i * GT, GT)],
                                  X[:].rearrange("p g d -> p (g d)")).then_inc(once("x_kept"), 1)

        def second_pool(pool, i):
            nc.gpsimd.tensor_copy(CT[:, :], ctx_all[:, bass.ds(i * GC, GC)]).then_inc(sem("ctx_ready"), 1)
            add_bias(pool, 0, r("l3x_bo"))
            clear_values(pool, 0, GROUP * VW)
            spread_all(pool, 0, CTX, "k_kept", 1)
            add_bias(pool, 1, r("l3f_b"))

        pool_stages = [l0x_pool, l0f_pool, l1a_pool, l1x_pool, l1f_pool, l2a_pool, l2x_pool, l2f_pool]
        act_stages = [l0x_act, l0f_act, l1a_act, l1x_act, l1f_act, l2a_act, l2x_act, l2f_act]
        dve_stages = [l0x_dve, l0f_dve, l1a_dve, l1x_dve, l1f_dve, l2a_dve, l2x_dve, l2f_dve]
        pe_stages = [l0x_pe, l0f_pe, l1a_pe, l1x_pe, l1f_pe, l2a_pe, l2x_pe, l2f_pe]

        def load_all(sp):
            cuts = [0] + [W128[n][0] for n in W128_CUTS] + [W128_N]

            def load_weights(n):
                sp.dma_start(w128[:, cuts[n]:cuts[n + 1]], w128_in[:, cuts[n]:cuts[n + 1]]
                             ).then_inc(once(f"weights{n}"), 16)

            sp.dma_start(x_all[:, :], x_in).then_inc(once("x_loaded"), 16)
            sp.dma_start(con[:, :], con_in).then_inc(once("con_loaded"), 16)
            load_weights(0)
            sp.dma_start(row[:, :], row_in.to_broadcast([128, ROW_N])).then_inc(once("row_loaded"), 16)
            sp.dma_start(ctx_all[:, :], ctx_in).then_inc(once("ctx_loaded"), 16)
            sp.dma_start(mask_u8[:, :], mask_in.to_broadcast([128, BATCH * CTX])).then_inc(once("ctx_loaded"), 16)
            sp.dma_start(w64[:, :], w64_in).then_inc(once("w64_loaded"), 16)
            sp.dma_start(w16[:, :], w16_in).then_inc(once("w64_loaded"), 16)
            sp.dma_start(w8[:, :], w8_in).then_inc(once("w64_loaded"), 16)
            for n in range(1, len(cuts) - 1):
                load_weights(n)

        def once_pool(pool):
            nc.gpsimd.memset(eps_col[:, :], EPS).then_inc(once("consts"), 1)
            nc.gpsimd.memset(one_col[:, :], 1.0).then_inc(once("consts"), 1)

        def once_dve(dve):
            dve.wait_ge(once("con_loaded"), 16)
            dve.wait_ge(once("w64_loaded"), 48)
            dve.wait_ge(once("row_loaded"), 16)
            nc.vector.tensor_copy(ident_bf[:, :], ident).then_inc(once("casts"), 1)
            nc.vector.tensor_copy(causal_bf[:], bc(c("causal"), 1, 4)).then_inc(once("casts"), 1)
            nc.vector.tensor_copy(row0_bf[:, :], c("row0")).then_inc(once("casts"), 1)
            nc.vector.tensor_copy(w3_rep[:, :], h64("l1x_w3").to_broadcast([64, 128])).then_inc(once("casts"), 1)
            nc.vector.tensor_scalar(att_mix[:, :], r("l2x_w"), -1.0, 1.0, ALU.mult, ALU.add).then_inc(once("casts"), 1)

        def turn_around(eng, i, first):
            eng.drain().then_inc(once("iteration_done"), 1)
            eng.wait_ge(once("iteration_go"), i + first + 1)

        @block.gpsimd
        def _(pool):
            once_pool(pool)
            with pool.Fori(0, GROUPS) as i:
                l0a_pool(pool, i)
                for s in pool_stages:
                    s(pool)
                turn_around(pool, i, 0)
            with pool.Fori(0, GROUPS) as i:
                second_pool(pool, i)
                turn_around(pool, i, GROUPS)

        @block.scalar
        def _(act):
            with act.Fori(0, GROUPS) as i:
                act.preload_act_table_set("natural_log_exp_and_others")
                link = linker(act, "act_chain")
                l0a_act(act, link)
                for s in act_stages:
                    s(act, link)
                l3a_first_act(act, i)
                turn_around(act, i, 0)
            norm_channels_act(act)
            with act.Fori(0, GROUPS) as i:
                act.preload_act_table_set("natural_log_exp_and_others")
                second_act(act, linker(act, "act_chain"), i)
                turn_around(act, i, GROUPS)

        @block.vector
        def _(dve):
            once_dve(dve)
            with dve.Fori(0, GROUPS) as i:
                link = linker(dve, "dve_chain")
                l0a_dve(dve, link, i)
                for s in dve_stages:
                    s(dve, link)
                dve.wait_ge(sem("x_ready"), GROUP * 10)
                nc.vector.tensor_copy(x_all[:, bass.ds(i * GT, GT)],
                                      X[:].rearrange("p g d -> p (g d)")).then_inc(once("x_kept"), 1)
                turn_around(dve, i, 0)
            norm_channels_dve(dve)
            with dve.Fori(0, GROUPS) as i:
                second_dve(dve, linker(dve, "dve_chain2"), i)
                turn_around(dve, i, GROUPS)

        @block.tensor
        def _(pe):
            with pe.Fori(0, GROUPS) as i:
                l0a_pe(pe)
                for s in pe_stages:
                    s(pe)
                l3a_first_pe(pe)
                turn_around(pe, i, 0)
            turn_quantised(pe)
            with pe.Fori(0, GROUPS) as i:
                second_pe(pe)
                turn_around(pe, i, GROUPS)

        @block.sync
        def _(sp):
            load_all(sp)
            numbers = sorted(s.num for s in body_sems.values())
            ends = [i for i in range(1, len(numbers) + 1) if i == len(numbers) or numbers[i] > numbers[i - 1] + 1]
            runs = [range(numbers[i], numbers[j - 1] + 1) for i, j in zip([0] + ends[:-1], ends)]
            for turn in range(2 * GROUPS):
                sp.wait_ge(once("iteration_done"), 4 * (turn + 1))
                for numbers_of_run in runs:
                    last = sp.sem_clear(numbers_of_run)
                last.then_inc(once("iteration_go"), 1)
            sp.wait_ge(once("x_kept"), 2 * GROUPS)
            sp.dma_start(out, x_all[:, :]).then_inc(once("stored"), 16)
            sp.wait_ge(once("stored"), 16)


def _pack(pieces, rows):
    return np.ascontiguousarray(np.concatenate([np.asarray(p).reshape(rows, -1) for p in pieces], axis=1))


def kernel(**t):
    import concourse.bacc as _bacc
    from concourse.bass_utils import run_bass_kernel_spmd as _run

    a = {k: np.asarray(v) for k, v in t.items()}
    wqkv = a["L2_attn_W_qkv"]
    swap = np.arange(128) ^ 1
    wkv = a["L2_xattn_w_kv"]
    spread = np.arange(128).reshape(4, 4, DH).transpose(1, 0, 2).reshape(128)
    w128 = {
        "l0a_gamma": a["L0_attn_gamma"], "l0a_beta": a["L0_attn_beta"],
        "l0a_wk": a["L0_attn_Wk"].T, "l0a_wq": a["L0_attn_Wq"].T, "l0a_wv": a["L0_attn_Wv"].T,
        "l0x_wq": a["L0_xattn_wq"], "l0x_wk": a["L0_xattn_wk"], "l0x_wv": a["L0_xattn_wv"],
        "l0x_wo": a["L0_xattn_wo"][spread], "l0x_bq": a["L0_xattn_bq"], "l0x_bk": a["L0_xattn_bk"],
        "l0f_wg": a["L0_ffn_Wg"],
        "l0f_b1": a["L0_ffn_b1"].reshape(8, 4, 128).transpose(2, 0, 1),
        "l0f_w1": a["L0_ffn_W1"].transpose(1, 0, 2),
        "l0f_w2": a["L0_ffn_W2"].reshape(8, 4, 128, 128).transpose(2, 0, 1, 3),
        "l1a_wq": a["L1_attn_Wq"], "l1a_wk": a["L1_attn_Wk"], "l1a_wv": a["L1_attn_Wv"],
        "l1a_wg": a["L1_attn_Wg"], "l1a_w1": a["L1_attn_gk_w1"], "l1a_b2": a["L1_attn_gk_b2"],
        "l1a_wo": a["L1_attn_Wo"].reshape(2, 128, 128).transpose(1, 0, 2),
        "l1x_wq": a["L1_xattn_Wq"].T, "l1x_wk": a["L1_xattn_Wk"].T, "l1x_wv": a["L1_xattn_Wv"].T,
        "l1x_wo": a["L1_xattn_Wo"].T[spread], "l1x_bq": a["L1_xattn_bq"], "l1x_bk": a["L1_xattn_bk"],
        "l1f_wg": a["L1_ffn_gate_w"].T, "l1f_b1": a["L1_ffn_b1"].T, "l1f_b2": a["L1_ffn_b2"].T,
        "l1f_w1": a["L1_ffn_w1"].transpose(1, 0, 2), "l1f_w2": a["L1_ffn_w2"].transpose(1, 0, 2),
        "l1f_w3": a["L1_ffn_w3"].transpose(1, 0, 2),
        "l2a_wq": wqkv[:, 0:128], "l2a_wk": wqkv[:, 128:256],
        "l2a_wqs": wqkv[:, 0:128][:, swap], "l2a_wks": wqkv[:, 128:256][:, swap],
        "l2a_wv": wqkv[:, 256:384], "l2a_wo": a["L2_attn_W_out"][spread],
        "l2x_wk": wkv[:, 0:128], "l2x_wv": wkv[:, 128:256], "l2x_wq": a["L2_xattn_w_q"],
        "l2x_wla": a["L2_xattn_w_la"], "l2x_wo": a["L2_xattn_w_proj"][spread],
        "l2f_wq": a["L2_ffn_Wq"], "l2f_wk": a["L2_ffn_Wk"],
        "l2f_wg": np.concatenate([a["L2_ffn_Ws"], a["L2_ffn_Wd"]], axis=1),
        "l2f_wv": a["L2_ffn_Wv"].transpose(1, 0, 2),
        "l2f_wo": a["L2_ffn_Wo"].reshape(320, 128)[:256].reshape(2, 128, 128).transpose(1, 0, 2),
        "l3a_w": a["L3_attn_W_attn"].reshape(128, 3, 128).transpose(2, 1, 0),
        "l3a_wp": a["L3_attn_W_proj"], "l3a_wpT": a["L3_attn_W_proj"].T,
        "l3a_gamma": a["L3_attn_bn_gamma"].reshape(3, 128).T, "l3a_beta": a["L3_attn_bn_beta"].reshape(3, 128).T,
        "l3x_wq": a["L3_xattn_Wq"], "l3x_wo": a["L3_xattn_Wo"][spread], "l3x_bq": a["L3_xattn_bq"],
        "l3f_w": a["L3_ffn_weight"],
    }
    w64 = {
        "l0a_bk": a["L0_attn_bk"], "l0a_bq": a["L0_attn_bq"], "l1x_w2": a["L1_xattn_w2"].T,
        "l1x_w3": a["L1_xattn_w3"].T, "l1x_b1": a["L1_xattn_b1"], "l1x_b2": a["L1_xattn_b2"],
        "l2f_wo2": a["L2_ffn_Wo"].reshape(320, 128)[256:],
        "l3a_A": a["L3_attn_lora_attn_A"].T, "l3a_B": a["L3_attn_lora_attn_B"],
        "l3a_pA": a["L3_attn_lora_proj_A"].T, "l3a_pB": a["L3_attn_lora_proj_B"],
    }
    row = {
        "l0a_bv": a["L0_attn_bv"], "l0x_bv": a["L0_xattn_bv"], "l0x_bo": a["L0_xattn_bo"], "l0f_bg": a["L0_ffn_bg"],
        "l1a_gn": a["L1_attn_g_norm_w"], "l1x_bv": a["L1_xattn_bv"], "l1x_bo": a["L1_xattn_bo"],
        "l1x_w1": a["L1_xattn_w1"].T, "l1x_b3": a["L1_xattn_b3"], "l1f_bg": a["L1_ffn_gate_b"],
        "l2a_bo": a["L2_attn_b_out"], "l2x_bo": a["L2_xattn_b_proj"], "l2x_w": a["L2_xattn_att_weight"],
        "l3x_bv": a["L3_xattn_bq"], "l3x_bo": a["L3_xattn_bo"], "l3f_b": a["L3_ffn_bias"],
    }
    arrays = {
        "x_in": np.ascontiguousarray(a["x"].transpose(1, 0, 2)).reshape(128, BATCH * DIM),
        "ctx_in": np.ascontiguousarray(a["ctx_1024"].transpose(2, 0, 1)).reshape(128, BATCH * CTX),
        "mask_in": np.ascontiguousarray(a["mask_BxS2_bk0"]).reshape(1, BATCH * CTX),
        "w128_in": _pack([w128[n] for n in W128], 128),
        "w64_in": _pack([w64[n] for n in W64], 64),
        "w16_in": np.ascontiguousarray(a["L1_attn_gk_w2"]),
        "w8_in": _pack([a["L0_ffn_b2"], a["L1_ffn_b3"]], 8),
        "row_in": _pack([row[n] for n in ROW], 1),
        "con_in": constants(),
    }
    nc = _bacc.Bacc("TRN2", target_bir_lowering=False, num_devices=1)
    args = [nc.dram_tensor(n, v.shape, mybir.dt.from_np(v.dtype), kind="ExternalInput").ap()
            for n, v in arrays.items()]
    out = nc.dram_tensor("out", (128, BATCH * DIM), F32, kind="ExternalOutput").ap()
    decoder(nc, *args, out)
    r = _run(nc, [arrays], core_ids=[0])
    return np.ascontiguousarray(r.results[0]["out"].reshape(TOK, BATCH, DIM).transpose(1, 0, 2))
```
